# Optimizing a Trainium2 kernel written in Bass

```python
import numpy as np
import jax
import jax.numpy as jnp

def _softmax(x, axis=-1):
    return jax.nn.softmax(x, axis=axis)

def _gelu(x):
    return jax.nn.gelu(x, approximate=True)

def _silu(x):
    return jax.nn.silu(x)

def _sigmoid(x):
    return jax.nn.sigmoid(x)

def _layernorm(x, axis=-1, eps=1e-05):
    m = jnp.mean(x, axis=axis, keepdims=True)
    v = jnp.var(x, axis=axis, keepdims=True)
    return (x - m) / jnp.sqrt(v + eps)

def _scatter_add(tgt, idx, src, axis=0):
    return tgt.at[idx].add(src)

def _segment_sum(src, seg, n):
    return jax.ops.segment_sum(src, seg, n)
kernel_name = 'mk_adaln_d2_jaxref_r8_2b1cf7'

def setup_inputs(seed: int=0):
    np.random.seed(seed)
    _w = jnp.asarray

    def _L0_attn_setup():
        import jax, jax.numpy as jnp
        import numpy as np
        NUM_HEADS = 16
        EPS = 1e-06

        def elu_plus_one(x):
            return jax.nn.elu(x) + 1.0
        key = jax.random.key(seed)
        ks = jax.random.split(key, 9)
        B, L, E = (4, 512, 128)
        s = 1.0 / np.sqrt(E)
        return {'query': jax.random.normal(ks[0], (B, L, E), jnp.float32), 'Wq': jax.random.normal(ks[1], (E, E), jnp.float32) * s, 'bq': jax.random.normal(ks[2], (E,), jnp.float32) * 0.01, 'Wk': jax.random.normal(ks[3], (E, E), jnp.float32) * s, 'bk': jax.random.normal(ks[4], (E,), jnp.float32) * 0.01, 'Wv': jax.random.normal(ks[5], (E, E), jnp.float32) * s, 'bv': jax.random.normal(ks[6], (E,), jnp.float32) * 0.01, 'Wo': jax.random.normal(ks[7], (E, E), jnp.float32) * s, 'bo': jax.random.normal(ks[8], (E,), jnp.float32) * 0.01}
    _L0_attn_in = _L0_attn_setup()

    def _L0_ffn_setup():
        import jax, jax.numpy as jnp
        import numpy as np
        H, E, DFF = (128, 8, 512)
        key = jax.random.key(seed)
        ks = jax.random.split(key, 7)
        s = lambda *shape: 1.0 / np.sqrt(shape[-2] if len(shape) > 1 else shape[-1])
        x = jax.random.normal(ks[0], (2, 256, H), dtype=jnp.float32)
        Wr = jax.random.normal(ks[1], (H, E), dtype=jnp.float32) * (1.0 / np.sqrt(H))
        br = jnp.zeros((E,), dtype=jnp.float32)
        W1 = jax.random.normal(ks[2], (E, H, DFF), dtype=jnp.float32) * (1.0 / np.sqrt(H))
        b1 = jnp.zeros((E, DFF), dtype=jnp.float32)
        W2 = jax.random.normal(ks[3], (E, DFF, H), dtype=jnp.float32) * (1.0 / np.sqrt(DFF))
        b2 = jnp.zeros((E, H), dtype=jnp.float32)
        return {'x': x, 'Wr': Wr, 'br': br, 'W1': W1, 'b1': b1, 'W2': W2, 'b2': b2}
    _L0_ffn_in = _L0_ffn_setup()
    _L0_c = _w((lambda *s: np.random.randn(*s).astype(np.float32) * 0.05)(4, 128))
    _L0_wmod = _w((lambda *s: np.random.randn(*s).astype(np.float32) * 0.05)(128, 6 * 128) * 128 ** (-0.5))

    def _L1_attn_setup():
        import jax, jax.numpy as jnp
        import numpy as np
        NUM_HEAD = 16
        D_Q = 64
        D_KV = 64
        ROPE_BASE = 10000.0

        def _cos_sin(seq_len, dim):
            pos = jnp.arange(seq_len, dtype=jnp.float32)[:, None]
            ids = jnp.arange(dim // 2, dtype=jnp.float32)
            theta = ROPE_BASE ** (-2.0 * ids) / (dim // 2)
            r = pos * theta[None, :]
            return (jnp.cos(r), jnp.sin(r))

        def _rope(x, cos, sin):
            b, s, d = x.shape
            xv = x.reshape(b, s, d // 2, 2)
            x0, x1 = (xv[..., 0], xv[..., 1])
            out = jnp.stack([x0 * cos - x1 * sin, x1 * cos + x0 * sin], axis=-1)
            return out.reshape(b, s, d)
        key = jax.random.key(seed)
        ks = jax.random.split(key, 10)
        d_model, d_q, d_kv = (128, D_Q, D_KV)
        b, s = (2, 256)
        w = lambda k, i, o: jax.random.normal(k, (i, o), dtype=jnp.float32) * 0.02
        return {'x': jax.random.normal(ks[0], (b, s, d_model), dtype=jnp.float32), 'Wd_q_w': w(ks[1], d_model, d_q), 'Wd_q_b': jnp.zeros((d_q,), jnp.float32), 'Wu_q_w': w(ks[2], d_q, d_model), 'Wu_q_b': jnp.zeros((d_model,), jnp.float32), 'Wq_r_w': w(ks[3], d_q, d_model), 'Wq_r_b': jnp.zeros((d_model,), jnp.float32), 'Wk_r_w': w(ks[4], d_model, d_model), 'Wk_r_b': jnp.zeros((d_model,), jnp.float32), 'Wd_kv_w': w(ks[5], d_model, d_kv), 'Wd_kv_b': jnp.zeros((d_kv,), jnp.float32), 'Wu_k_w': w(ks[6], d_kv, d_model), 'Wu_k_b': jnp.zeros((d_model,), jnp.float32), 'Wu_v_w': w(ks[7], d_kv, d_model), 'Wu_v_b': jnp.zeros((d_model,), jnp.float32), 'Wo_w': w(ks[8], d_model, d_model), 'Wo_b': jnp.zeros((d_model,), jnp.float32)}
    _L1_attn_in = _L1_attn_setup()

    def _L1_ffn_setup():
        import jax, jax.numpy as jnp
        import numpy as np
        B, S, H = (2, 256, 128)
        N, F, SF, K = (16, 128, 512, 1)
        key = jax.random.key(seed)
        ks = jax.random.split(key, 7)
        std = 0.02
        return {'hidden_states': jax.random.normal(ks[0], (B, S, H), dtype=jnp.float32), 'router_w': jax.random.normal(ks[1], (N, H), dtype=jnp.float32) * std, 'gate_up_proj': jax.random.normal(ks[2], (N, H, 2 * F), dtype=jnp.float32) * std, 'down_proj': jax.random.normal(ks[3], (N, F, H), dtype=jnp.float32) * std, 'shared_gate_w': jax.random.normal(ks[4], (SF, H), dtype=jnp.float32) * std, 'shared_up_w': jax.random.normal(ks[5], (SF, H), dtype=jnp.float32) * std, 'shared_down_w': jax.random.normal(ks[6], (H, SF), dtype=jnp.float32) * std}
    _L1_ffn_in = _L1_ffn_setup()
    _L1_c = _w((lambda *s: np.random.randn(*s).astype(np.float32) * 0.05)(4, 128))
    _L1_wmod = _w((lambda *s: np.random.randn(*s).astype(np.float32) * 0.05)(128, 6 * 128) * 128 ** (-0.5))
    _d = {'L0_attn_query': _L0_attn_in['query'], 'L0_attn_Wq': _L0_attn_in['Wq'], 'L0_attn_bq': _L0_attn_in['bq'], 'L0_attn_Wk': _L0_attn_in['Wk'], 'L0_attn_bk': _L0_attn_in['bk'], 'L0_attn_Wv': _L0_attn_in['Wv'], 'L0_attn_bv': _L0_attn_in['bv'], 'L0_attn_Wo': _L0_attn_in['Wo'], 'L0_attn_bo': _L0_attn_in['bo'], 'L0_ffn_Wr': _L0_ffn_in['Wr'], 'L0_ffn_br': _L0_ffn_in['br'], 'L0_ffn_W1': _L0_ffn_in['W1'], 'L0_ffn_b1': _L0_ffn_in['b1'], 'L0_ffn_W2': _L0_ffn_in['W2'], 'L0_ffn_b2': _L0_ffn_in['b2'], 'L0_c': _L0_c, 'L0_wmod': _L0_wmod, 'L1_attn_Wd_q_w': _L1_attn_in['Wd_q_w'], 'L1_attn_Wd_q_b': _L1_attn_in['Wd_q_b'], 'L1_attn_Wu_q_w': _L1_attn_in['Wu_q_w'], 'L1_attn_Wu_q_b': _L1_attn_in['Wu_q_b'], 'L1_attn_Wq_r_w': _L1_attn_in['Wq_r_w'], 'L1_attn_Wq_r_b': _L1_attn_in['Wq_r_b'], 'L1_attn_Wk_r_w': _L1_attn_in['Wk_r_w'], 'L1_attn_Wk_r_b': _L1_attn_in['Wk_r_b'], 'L1_attn_Wd_kv_w': _L1_attn_in['Wd_kv_w'], 'L1_attn_Wd_kv_b': _L1_attn_in['Wd_kv_b'], 'L1_attn_Wu_k_w': _L1_attn_in['Wu_k_w'], 'L1_attn_Wu_k_b': _L1_attn_in['Wu_k_b'], 'L1_attn_Wu_v_w': _L1_attn_in['Wu_v_w'], 'L1_attn_Wu_v_b': _L1_attn_in['Wu_v_b'], 'L1_attn_Wo_w': _L1_attn_in['Wo_w'], 'L1_attn_Wo_b': _L1_attn_in['Wo_b'], 'L1_ffn_router_w': _L1_ffn_in['router_w'], 'L1_ffn_gate_up_proj': _L1_ffn_in['gate_up_proj'], 'L1_ffn_down_proj': _L1_ffn_in['down_proj'], 'L1_ffn_shared_gate_w': _L1_ffn_in['shared_gate_w'], 'L1_ffn_shared_up_w': _L1_ffn_in['shared_up_w'], 'L1_ffn_shared_down_w': _L1_ffn_in['shared_down_w'], 'L1_c': _L1_c, 'L1_wmod': _L1_wmod}
    _x0 = _d['L0_attn_query']
    _d['L0_attn_query'] = jax.random.normal(jax.random.fold_in(jax.random.key(seed), 1), (4, 1024, 128), dtype=_x0.dtype)
    del _x0
    return _d

def reference(L0_attn_query, L0_attn_Wq, L0_attn_bq, L0_attn_Wk, L0_attn_bk, L0_attn_Wv, L0_attn_bv, L0_attn_Wo, L0_attn_bo, L0_ffn_Wr, L0_ffn_br, L0_ffn_W1, L0_ffn_b1, L0_ffn_W2, L0_ffn_b2, L0_c, L0_wmod, L1_attn_Wd_q_w, L1_attn_Wd_q_b, L1_attn_Wu_q_w, L1_attn_Wu_q_b, L1_attn_Wq_r_w, L1_attn_Wq_r_b, L1_attn_Wk_r_w, L1_attn_Wk_r_b, L1_attn_Wd_kv_w, L1_attn_Wd_kv_b, L1_attn_Wu_k_w, L1_attn_Wu_k_b, L1_attn_Wu_v_w, L1_attn_Wu_v_b, L1_attn_Wo_w, L1_attn_Wo_b, L1_ffn_router_w, L1_ffn_gate_up_proj, L1_ffn_down_proj, L1_ffn_shared_gate_w, L1_ffn_shared_up_w, L1_ffn_shared_down_w, L1_c, L1_wmod):

    def _L0_attn_ref(query, Wq, bq, Wk, bk, Wv, bv, Wo, bo):
        import jax, jax.numpy as jnp
        import numpy as np
        NUM_HEADS = 16
        EPS = 1e-06

        def elu_plus_one(x):
            return jax.nn.elu(x) + 1.0
        B, L, E = query.shape
        H = NUM_HEADS
        d = E // H

        def proj(x, W, b):
            return jnp.einsum('ble,fe->blf', x, W) + b

        def heads(x):
            return x.reshape(B, L, H, d).transpose(0, 2, 1, 3)
        Q = heads(proj(query, Wq, bq))
        K = heads(proj(query, Wk, bk))
        V = heads(proj(query, Wv, bv))
        phiQ = elu_plus_one(Q)
        phiK = elu_plus_one(K)
        S = jnp.einsum('bhki,bhkj->bhij', phiK, V)
        Z = phiK.sum(axis=-2)
        num = jnp.einsum('bhqi,bhij->bhqj', phiQ, S)
        denom = jnp.einsum('bhqi,bhi->bhq', phiQ, Z)[..., None] + EPS
        context = (num / denom).transpose(0, 2, 1, 3).reshape(B, L, E)
        return jnp.einsum('ble,fe->blf', context, Wo) + bo

    def _L0_ffn_ref(x, Wr, br, W1, b1, W2, b2):
        import jax, jax.numpy as jnp
        import numpy as np
        H, E, DFF = (128, 8, 512)
        B, S, Hd = x.shape
        n_exp = W1.shape[0]
        xt = x.reshape(-1, Hd)
        logits = xt @ Wr + br
        probs = jax.nn.softmax(logits, axis=-1)
        gate = jnp.max(probs, axis=-1)
        idx = jnp.argmax(probs, axis=-1)
        h1 = jnp.maximum(jnp.einsum('th,ehf->etf', xt, W1) + b1[:, None, :], 0.0)
        ye = jnp.einsum('etf,efh->eth', h1, W2) + b2[:, None, :]
        onehot = jax.nn.one_hot(idx, n_exp, dtype=xt.dtype)
        y = jnp.einsum('te,eth->th', onehot, ye) * gate[:, None]
        return y.reshape(B, S, Hd)

    def _L1_attn_ref(x, Wd_q_w, Wd_q_b, Wu_q_w, Wu_q_b, Wq_r_w, Wq_r_b, Wk_r_w, Wk_r_b, Wd_kv_w, Wd_kv_b, Wu_k_w, Wu_k_b, Wu_v_w, Wu_v_b, Wo_w, Wo_b):
        import jax, jax.numpy as jnp
        import numpy as np
        NUM_HEAD = 16
        D_Q = 64
        D_KV = 64
        ROPE_BASE = 10000.0

        def _cos_sin(seq_len, dim):
            pos = jnp.arange(seq_len, dtype=jnp.float32)[:, None]
            ids = jnp.arange(dim // 2, dtype=jnp.float32)
            theta = ROPE_BASE ** (-2.0 * ids) / (dim // 2)
            r = pos * theta[None, :]
            return (jnp.cos(r), jnp.sin(r))

        def _rope(x, cos, sin):
            b, s, d = x.shape
            xv = x.reshape(b, s, d // 2, 2)
            x0, x1 = (xv[..., 0], xv[..., 1])
            out = jnp.stack([x0 * cos - x1 * sin, x1 * cos + x0 * sin], axis=-1)
            return out.reshape(b, s, d)
        b, s, d_model = x.shape
        h = NUM_HEAD
        hd = d_model // h
        scale = jnp.sqrt(jnp.float32(h + D_KV + D_Q))

        def heads(t):
            return t.reshape(b, s, h, hd).transpose(0, 2, 1, 3)
        cos, sin = _cos_sin(s, d_model)
        ct_q = x @ Wd_q_w + Wd_q_b
        qt_c = heads(ct_q @ Wu_q_w + Wu_q_b)
        qt_r = heads(_rope(ct_q @ Wq_r_w + Wq_r_b, cos, sin))
        query = qt_c + qt_r
        ct_kv = x @ Wd_kv_w + Wd_kv_b
        kt_c = heads(ct_kv @ Wu_k_w + Wu_k_b)
        kt_r = heads(_rope(x @ Wk_r_w + Wk_r_b, cos, sin))
        key = kt_c + kt_r
        value = heads(ct_kv @ Wu_v_w + Wu_v_b)
        attn = jnp.einsum('bhqd,bhkd->bhqk', query, key) / scale
        attn = jax.nn.softmax(attn, axis=-1)
        out = jnp.einsum('bhqk,bhkd->bhqd', attn, value)
        out = out.transpose(0, 2, 1, 3).reshape(b, s, d_model)
        return out @ Wo_w + Wo_b

    def _L1_ffn_ref(hidden_states, router_w, gate_up_proj, down_proj, shared_gate_w, shared_up_w, shared_down_w):
        import jax, jax.numpy as jnp
        import numpy as np
        B, S, H = (2, 256, 128)
        N, F, SF, K = (16, 128, 512, 1)
        b, s, h = hidden_states.shape
        hidden = hidden_states.reshape(-1, h)
        t = hidden.shape[0]
        logits = hidden @ router_w.T
        top_vals, top_idx = jax.lax.top_k(logits, K)
        scores = jnp.full_like(logits, -jnp.inf)
        scores = scores.at[jnp.arange(t)[:, None], top_idx].set(top_vals)
        scores = jax.nn.sigmoid(scores.astype(jnp.float32)).astype(hidden.dtype)
        routed_in = hidden[None, :, :] * scores.T[:, :, None]
        gate_up = jnp.einsum('nth,nhf->ntf', routed_in, gate_up_proj)
        gate, up = jnp.split(gate_up, 2, axis=-1)
        routed_out = jnp.einsum('ntf,nfh->nth', up * jax.nn.silu(gate), down_proj)
        expert_sum = routed_out.sum(axis=0)
        shared = jax.nn.silu(hidden @ shared_gate_w.T) * (hidden @ shared_up_w.T) @ shared_down_w.T
        return (shared + expert_sum).reshape(b, s, h)
    x = L0_attn_query
    mod = (_silu(L0_c) @ L0_wmod).reshape(L0_c.shape[0], 6, 1, -1)
    sa, ca, ga, sb, cb, gb = (mod[:, 0], mod[:, 1], mod[:, 2], mod[:, 3], mod[:, 4], mod[:, 5])
    ga = (2 * (ga >= 0) - 1) * jnp.maximum(jnp.abs(ga), 0.25)
    gb = (2 * (gb >= 0) - 1) * jnp.maximum(jnp.abs(gb), 0.25)
    h = _layernorm(x, axis=-1) * (1 + ca) + sa
    x = x + ga * _L0_attn_ref(h, L0_attn_Wq, L0_attn_bq, L0_attn_Wk, L0_attn_bk, L0_attn_Wv, L0_attn_bv, L0_attn_Wo, L0_attn_bo)
    h = _layernorm(x, axis=-1) * (1 + cb) + sb
    x = x + gb * _L0_ffn_ref(h, L0_ffn_Wr, L0_ffn_br, L0_ffn_W1, L0_ffn_b1, L0_ffn_W2, L0_ffn_b2)
    mod = (_silu(L1_c) @ L1_wmod).reshape(L1_c.shape[0], 6, 1, -1)
    sa, ca, ga, sb, cb, gb = (mod[:, 0], mod[:, 1], mod[:, 2], mod[:, 3], mod[:, 4], mod[:, 5])
    ga = (2 * (ga >= 0) - 1) * jnp.maximum(jnp.abs(ga), 0.25)
    gb = (2 * (gb >= 0) - 1) * jnp.maximum(jnp.abs(gb), 0.25)
    h = _layernorm(x, axis=-1) * (1 + ca) + sa
    x = x + ga * _L1_attn_ref(h, L1_attn_Wd_q_w, L1_attn_Wd_q_b, L1_attn_Wu_q_w, L1_attn_Wu_q_b, L1_attn_Wq_r_w, L1_attn_Wq_r_b, L1_attn_Wk_r_w, L1_attn_Wk_r_b, L1_attn_Wd_kv_w, L1_attn_Wd_kv_b, L1_attn_Wu_k_w, L1_attn_Wu_k_b, L1_attn_Wu_v_w, L1_attn_Wu_v_b, L1_attn_Wo_w, L1_attn_Wo_b)
    h = _layernorm(x, axis=-1) * (1 + cb) + sb
    x = x + gb * _L1_ffn_ref(h, L1_ffn_router_w, L1_ffn_gate_up_proj, L1_ffn_down_proj, L1_ffn_shared_gate_w, L1_ffn_shared_up_w, L1_ffn_shared_down_w)
    return x

_drawn_inputs = setup_inputs


def setup_inputs(seed=0):
    import zlib

    import numpy as np

    out = dict(_drawn_inputs(seed))
    spreads = {'L0_ffn_br': (0.0, 0.32),
     'L0_ffn_b1': (0.0, 0.8),
     'L0_ffn_b2': (0.0, 0.8),
     'L1_attn_Wd_q_b': (0.0, 0.8),
     'L1_attn_Wu_q_b': (0.0, 0.8),
     'L1_attn_Wq_r_b': (0.0, 0.8),
     'L1_attn_Wk_r_b': (0.0, 0.8),
     'L1_attn_Wd_kv_b': (0.0, 0.8),
     'L1_attn_Wu_k_b': (0.0, 0.8),
     'L1_attn_Wu_v_b': (0.0, 0.8),
     'L1_attn_Wo_b': (0.0, 0.298)}
    factors = {'L0_attn_Wq': 8.0,
     'L0_attn_bq': 8.0,
     'L0_attn_Wk': 7.021,
     'L0_attn_bk': 8.0,
     'L0_attn_Wv': 5.146,
     'L0_attn_bv': 8.0,
     'L0_attn_Wo': 5.082,
     'L0_attn_bo': 8.0,
     'L1_attn_Wd_q_w': 8.0,
     'L1_attn_Wu_q_w': 8.0,
     'L1_attn_Wq_r_w': 8.0,
     'L1_attn_Wk_r_w': 8.0,
     'L1_attn_Wd_kv_w': 8.0,
     'L1_attn_Wu_k_w': 8.0,
     'L1_attn_Wu_v_w': 8.0,
     'L1_attn_Wo_w': 8.0,
     'L1_ffn_router_w': 8.0,
     'L1_ffn_gate_up_proj': 8.0,
     'L1_ffn_down_proj': 8.0,
     'L1_ffn_shared_gate_w': 8.0,
     'L1_ffn_shared_up_w': 8.0,
     'L1_ffn_shared_down_w': 8.0}
    for name, (base, spread) in spreads.items():
        noise = np.random.default_rng([zlib.crc32(name.encode()), seed]).standard_normal(out[name].shape)
        drawn = base * np.exp(spread * noise) if base else spread * noise
        out[name] = jnp.asarray(drawn.astype(out[name].dtype))
    for name, factor in factors.items():
        out[name] = (out[name] * factor).astype(out[name].dtype)
    return out
```

```python
from contextlib import ExitStack

import concourse.bass as bass
import numpy as np
from concourse import mybir

F32, BF16, I32, U32 = mybir.dt.float32, mybir.dt.bfloat16, mybir.dt.int32, mybir.dt.uint32
ALU = mybir.AluOpType
ACT = mybir.ActivationFunctionType
AX = mybir.AxisListType

P = 128
B, L = 4, 1024
TB = L // P
NT = B * TB
H, HD = 16, 8
E0, F0 = 8, 512
E1, F1 = 16, 128
FS = 512
DR = 64
NS0 = NT + E0
NS1 = NT + E1
FC0 = F0 // P
FCS = FS // P
SA, CA, GA, SB, CB, GB = range(6)
LN_EPS = 1e-5
DEN_EPS = 1e-6
INV_SCALE = 1.0 / 12.0
NPART = 6
KROWS = NPART * HD
MROWS = 3
VW = 32


class Link:

    def __init__(self, eng, sem, base=0):
        self.eng, self.sem, self.base, self.n = eng, sem, base, 0

    def __call__(self, ins):
        self.n += 1
        ins.then_inc(self.sem, 1)
        self.eng.wait_ge(self.sem, self.base + self.n)


class Names:

    turn, halves = 0, ()

    @classmethod
    def start(cls, nc):
        free = list(nc.free_semaphores)
        cls.turn, cls.halves = 0, (free[0::2], free[1::2])

    def __init__(self, nc, prefix=""):
        self.nc, self.prefix, self.ctx, self.sems = nc, prefix, ExitStack(), []
        if prefix:
            self.numbers = iter(Names.halves[Names.turn])
            Names.turn = 1 - Names.turn

    def __enter__(self):
        return self

    def __exit__(self, *a):
        if self.sems:
            self.nc.clear_and_free_semaphores(self.sems)
        return self.ctx.__exit__(*a)

    def sb(self, name, shape, dt=F32):
        return self.ctx.enter_context(self.nc.sbuf_tensor(self.prefix + name, shape, dt))

    def ps(self, name, shape, dt=F32):
        return self.ctx.enter_context(self.nc.psum_tensor(self.prefix + name, shape, dt))

    def sem(self, name):
        self.sems.append(self.nc.alloc_semaphore(self.prefix + name, next(self.numbers)))
        return self.sems[-1]


def wait_apart(eng, sem, value, least=1):
    value = value if isinstance(value, int) else eng.to_reg(value)
    eng.wait_ge(sem, least)
    eng.wait_ge(sem, value)


def batches(eng, n, body):
    body(0, True)
    with eng.Fori(1, n) as i:
        body(i, False)


def phase_load(nc, D, M):
    with Names(nc, "ld_") as n:
        ld_x, ld_w = n.sem("ld_x"), n.sem("ld_w")
        ld_c, zero_ready = n.sem("ld_c"), n.sem("zero_ready")
        act_done, dve_step, sc_ready = n.sem("act_done"), n.sem("dve_step"), n.sem("sc_ready")
        mod_mm, mod_out = n.sem("mod_mm"), n.sem("mod_out")
        col_mm = n.sem("col_mm")
        wmod = n.sb("wmod", [P, 2, 6 * P])
        cT = n.sb("cT", [P, 2, B])
        e = n.sb("sig_e", [P, 2, B])
        sc = n.sb("silu_c", [P, 2, B])
        scb = n.sb("silu_c_bc", [P, 2 * B, P])
        mod_ps = [n.ps(f"mod_ps{i}", [P, 1024]) for i in range(2)]
        col_ps = n.ps("col_ps", [P, 512])
        w_loads = [
            (M.ident, D["ident"]), (M.wq0, D["wq0"]), (M.wkv0, D["wkv0"]), (M.wo0, D["wo0"]),
            (M.bq0, D["bq0"]), (M.bkv0, D["bkv0"].partition_broadcast(P)), (M.bo0, D["bo0"].partition_broadcast(P)),
            (M.blockmask, D["blockmask"]), (M.headmask, D["headmask"]),
        ]
        w_late = [
            (M.tri, D["tri"]), (M.onesm, D["onesm"]), (M.idents, D["idents"].partition_broadcast(P)),
            (M.tiles, D["tiles"].partition_broadcast(P)),
            (M.wr0, D["wr0"]), (M.br0, D["br0"].partition_broadcast(P)),
            (M.w10, D["w10"]), (M.w20, D["w20"]),
            (M.b10, D["b10"].partition_broadcast(P)), (M.b20, D["b20"].partition_broadcast(P)),
            (M.wd1, D["wd1"]), (M.wuq1, D["wuq1"]), (M.wukv1, D["wukv1"]), (M.wkr1, D["wkr1"]),
            (M.bcol1, D["bcol1"]), (M.bv1, D["bv1"].partition_broadcast(P)),
            (M.wo1, D["wo1"]), (M.bo1, D["bo1"].partition_broadcast(P)),
            (M.wr1, D["wr1"]),
        ]
        with nc.Block() as block:
            @block.sync
            def _(sp):
                sp.dma_start(cT[:], D["cT"]).then_inc(ld_c, 16)
                sp.dma_start(wmod[:], D["wmod"]).then_inc(ld_c, 16)
                for b in range(B):
                    sp.dma_start(M.x[:, b * TB:(b + 1) * TB, :],
                                 D["x"][b].rearrange("(t p) e -> p t e", p=P)).then_inc(ld_x, 16)
                sp.wait_ge(zero_ready, 1)
                for l, ns in enumerate((NS0, NS1)):
                    sp.dma_start(M.sorted[l].rearrange("(s p) e -> p s e", p=P),
                                 M.zeros[:].unsqueeze(1).to_broadcast([P, ns, P])).then_inc(ld_w, 16)
                for dst, src in w_loads:
                    sp.dma_start(dst[:], src).then_inc(ld_w, 16)
                for dst, src in w_late:
                    sp.dma_start(dst[:], src).then_inc(ld_w, 16)
                sp.wait_ge(ld_w, 16 * (2 + len(w_loads) + len(w_late)))

            @block.scalar
            def _(act):
                act.wait_ge(ld_c, 32)
                act.activation(e[:], cT[:], ACT.Exp, scale=-1.0).then_inc(act_done, 1)

            @block.tensor
            def _(pe):
                pe.wait_ge(sc_ready, 1)
                for k in range(2 * B):
                    if k >= 2:
                        pe.wait_ge(mod_out, k - 1)
                    for c0, c1 in ((0, 512), (512, 768)):
                        mm = pe.matmul(mod_ps[k % 2][:, c0:c1], scb[:, k, :], wmod[:, k // B, c0:c1],
                                       start=True, stop=True)
                    mm.then_inc(mod_mm, 1)
                for l in range(2):
                    for j in (SA, CA):
                        mm = pe.matmul(col_ps[:, (2 * l + j) * B:(2 * l + j + 1) * B],
                                       wmod[:, l, j * P:(j + 1) * P], sc[:, l, :], start=True, stop=True)
                mm.then_inc(col_mm, 1)

            @block.vector
            def _(dve):
                link = Link(dve, dve_step)
                dve.memset(M.zeros[:], 0.0).then_inc(zero_ready, 1)
                link(dve.memset(M.half[:], -0.5))
                dve.wait_ge(ld_w, 16 * (2 + len(w_loads) + len(w_late)))
                dve.tensor_copy(M.identb[:], M.ident[:])
                dve.wait_ge(act_done, 1)
                link(dve.tensor_scalar(e[:], e[:], 1.0, None, ALU.add))
                link(dve.reciprocal(e[:], e[:]))
                link(dve.tensor_tensor(sc[:], cT[:], e[:], ALU.mult))
                dve.tensor_copy(scb[:], sc[:].rearrange("p l b -> p (l b)").unsqueeze(2).to_broadcast([P, 2 * B, P])).then_inc(sc_ready, 1)
                for b in range(B):
                    dve.wait_ge(ld_x, 16 * B)
                    for t in range(b * TB, (b + 1) * TB):
                        dve.bn_stats(M.stats[:, t, :], M.x[:, t, :])
                for k in range(2 * B):
                    dve.wait_ge(mod_mm, k + 1)
                    dve.tensor_copy(M.mod[:, k // B, k % B, :], mod_ps[k % 2][:, 0:6 * P]).then_inc(mod_out, 1)
                dve.wait_ge(mod_out, 2 * B)
                dve.wait_ge(col_mm, 1)
                link(dve.tensor_copy(M.modcol[:], col_ps[:, 0:4 * B].rearrange("p (l j b) -> p l j b", l=2, j=2)))
                link(dve.tensor_scalar(M.modcol[:, :, 1, :], M.modcol[:, :, 1, :], 1.0, None, ALU.add))
                for l in range(2):
                    cb = M.mod[:, l, :, CB * P:(CB + 1) * P]
                    link(dve.tensor_scalar(cb, cb, 1.0, None, ALU.add))
                    for g in (GA, GB):
                        gv = M.mod[:, l, :, g * P:(g + 1) * P]
                        s = scb[:, 0:B, :]
                        a = scb[:, B:2 * B, :]
                        link(dve.tensor_scalar(s, gv, 0.0, 2.0, ALU.is_ge, ALU.mult))
                        link(dve.tensor_scalar(a, gv, -1.0, None, ALU.mult))
                        link(dve.tensor_tensor(a, a, gv, ALU.max))
                        link(dve.tensor_scalar(a, a, 0.25, None, ALU.max))
                        link(dve.scalar_tensor_tensor(out=gv, in0=s, scalar=-1.0, in1=a, op0=ALU.add, op1=ALU.mult))


def mean_and_rstd(dve, pool, link, M, var_ready, rstd_ready):
    st = M.stats
    if dve is not None:
        link(dve.tensor_tensor(M.ln_d[:], st[:, :, 1], st[:, :, 4], ALU.subtract))
        link(dve.scalar_tensor_tensor(out=M.ln_v[:], in0=M.ln_d[:], scalar=P / 4.0, in1=M.ln_d[:],
                                      op0=ALU.mult, op1=ALU.mult))
        link(dve.tensor_tensor(M.ln_v[:], M.ln_v[:], st[:, :, 2], ALU.add))
        link(dve.tensor_tensor(M.ln_v[:], M.ln_v[:], st[:, :, 5], ALU.add))
        dve.tensor_scalar(M.ln_v[:], M.ln_v[:], 1.0 / P, LN_EPS, ALU.mult, ALU.add).then_inc(var_ready, 1)
        link(dve.tensor_tensor(M.mean[:], st[:, :, 1], st[:, :, 4], ALU.add))
        link(dve.tensor_scalar(M.mean[:], M.mean[:], 0.5, None, ALU.mult))
    if pool is not None:
        pool.wait_ge(var_ready, 1)
        pool.tensor_tensor(M.rstd[:], M.ln_v[:], M.half[:], ALU.pow).then_inc(rstd_ready, 1)


def phase_linear_attention(nc, D, M):
    with Names(nc, "la_") as n:
        var_ready, rstd_ready = n.sem("var_ready"), n.sem("rstd_ready")
        dve_ln, dve_step = n.sem("dve_ln"), n.sem("dve_step")
        xn_ready, xn_T, hT_ready = n.sem("xn_ready"), n.sem("xn_T"), n.sem("hT_ready")
        kv_ones = n.sem("kv_ones")
        q_neg, k_neg = n.sem("q_neg"), n.sem("k_neg")
        q_mm, q_act, phiq_ready = n.sem("q_mm"), n.sem("q_act"), n.sem("phiq_ready")
        kv_mm, kv_bias, k_act, phik_ready = n.sem("kv_mm"), n.sem("kv_bias"), n.sem("k_act"), n.sem("phik_ready")
        s_mm, s_ready, num_mm, ctx_ready = n.sem("s_mm"), n.sem("s_ready"), n.sem("num_mm"), n.sem("ctx_ready")
        ctx_T, ctxT_ready, wog_ready, bog_added = n.sem("ctx_T"), n.sem("ctxT_ready"), n.sem("wog_ready"), n.sem("bog_added")
        pool_step, o_mm, x_done = n.sem("pool_step"), n.sem("o_mm"), n.sem("x_done")
        psT = n.ps("psT", [P, L])
        psQ = n.ps("psQ", [P, L])
        psKV = n.ps("psKV", [P, 2 * L])
        xn = n.sb("xn", [P, TB, P])
        hT = n.sb("hT", [P, L])
        eq, rq, phiq = n.sb("eq", [P, L]), n.sb("rq", [P, L]), n.sb("phiq", [P, L])
        ek, rk, phik = n.sb("ek", [P, TB, P]), n.sb("rk", [P, TB, P]), n.sb("phik", [P, TB, P])
        kvb = n.sb("kvb", [P, TB, 2 * P + 1])
        sm = n.sb("sm", [P, P + H])
        rden = n.sb("rden", [P, TB, H])
        ctx = n.sb("ctx", [P, TB, P])
        ctxT = n.sb("ctxT", [P, L])
        wog, bog = n.sb("wog", [P, P]), n.sb("bog", [P, P])
        NW = P + H
        TPK = 512 // NW
        groups = [(t, min(t + TPK, TB)) for t in range(0, TB, TPK)]

        def num_at(t):
            return psKV[:, (t // TPK) * 512 + (t % TPK) * NW:(t // TPK) * 512 + (t % TPK + 1) * NW]

        NG = len(groups)

        with nc.Block() as block:
            @block.gpsimd
            def _(pool):
                mean_and_rstd(None, pool, None, M, var_ready, rstd_ready)

                def batch(b, first):
                    if not first:
                        pool.wait_ge(o_mm, b * 2)
                        pool.wait_ge(bog_added, b)
                    ga = M.mod[:, 0, b, GA * P:(GA + 1) * P]
                    pool.tensor_tensor(bog[:], M.bo0[:], ga, ALU.mult).then_inc(pool_step, 1)
                    pool.tensor_tensor(wog[:], M.wo0[:], ga, ALU.mult).then_inc(wog_ready, 1)
                    pool.wait_ge(pool_step, b + 1)
                    pool.wait_ge(k_act, b * 2 + 2)
                    pool.tensor_tensor(phik[:], ek[:], rk[:], ALU.add).then_inc(phik_ready, 1)
                    pool.wait_ge(xn_ready, b * TB + TB)
                    xb = M.x[:, bass.ds(b * TB, TB), :]
                    pool.tensor_tensor(xb, xb, bog[:].unsqueeze(1).to_broadcast([P, TB, P]),
                                       ALU.add).then_inc(bog_added, 1)

                batches(pool, B, batch)

            @block.vector
            def _(dve):
                dve.memset(kvb[:, :, 2 * P:2 * P + 1], 1.0).then_inc(kv_ones, 1)
                mean_and_rstd(dve, None, Link(dve, dve_ln), M, var_ready, rstd_ready)
                dve.wait_ge(rstd_ready, 1)

                def batch(b, first):
                    link = Link(dve, dve_step, b * (2 * NG + 2))
                    if not first:
                        dve.wait_ge(xn_T, b * 2)
                    for t in range(TB):
                        i = b * TB + t
                        dve.tensor_scalar(xn[:, t, :], M.x[:, i, :], M.mean[:, bass.ds(i, 1)],
                                          M.rstd[:, bass.ds(i, 1)], ALU.subtract, ALU.mult).then_inc(xn_ready, 1)
                    if not first:
                        dve.wait_ge(num_mm, b * NG)
                    for j in range(2):
                        dve.wait_ge(q_mm, b * 2 + j + 1)
                        cols = slice(j * 512, (j + 1) * 512)
                        dve.tensor_scalar(eq[:, cols], psQ[:, cols], M.bq0[:, 0:1], 0.0, ALU.add,
                                          ALU.min).then_inc(q_neg, 1)
                    for j in range(4):
                        dve.wait_ge(kv_mm, b * 4 + j + 1)
                        dve.tensor_tensor(kvb[:, 2 * j:2 * j + 2, 0:2 * P],
                                          psKV[:, j * 512:(j + 1) * 512].rearrange("p (t f) -> p t f", t=2),
                                          M.bkv0[:].unsqueeze(1).to_broadcast([P, 2, 2 * P]),
                                          ALU.add).then_inc(kv_bias, 1)
                    dve.wait_ge(kv_bias, b * 4 + 4)
                    dve.tensor_scalar(ek[:], kvb[:, :, 0:P], 0.0, None, ALU.min).then_inc(k_neg, 1)
                    dve.wait_ge(q_act, b * 2 + 2)
                    dve.tensor_tensor(phiq[:], eq[:], rq[:], ALU.add).then_inc(phiq_ready, 1)
                    dve.wait_ge(s_mm, b + 1)
                    dve.tensor_tensor(sm[:, 0:P], psT[:, 0:P], M.blockmask[:], ALU.mult).then_inc(s_ready, 1)
                    dve.tensor_scalar(sm[:, P:NW], M.headmask[:], psT[:, P:P + 1], None, ALU.mult).then_inc(s_ready, 1)
                    for g, (t0, t1) in enumerate(groups):
                        dve.wait_ge(num_mm, b * NG + g + 1)
                        nd = psKV[:, g * 512:g * 512 + (t1 - t0) * NW].rearrange("p (t f) -> p t f", f=NW)
                        link(dve.tensor_scalar(rden[:, t0:t1, :], nd[:, :, P:NW], DEN_EPS, None, ALU.add))
                        link(dve.reciprocal(rden[:, t0:t1, :], rden[:, t0:t1, :]))
                        dve.tensor_tensor(ctx[:, t0:t1, :].rearrange("p t (h d) -> p t h d", h=H),
                                          nd[:, :, 0:P].rearrange("p t (h d) -> p t h d", h=H),
                                          rden[:, t0:t1, :].unsqueeze(3).to_broadcast([P, t1 - t0, H, HD]),
                                          ALU.mult).then_inc(ctx_ready, 1)
                    dve.wait_ge(bog_added, b + 1)
                    for j in range(2):
                        dve.wait_ge(o_mm, b * 2 + j + 1)
                        xj = M.x[:, bass.ds(b * TB + 4 * j, 4), :]
                        link(dve.tensor_tensor(xj, xj, psT[:, j * 512:(j + 1) * 512].rearrange("p (t f) -> p t f", t=4),
                                               ALU.add))
                        for t in range(4 * j, 4 * j + 4):
                            ins = dve.bn_stats(M.stats[:, b * TB + t, :], M.x[:, b * TB + t, :])
                    ins.then_inc(x_done, 1)

                batches(dve, B, batch)

            @block.scalar
            def _(act):
                def batch(b, first):
                    if not first:
                        act.wait_ge(s_mm, b)
                        act.wait_ge(num_mm, b * NG)
                    for j in range(2):
                        wait_apart(act, xn_T, b * 2 + j + 1)
                        act.activation(hT[:, j * 512:(j + 1) * 512], psT[:, j * 512:(j + 1) * 512], ACT.Identity,
                                       bias=M.modcol[:, 0, 0, bass.ds(b, 1)],
                                       scale=M.modcol[:, 0, 1, bass.ds(b, 1)]).then_inc(hT_ready, 1)
                    for j in range(2):
                        cols = slice(j * 512, (j + 1) * 512)
                        act.wait_ge(q_neg, b * 2 + j + 1)
                        act.activation(rq[:, cols], psQ[:, cols], ACT.Relu, bias=M.bq0[:, 0:1])
                        act.activation(eq[:, cols], eq[:, cols], ACT.Exp).then_inc(q_act, 1)
                    act.wait_ge(kv_bias, b * 4 + 4)
                    act.activation(rk[:], kvb[:, :, 0:P], ACT.Relu).then_inc(k_act, 1)
                    act.wait_ge(k_neg, b + 1)
                    act.activation(ek[:], ek[:], ACT.Exp).then_inc(k_act, 1)
                    for j in range(2):
                        act.wait_ge(ctx_T, b * 2 + j + 1)
                        act.activation(ctxT[:, j * 512:(j + 1) * 512], psQ[:, j * 512:(j + 1) * 512],
                                       ACT.Copy).then_inc(ctxT_ready, 1)

                batches(act, B, batch)

            @block.tensor
            def _(pe):
                def batch(b, first):
                    if not first:
                        pe.wait_ge(x_done, b)
                    for t in range(TB):
                        pe.wait_ge(xn_ready, b * TB + t + 1)
                        mm = pe.transpose(psT[:, t * P:(t + 1) * P], xn[:, t, :], M.ident[:])
                        if t % 4 == 3:
                            mm.then_inc(xn_T, 1)
                    for j in range(2):
                        pe.wait_ge(hT_ready, b * 2 + j + 1)
                        cols = slice(j * 512, (j + 1) * 512)
                        pe.matmul(psQ[:, cols], M.wq0[:], hT[:, cols], start=True, stop=True).then_inc(q_mm, 1)
                    for t in range(TB):
                        mm = pe.matmul(psKV[:, t * 256:(t + 1) * 256], hT[:, t * P:(t + 1) * P], M.wkv0[:],
                                       start=True, stop=True)
                        if t % 2 == 1:
                            mm.then_inc(kv_mm, 1)
                    pe.wait_ge(phik_ready, b + 1)
                    if first:
                        pe.wait_ge(kv_ones, 1)
                    for t in range(TB):
                        mm = pe.matmul(psT[:, 0:P + 1], phik[:, t, :], kvb[:, t, P:2 * P + 1],
                                       start=(t == 0), stop=(t == TB - 1))
                    mm.then_inc(s_mm, 1)
                    pe.wait_ge(phiq_ready, b + 1)
                    pe.wait_ge(s_ready, b * 2 + 2)
                    for g, (t0, t1) in enumerate(groups):
                        for t in range(t0, t1):
                            mm = pe.matmul(num_at(t), phiq[:, t * P:(t + 1) * P], sm[:], start=True, stop=True)
                        mm.then_inc(num_mm, 1)
                    for t in range(TB):
                        pe.wait_ge(ctx_ready, b * NG + t // TPK + 1)
                        mm = pe.transpose(psQ[:, t * P:(t + 1) * P], ctx[:, t, :], M.ident[:])
                        if t % 4 == 3:
                            mm.then_inc(ctx_T, 1)
                    pe.wait_ge(wog_ready, b + 1)
                    for t in range(TB):
                        pe.wait_ge(ctxT_ready, b * 2 + t // 4 + 1)
                        mm = pe.matmul(psT[:, t * P:(t + 1) * P], ctxT[:, t * P:(t + 1) * P], wog[:],
                                       start=True, stop=True)
                        if t % 4 == 3:
                            mm.then_inc(o_mm, 1)

                batches(pe, B, batch)


def phase_route(nc, D, M, l):
    E, NS, wr = ((E0, NS0, M.wr0), (E1, NS1, M.wr1))[l]
    with Names(nc, f"rt{l}_") as n:
        var_ready, rstd_ready = n.sem("var_ready"), n.sem("rstd_ready")
        dve_ln, dve_step = n.sem("dve_ln"), n.sem("dve_step")
        xn_ready, h_ready, h_T, hT_ready = n.sem("xn_ready"), n.sem("h_ready"), n.sem("h_T"), n.sem("hT_ready")
        lg_mm, lg_out, shifted, exp_done = n.sem("lg_mm"), n.sem("lg_out"), n.sem("shifted"), n.sem("exp_done")
        oh_ready, rank_mm, slot_ready, scattered = n.sem("oh_ready"), n.sem("rank_mm"), n.sem("slot_ready"), n.sem("scattered")
        dve_rt, half_done = n.sem("dve_rt"), n.sem("half_done")
        psT = [n.ps(f"psT{i}", [P, 512]) for i in range(2)]
        psL = [n.ps(f"psL{i}", [P, TB * E]) for i in range(2)]
        psR, psN = n.ps("psR", [P, NT * E]), n.ps("psN", [P, NT * E])
        xn = n.sb("xn", [P, TB, P])
        lg, t1, oh = n.sb("lg", [P, NT, E]), n.sb("t1", [P, NT, E]), n.sb("oh", [P, NT, E])
        scan = [n.sb(f"scan{i}", [P, NT, E]) for i in range(2)]
        tot = n.sb("tot", [P, NT, E])
        r1 = n.sb("r1", [P, NT])
        cnt = [n.sb(f"cnt{i}", [P, E]) for i in range(3)]
        cnti = n.sb("cnti", [P, E], I32)
        cmp, cmps = n.sb("cmp", [1, NS, E]), n.sb("cmps", [1, NS])
        posf = n.sb("posf", [P, NT])

        def per_tile(v):
            return v.unsqueeze(2).to_broadcast([P, NT, E])

        def per_expert(v, k=NT):
            return v.unsqueeze(1).to_broadcast([v.shape[0], k, E])

        ld_experts = n.sem("ld_experts")

        with nc.Block() as block:
            @block.sync
            def _(sp):
                if l == 1:
                    for dst, name in ((M.wgu1, "wgu1"), (M.wdn1, "wdn1"), (M.wsg1, "wsg1"), (M.wsd1, "wsd1")):
                        sp.dma_start(dst[:], D[name]).then_inc(ld_experts, 16)
                    sp.wait_ge(ld_experts, 16 * 4)

            @block.vector
            def _(dve):
                mean_and_rstd(dve, None, Link(dve, dve_ln), M, var_ready, rstd_ready)
                dve.wait_ge(rstd_ready, 1)

                def batch(b, first):
                    link = Link(dve, dve_step, b * (TB + 1))
                    for t in range(TB):
                        i = b * TB + t
                        ins = dve.tensor_scalar(xn[:, t, :], M.x[:, i, :], M.mean[:, bass.ds(i, 1)],
                                                M.rstd[:, bass.ds(i, 1)], ALU.subtract, ALU.mult)
                        ins.then_inc(dve_step, 1)
                        link.n += 1
                    dve.wait_ge(dve_step, link.base + link.n)
                    link(dve.tensor_tensor(xn[:], xn[:], M.mod[:, l, b, CB * P:(CB + 1) * P].unsqueeze(1).to_broadcast([P, TB, P]),
                                           ALU.mult))
                    dve.tensor_tensor(M.h[:, bass.ds(b * TB, TB), :], xn[:],
                                      M.mod[:, l, b, SB * P:(SB + 1) * P].unsqueeze(1).to_broadcast([P, TB, P]),
                                      ALU.add).then_inc(h_ready, 1)

                def batch_all(b, first):
                    if not first:
                        dve.wait_ge(h_ready, b)
                    batch(b, first)

                batches(dve, B, batch_all)
                for b in range(B):
                    dve.wait_ge(lg_mm, b + 1)
                    src = psL[b % 2][:].rearrange("p (t e) -> p t e", e=E)
                    dst = lg[:, b * TB:(b + 1) * TB, :]
                    if l == 0:
                        dve.tensor_tensor(dst, src, per_expert(M.br0[:], TB), ALU.add).then_inc(lg_out, 1)
                    else:
                        dve.tensor_copy(dst, src).then_inc(lg_out, 1)
                dve.wait_ge(lg_out, B)
                link = Link(dve, dve_rt)
                link(dve.tensor_reduce(r1[:], lg[:], AX.X, ALU.max))
                if l == 0:
                    dve.tensor_tensor(t1[:], lg[:], per_tile(r1[:]), ALU.subtract).then_inc(shifted, 1)
                    dve.wait_ge(exp_done, 1)
                    link(dve.tensor_reduce(posf[:], t1[:], AX.X, ALU.add))
                    link(dve.tensor_reduce(r1[:], t1[:], AX.X, ALU.max))
                    link(dve.reciprocal(posf[:], posf[:]))
                    link(dve.tensor_tensor(M.gate[:], r1[:], posf[:], ALU.mult))
                    link(dve.tensor_tensor(oh[:], t1[:], per_tile(r1[:]), ALU.is_equal))
                else:
                    dve.tensor_scalar(posf[:], r1[:], -1.0, 88.0, ALU.mult, ALU.min).then_inc(shifted, 1)
                    dve.wait_ge(exp_done, 1)
                    link(dve.tensor_scalar(posf[:], posf[:], 1.0, None, ALU.add))
                    link(dve.reciprocal(M.gate[:], posf[:]))
                    link(dve.tensor_tensor(oh[:], lg[:], per_tile(r1[:]), ALU.is_equal))
                link(dve.scalar_tensor_tensor(out=t1[:], in0=oh[:], scalar=-64.0, in1=per_expert(M.idents[:, 0:E]),
                                              op0=ALU.mult, op1=ALU.add))
                link(dve.tensor_reduce(r1[:], t1[:], AX.X, ALU.min))
                dve.tensor_tensor(oh[:], t1[:], per_tile(r1[:]), ALU.is_equal).then_inc(oh_ready, 1)
                if l == 1:
                    dve.wait_ge(h_T, 2 * B)
                    for i in range(NT):
                        dve.tensor_scalar(M.h[:, i, :], M.h[:, i, :], M.gate[:, i:i + 1], None, ALU.mult).then_inc(half_done, 1)
                dve.wait_ge(rank_mm, 2)
                link(dve.tensor_copy(tot[:], psN[:].rearrange("p (t e) -> p t e", e=E)))
                src, d, k = tot, 1, 0
                while d < NT:
                    dst = scan[k % 2]
                    link(dve.tensor_copy(dst[:, 0:d, :], src[:, 0:d, :]))
                    link(dve.tensor_tensor(dst[:, d:NT, :], src[:, d:NT, :], src[:, 0:NT - d, :], ALU.add))
                    src, d, k = dst, 2 * d, k + 1
                link(dve.tensor_scalar(cnt[0][:], src[:, NT - 1, :], float(P - 1), None, ALU.add))
                link(dve.tensor_copy(cnti[:], cnt[0][:]))
                link(dve.tensor_scalar(cnti[:], cnti[:], P.bit_length() - 1, None, ALU.arith_shift_right))
                link(dve.tensor_copy(cnt[2][:], cnti[:]))
                ends, d, k = cnt[2], 1, 0
                while d < E:
                    dst = cnt[k % 2]
                    link(dve.tensor_copy(dst[:, 0:d], ends[:, 0:d]))
                    link(dve.tensor_tensor(dst[:, d:E], ends[:, d:E], ends[:, 0:E - d], ALU.add))
                    ends, d, k = dst, 2 * d, k + 1
                starts = cnt[k % 2]
                link(dve.tensor_tensor(starts[:], ends[:], cnt[2][:], ALU.subtract))
                link(dve.tensor_tensor(t1[:], src[:], tot[:], ALU.subtract))
                link(dve.scalar_tensor_tensor(out=t1[:], in0=per_expert(starts[:]), scalar=float(P), in1=t1[:],
                                              op0=ALU.mult, op1=ALU.add))
                link(dve.tensor_tensor(t1[:], t1[:], psR[:].rearrange("p (t e) -> p t e", e=E), ALU.add))
                link(dve.tensor_tensor(t1[:], t1[:], oh[:], ALU.mult))
                link(dve.tensor_reduce(posf[:], t1[:], AX.X, ALU.add))
                dve.tensor_copy(M.slot[:], posf[:]).then_inc(slot_ready, 1)
                link(dve.tensor_tensor(cmp[:], M.tiles[0:1, 0:NS].unsqueeze(2).to_broadcast([1, NS, E]),
                                       per_expert(ends[0:1, :], NS), ALU.is_ge))
                link(dve.tensor_reduce(cmps[:], cmp[:], AX.X, ALU.add))
                link(dve.tensor_scalar(cmps[:], cmps[:], float(E - 1), None, ALU.min))
                link(dve.tensor_copy(M.expert[:, 0:NS], cmps[:]))

            @block.gpsimd
            def _(pool):
                mean_and_rstd(None, pool, None, M, var_ready, rstd_ready)
                pool.wait_ge(slot_ready, 1)
                if l == 1:
                    pool.wait_ge(half_done, NT)
                for i in range(NT):
                    pool.indirect_dma_start(
                        out=M.sorted[l][:, :], out_offset=bass.IndirectOffsetOnAxis(ap=M.slot[:, i:i + 1], axis=0),
                        in_=M.h[:, i, :], in_offset=None).then_inc(scattered, 16)
                pool.wait_ge(scattered, 16 * NT)

            @block.tensor
            def _(pe):
                for b in range(B):
                    pe.wait_ge(h_ready, b + 1)
                    for j in range(2):
                        if b >= 1:
                            pe.wait_ge(hT_ready, 2 * (b - 1) + j + 1)
                        for t in range(4):
                            mm = pe.transpose(psT[j][:, t * P:(t + 1) * P], M.h[:, b * TB + 4 * j + t, :], M.ident[:])
                        mm.then_inc(h_T, 1)
                    if b >= 2:
                        pe.wait_ge(lg_out, b - 1)
                    for t in range(TB):
                        pe.wait_ge(hT_ready, 2 * b + t // 4 + 1)
                        i = b * TB + t
                        mm = pe.matmul(psL[b % 2][:, t * E:(t + 1) * E], M.hT[:, i * P:(i + 1) * P], wr[:],
                                       start=True, stop=True)
                    mm.then_inc(lg_mm, 1)
                pe.wait_ge(oh_ready, 1)
                flat = oh[:].rearrange("p t e -> p (t e)")
                pe.matmul(psR[:], M.tri[:], flat, start=True, stop=True).then_inc(rank_mm, 1)
                pe.matmul(psN[:], M.onesm[:], flat, start=True, stop=True).then_inc(rank_mm, 1)

            @block.scalar
            def _(act):
                for b in range(B):
                    for j in range(2):
                        act.wait_ge(h_T, 2 * b + j + 1)
                        c = (2 * b + j) * 512
                        act.activation(M.hT[:, c:c + 512], psT[j][:], ACT.Copy).then_inc(hT_ready, 1)
                act.wait_ge(shifted, 1)
                v = t1 if l == 0 else posf
                act.activation(v[:], v[:], ACT.Exp).then_inc(exp_done, 1)


class Steps:

    UNROLL = 8

    def __init__(self, n, lag):
        assert n % self.UNROLL == 0
        self.n, self.lag = n, lag

    def run(self, eng, step):
        for r in range(self.UNROLL):
            step(0, r)
        with eng.Fori(1, self.n // self.UNROLL) as i:
            for r in range(self.UNROLL):
                step(i, r)
        for r in range(self.lag):
            step(self.n // self.UNROLL, r)

    def has(self, j):
        return not isinstance(j, int) or 0 <= j < self.n


def after(j, k):
    return not isinstance(j, int) or j >= k


GT = 4


def move_tiles(sp, n, src, dst, rows, y, loaded, stored, x_T, y_ready):
    ng = n // GT

    def group(g, q):
        if not isinstance(g, int) or g < ng:
            if not isinstance(g, int) or g >= 2:
                wait_apart(sp, x_T, g - 1)
            sp.dma_start(rows[q][:], src[:, bass.ds(g * GT, GT), :]).then_inc(loaded[q], 16)
        if not isinstance(g, int) or g >= 2:
            wait_apart(sp, y_ready, (g - 1) * GT)
            sp.dma_start(dst[:, bass.ds((g - 2) * GT, GT), :], y[q][:]).then_inc(stored[q], 16)

    for q in range(2):
        group(q, q)
    with sp.Fori(1, ng // 2) as i:
        for q in range(2):
            group(i * 2 + q, q)
    for q in range(2):
        group(ng + q, q)
    for q in range(2):
        sp.wait_ge(stored[q], 16 * (ng // 2))


def phase_experts0(nc, D, M):
    S = Steps(NS0, 3)
    U = S.UNROLL
    with Names(nc, "e0_") as n:
        loaded = [n.sem(f"loaded{i}") for i in range(2)]
        x_T, xT_ready, mm1_done, h1_ready = n.sem("x_T"), n.sem("xT_ready"), n.sem("mm1_done"), n.sem("h1_ready")
        h1_T, h1T_ready, mm2_done, y_ready = n.sem("h1_T"), n.sem("h1T_ready"), n.sem("mm2_done"), n.sem("y_ready")
        stored = [n.sem(f"stored{i}") for i in range(2)]
        rows = [n.sb(f"rows{i}", [P, GT, P]) for i in range(2)]
        xT = [n.sb(f"xT{i}", [P, GT, P]) for i in range(2)]
        h1 = [n.sb(f"h1{i}", [P, F0]) for i in range(2)]
        h1T = [n.sb(f"h1T{i}", [P, FC0, P]) for i in range(2)]
        y = [n.sb(f"y{i}", [P, GT, P]) for i in range(2)]
        psX = [n.ps(f"psX{i}", [P, 512]) for i in range(2)]
        ps1 = [n.ps(f"ps1{i}", [P, 512]) for i in range(2)]
        ps2 = [n.ps(f"ps2{i}", [P, 512]) for i in range(2)]
        psY = [n.ps(f"psY{i}", [P, 512]) for i in range(2)]
        src = M.sorted[0].rearrange("(s p) e -> p s e", p=P)
        dst = M.result[0].rearrange("(s p) e -> p s e", p=P)

        with nc.Block() as block:
            @block.sync
            def _(sp):
                move_tiles(sp, NS0, src, dst, rows, y, loaded, stored, x_T, y_ready)

            @block.tensor
            def _(pe):
                def step(i, r):
                    k, gs = i * U + r, r // GT
                    if S.has(k) and r % GT == 0:
                        pe.wait_ge(loaded[gs], i * 16 + 16)
                        if after(k, U):
                            pe.wait_ge(xT_ready, i * 2 + gs - 1)
                        for t in range(GT):
                            mm = pe.transpose(psX[gs][:, t * P:(t + 1) * P], rows[gs][:, t, :], M.ident[:])
                        mm.then_inc(x_T, 1)
                    if S.has(k - 1):
                        j = (r - 1) % U
                        e = pe.value_load(M.expert[0:1, bass.ds(k - 1, 1)], min_val=0, max_val=E0 - 1)
                        if j % GT == 0:
                            pe.wait_ge(xT_ready, i * 2 + (r - 1) // GT + 1)
                        if after(k - 1, 2):
                            pe.wait_ge(h1_ready, k - 2)
                        pe.matmul(ps1[j % 2][:], xT[j // GT][:, j % GT, :], M.w10[:, bass.ds(e, 1), :], start=True,
                                  stop=True).then_inc(mm1_done, 1)
                    if S.has(k - 2):
                        q = r % 2
                        pe.wait_ge(h1_ready, k - 1)
                        if after(k - 2, 2):
                            pe.wait_ge(h1T_ready, k - 3)
                        for c in range(FC0):
                            mm = pe.transpose(ps2[q][:, c * P:(c + 1) * P], h1[q][:, c * P:(c + 1) * P], M.ident[:])
                        mm.then_inc(h1_T, 1)
                    if S.has(k - 3):
                        q = (r - 3) % 2
                        e = pe.value_load(M.expert[0:1, bass.ds(k - 3, 1)], min_val=0, max_val=E0 - 1)
                        pe.wait_ge(h1T_ready, k - 2)
                        if after(k - 3, 2):
                            pe.wait_ge(y_ready, k - 4)
                        for c in range(FC0):
                            mm = pe.matmul(psY[q][:, 0:P], h1T[q][:, c, :], M.w20[:, bass.ds(e, 1), c, :],
                                           start=(c == 0), stop=(c == FC0 - 1))
                        mm.then_inc(mm2_done, 1)

                S.run(pe, step)

            @block.vector
            def _(dve):
                def step(i, r):
                    k = i * U + r
                    if S.has(k - 1):
                        q = (r - 1) % 2
                        e = dve.value_load(M.expert[0:1, bass.ds(k - 1, 1)], min_val=0, max_val=E0 - 1)
                        dve.wait_ge(mm1_done, k)
                        if after(k - 1, 2):
                            dve.wait_ge(h1_T, k - 2)
                        dve.tensor_tensor(h1[q][:], ps1[q][:], M.b10[:, bass.ds(e, 1), :].rearrange("p o f -> p (o f)"),
                                          ALU.add).then_inc(h1_ready, 1)
                    if S.has(k - 3):
                        j = (r - 3) % U
                        e = dve.value_load(M.expert[0:1, bass.ds(k - 3, 1)], min_val=0, max_val=E0 - 1)
                        dve.wait_ge(mm2_done, k - 2)
                        if after(k - 3, U) and j % GT == 0:
                            dve.wait_ge(stored[j // GT], (i if r >= 3 else i - 1) * 16)
                        dve.tensor_tensor(y[j // GT][:, j % GT, :], psY[j % 2][:, 0:P],
                                          M.b20[:, bass.ds(e, 1), :].rearrange("p o f -> p (o f)"),
                                          ALU.add).then_inc(y_ready, 1)

                S.run(dve, step)

            @block.scalar
            def _(act):
                def step(i, r):
                    k, gs = i * U + r, r // GT
                    if S.has(k) and r % GT == 0:
                        act.wait_ge(x_T, i * 2 + gs + 1)
                        if after(k, U):
                            act.wait_ge(mm1_done, k - GT)
                        act.activation(xT[gs][:].rearrange("p t e -> p (t e)"), psX[gs][:], ACT.Copy).then_inc(xT_ready, 1)
                    if S.has(k - 2):
                        q = r % 2
                        act.wait_ge(h1_T, k - 1)
                        if after(k - 2, 2):
                            act.wait_ge(mm2_done, k - 3)
                        act.activation(h1T[q][:].rearrange("p c t -> p (c t)"), ps2[q][:], ACT.Relu).then_inc(h1T_ready, 1)

                S.run(act, step)


def phase_combine0(nc, D, M):
    with Names(nc, "c0_") as n:
        gathered = [n.sem(f"gathered{i}") for i in range(NT // 4)]
        weighed, added = n.sem("weighed"), n.sem("added")
        t = n.sb("weighted", [P, NT, P])
        with nc.Block() as block:
            @block.gpsimd
            def _(pool):
                for i in range(NT):
                    pool.indirect_dma_start(
                        out=M.h[:, i, :], out_offset=None, in_=M.result[0][:, :],
                        in_offset=bass.IndirectOffsetOnAxis(ap=M.slot[:, i:i + 1], axis=0)).then_inc(gathered[i // 4], 16)

            @block.vector
            def _(dve):
                for i in range(NT):
                    b = i // TB
                    if i % 4 == 0:
                        dve.wait_ge(gathered[i // 4], 64)
                    dve.scalar_tensor_tensor(out=t[:, i, :], in0=M.h[:, i, :], scalar=M.gate[:, i:i + 1],
                                             in1=M.mod[:, 0, b, GB * P:(GB + 1) * P], op0=ALU.mult,
                                             op1=ALU.mult).then_inc(weighed, 1)
                    if i >= 1:
                        dve.wait_ge(weighed, i)
                        dve.tensor_tensor(M.x[:, i - 1, :], M.x[:, i - 1, :], t[:, i - 1, :], ALU.add).then_inc(added, 1)
                    if i >= 2:
                        dve.wait_ge(added, i - 1)
                        dve.bn_stats(M.stats[:, i - 2, :], M.x[:, i - 2, :])
                dve.wait_ge(weighed, NT)
                dve.tensor_tensor(M.x[:, NT - 1, :], M.x[:, NT - 1, :], t[:, NT - 1, :], ALU.add).then_inc(added, 1)
                dve.wait_ge(added, NT)
                for i in (NT - 2, NT - 1):
                    dve.bn_stats(M.stats[:, i, :], M.x[:, i, :])


def phase_project1(nc, D, M):
    with Names(nc, "p1_") as n:
        ld = n.sem("ld_rope")
        var_ready, rstd_ready = n.sem("var_ready"), n.sem("rstd_ready")
        dve_ln, dve_step = n.sem("dve_ln"), n.sem("dve_step")
        xn_ready, xn_T, hT_ready = n.sem("xn_ready"), n.sem("xn_T"), n.sem("hT_ready")
        ct_mm, ct_ready, u_mm, rot_read = n.sem("ct_mm"), n.sem("ct_ready"), n.sem("u_mm"), n.sem("rot_read")
        v_mm, v_out, full_ready, part1, rest1, part2, part3 = (n.sem("v_mm"), n.sem("v_out"), n.sem("full_ready"),
            n.sem("part1"), n.sem("rest1"), n.sem("part2"), n.sem("part3"))
        qk_stored, v_stored = n.sem("qk_stored"), n.sem("v_stored")
        rope = n.sb("rope", [P, 2, L])
        xn = n.sb("xn", [P, 4, P])
        hT = [n.sb(f"hT{i}", [P, 512]) for i in range(2)]
        ctT = [n.sb(f"ctT{i}", [P, 512]) for i in range(2)]
        ras = [n.sb(f"ra{i}", [P, 512]) for i in range(2)]
        rbs = [n.sb(f"rb{i}", [P, 512]) for i in range(2)]
        full, rest = n.sb("full", [P, 2, 512]), n.sb("rest", [P, 2, 512])
        parts = [n.sb(f"part{i}", [P, 2, 512], BF16) for i in range(3)]
        vout = n.sb("vout", [P, 4, H, HD + 1])
        psT, psC = n.ps("psT", [P, 512]), n.ps("psC", [P, 512])
        psR = [[n.ps(f"psR{i}_{j}", [P, 512]) for j in range(3)] for i in range(2)]
        PARTS = ((0, 0), (0, 1), (1, 0), (1, 1), (0, 2), (2, 0))

        def halves(eng, body):
            def batch(b, first):
                for j in range(2):
                    body(b, j, b * 2 + j, first and j == 0)
            batches(eng, B, batch)

        with nc.Block() as block:
            @block.sync
            def _(sp):
                sp.dma_start(rope[:], D["rope"]).then_inc(ld, 16)

                def half(b, j, m, first):
                    cols = slice(j * 512, (j + 1) * 512)
                    wait_apart(sp, part3, m * 2 + 2)
                    for c, which in enumerate(PARTS):
                        for qk in range(2):
                            dst = M.qk_rows[qk][bass.ds(b * H, H), c * HD:(c + 1) * HD, cols]
                            sp.dma_start(dst, parts[which[qk]][:, qk, :]).then_inc(qk_stored, 16)
                    wait_apart(sp, v_out, m + 2)
                    for q in range(4):
                        sp.dma_start(M.v_rows[bass.ds(b * 4 + q, 1), :, 4 * j:4 * j + 4, :].rearrange("o p t c -> (o p) t c"),
                                     vout[:, :, 4 * q:4 * q + 4, :].rearrange("p t h c -> p t (h c)")).then_inc(v_stored, 16)

                halves(sp, half)
                sp.wait_ge(qk_stored, 16 * 2 * NPART * 2 * B)
                sp.wait_ge(v_stored, 16 * 4 * 2 * B)

            @block.gpsimd
            def _(pool):
                mean_and_rstd(None, pool, None, M, var_ready, rstd_ready)

                def half(b, j, m, first):
                    for qk in range(2):
                        pool.wait_ge(part2, m * 2 + qk + 1)
                        if not first and qk == 0:
                            pool.wait_ge(qk_stored, m * 2 * NPART * 16)
                        pool.tensor_tensor(parts[2][:, qk, :], rest[:, qk, :], parts[1][:, qk, :],
                                           ALU.subtract).then_inc(part3, 1)

                halves(pool, half)

            @block.vector
            def _(dve):
                dve.memset(vout[:, :, :, HD:HD + 1], 1.0).then_inc(v_out, 1)
                mean_and_rstd(dve, None, Link(dve, dve_ln), M, var_ready, rstd_ready)
                dve.wait_ge(rstd_ready, 1)
                dve.wait_ge(ld, 16)
                dve.wait_ge(v_out, 1)

                def half(b, j, m, first):
                    link = Link(dve, dve_step, m * 6)
                    if not first:
                        dve.wait_ge(xn_T, m)
                    for t in range(4):
                        i = b * TB + 4 * j + t
                        dve.tensor_scalar(xn[:, t, :], M.x[:, bass.ds(i, 1), :].rearrange("p o e -> p (o e)"), M.mean[:, bass.ds(i, 1)],
                                          M.rstd[:, bass.ds(i, 1)], ALU.subtract, ALU.mult).then_inc(xn_ready, 1)
                    for qk in range(2):
                        u, a, s = psR[qk]
                        bu = 1 + 3 * qk
                        ra, rb = ras[qk], rbs[qk]
                        if not first and qk == 0:
                            dve.wait_ge(full_ready, m * 2)
                        dve.wait_ge(u_mm, m * 2 + qk + 1)
                        dve.scalar_tensor_tensor(out=ra[:], in0=a[:], scalar=M.bcol1[:, bu + 1:bu + 2],
                                                 in1=rope[:, 0, j * 512:(j + 1) * 512], op0=ALU.add, op1=ALU.mult).then_inc(dve_step, 1)
                        link.n += 1
                        link(dve.scalar_tensor_tensor(out=rb[:], in0=s[:], scalar=M.bcol1[:, bu + 2:bu + 3],
                                                      in1=rope[:, 1, j * 512:(j + 1) * 512], op0=ALU.add, op1=ALU.mult))
                        link(dve.tensor_tensor(ra[:], ra[:], rb[:], ALU.add))
                        if not first:
                            dve.wait_ge(part1, m * 2)
                        dve.scalar_tensor_tensor(out=full[:, qk, :], in0=u[:], scalar=M.bcol1[:, bu:bu + 1],
                                                 in1=ra[:], op0=ALU.add, op1=ALU.add).then_inc(full_ready, 1)
                    dve.wait_ge(v_mm, m + 1)
                    if not first:
                        dve.wait_ge(v_stored, m * 64)
                    dve.tensor_tensor(vout[:, :, :, 0:HD], psT[:].rearrange("p (t h d) -> p t h d", t=4, h=H),
                                      M.bv1[:].rearrange("p (h d) -> p h d", h=H).unsqueeze(1).to_broadcast([P, 4, H, HD]),
                                      ALU.add).then_inc(v_out, 1)
                    for qk in range(2):
                        dve.wait_ge(part1, m * 2 + qk + 1)
                        if not first:
                            dve.wait_ge(part3, m * 2)
                        dve.tensor_tensor(rest[:, qk, :], full[:, qk, :], parts[0][:, qk, :],
                                          ALU.subtract).then_inc(rest1, 1)

                halves(dve, half)

            @block.scalar
            def _(act):
                def half(b, j, m, first):
                    if not first:
                        act.wait_ge(v_mm, m)
                    wait_apart(act, xn_T, m + 1)
                    act.activation(hT[0][:], psT[:], ACT.Identity, bias=M.modcol[:, 1, 0, bass.ds(b, 1)],
                                   scale=M.modcol[:, 1, 1, bass.ds(b, 1)]).then_inc(hT_ready, 1)
                    act.wait_ge(ct_mm, m + 1)
                    act.activation(ctT[0][:], psC[:], ACT.Identity, bias=M.bcol1[:, 0:1]).then_inc(ct_ready, 1)
                    for qk in range(2):
                        act.wait_ge(full_ready, m * 2 + qk + 1)
                        if not first and qk == 0:
                            act.wait_ge(qk_stored, m * 2 * NPART * 16)
                        act.activation(parts[0][:, qk, :], full[:, qk, :], ACT.Copy).then_inc(part1, 1)
                    for qk in range(2):
                        act.wait_ge(rest1, m * 2 + qk + 1)
                        act.activation(parts[1][:, qk, :], rest[:, qk, :], ACT.Copy).then_inc(part2, 1)

                halves(act, half)

            @block.tensor
            def _(pe):
                def half(b, j, m, first):
                    if not first:
                        pe.wait_ge(v_out, m + 1)
                    for t in range(4):
                        pe.wait_ge(xn_ready, m * 4 + t + 1)
                        mm = pe.transpose(psT[:, t * P:(t + 1) * P], xn[:, t, :], M.ident[:])
                    mm.then_inc(xn_T, 1)
                    pe.wait_ge(hT_ready, m + 1)
                    h, c = hT[0], ctT[0]
                    pe.matmul(psC[:], M.wd1[:], h[:], start=True, stop=True).then_inc(ct_mm, 1)
                    if not first:
                        pe.wait_ge(full_ready, m * 2)
                    for k in range(2):
                        pe.matmul(psR[1][1 + k][:], M.wkr1[:, k * P:(k + 1) * P], h[:], start=True, stop=True)
                    pe.wait_ge(ct_ready, m + 1)
                    for k in range(3):
                        mm = pe.matmul(psR[0][k][:], M.wuq1[:, k * P:(k + 1) * P], c[0:DR, :], start=True, stop=True)
                    mm.then_inc(u_mm, 1)
                    pe.matmul(psR[1][0][:], M.wukv1[DR:P, 0:P], c[DR:P, :], start=True, stop=True).then_inc(u_mm, 1)
                    for t in range(4):
                        mm = pe.matmul(psT[:, t * P:(t + 1) * P], c[DR:P, t * P:(t + 1) * P], M.wukv1[DR:P, P:2 * P],
                                       start=True, stop=True)
                    mm.then_inc(v_mm, 1)

                halves(pe, half)


QUAD = 4
NGRP = B * H // QUAD
KC = L // P
GSTEPS = 2 * KC
BODY = 2 * GSTEPS
AHEAD = 12
NSTEPS = NGRP * GSTEPS
VC = QUAD * (HD + 1)


def phase_attention1(nc, D, M):
    with Names(nc, "at_") as n:
        ones_set, group_in = n.sem("ones_set"), [n.sem(f"group_in{i}") for i in range(2)]
        a_mm, a_max, m_split, m_T, mT_out = n.sem("a_mm"), n.sem("a_max"), n.sem("m_split"), n.sem("m_T"), n.sem("mT_out")
        m_stored, m_in = n.sem("m_stored"), [n.sem(f"m_in{i}") for i in range(2)]
        s_mm, exp_done, pv_done, acc_out = n.sem("s_mm"), n.sem("exp_done"), n.sem("pv_done"), n.sem("acc_out")
        dve_step, ld_ones, zeroed = n.sem("dve_step"), n.sem("ld_ones"), n.sem("zeroed")
        k_zero, q_zero = n.sem("k_zero"), n.sem("q_zero")
        Q = [n.sb(f"Q{i}", [P, QUAD, L], BF16) for i in range(2)]
        K = [n.sb(f"K{i}", [P, 2, L], BF16) for i in range(2)]
        KA = [n.sb(f"KA{i}", [P, 2, L], BF16) for i in range(2)]
        V = [n.sb(f"V{i}", [P, KC, VC + VW], F32) for i in range(2)]
        ones = n.sb("ones", [P, L], BF16)
        pt = [n.sb(f"pt{i}", [P, QUAD, 512]) for i in range(2)]
        mx = n.sb("mx", [P, QUAD, 4])
        mr = n.sb("mr", [P, QUAD * 4])
        mp = n.sb("mp", [P, P // (QUAD * 4), QUAD * 4], BF16)
        mT = n.sb("mT", [MROWS * QUAD * 4, P], BF16)
        psA = [n.ps(f"psA{i}", [P, L]) for i in range(2)]
        psS = [n.ps(f"psS{i}", [P, 512]) for i in range(3)]
        acc = n.ps("acc", [P, 512])

        def a_step(s):
            w = s % GSTEPS
            half, kk = w // KC, w % KC
            return (s // GSTEPS) % 2, half, [(kk // 2, 2 * (kk % 2) + t) for t in range(2)]

        def bank(s, h):
            return ((s % GSTEPS) * QUAD + h) % 3

        def last_use(s, h):
            k, in_group = (s % GSTEPS) * QUAD + h, GSTEPS * QUAD
            return next(d for d in range(1, 8) if (k - d) % in_group % 3 == k % 3)

        def known(i, s):
            return i * BODY + s if isinstance(i, int) else None

        def beyond(i, s, n):
            return known(i, s) is None or known(i, s) >= n

        def exists(i, s):
            return known(i, s) is None or known(i, s) < NSTEPS

        def unit(i, s):
            return i * (BODY // KC) + s // KC

        def group(i, s):
            return i * (BODY // GSTEPS) + s // GSTEPS

        def iterations(eng, body):
            body(0)
            with eng.Fori(1, NGRP // 2 - 1) as i:
                body(i)
            body(NGRP // 2 - 1)

        with nc.Block() as block:
            @block.gpsimd
            def _(pool):
                for q in Q:
                    pool.memset(q[:], 0.0).then_inc(q_zero, 1)

            @block.sync
            def _(sp):
                sp.wait_ge(ones_set, 1)
                sp.wait_ge(k_zero, 4)
                sp.wait_ge(q_zero, 2)
                for k in K:
                    for r in range(2):
                        for p in range(2):
                            sp.dma_start(k[64 * r + KROWS:64 * r + KROWS + MROWS, p, :], ones[0:MROWS, :]).then_inc(ld_ones, 16)

                def load(g, a):
                    if not (isinstance(g, int) and g < 2):
                        wait_apart(sp, pv_done, (g - 1) * GSTEPS)
                    for r in range(2):
                        for rows, dst in ((M.qk_rows[0], Q[a][:, r::2, :]), (M.qk_rows[1], KA[a]), (M.qk_rows[1], K[a])):
                            src = rows[bass.ds(g * QUAD, QUAD), :, :].rearrange("(p r) c t -> r c p t", r=2)[r]
                            sp.dma_start(dst[64 * r:64 * r + KROWS, :, :], src).then_inc(group_in[a], 16)
                    sp.dma_start(V[a][:, :, 0:VC], M.v_rows[bass.ds(g, 1), :, :, :].rearrange("o p t c -> (o p) t c")).then_inc(group_in[a], 16)

                def maxima(pair, a, half):
                    u = pair * 2 + half
                    wait_apart(sp, mT_out, u + 1)
                    sp.dma_start(M.m_rows[half], mT[:]).then_inc(m_stored, 16)
                    wait_apart(sp, m_stored, (u + 1) * 16, 16)
                    src = M.m_rows[half].rearrange("(c p r t) q -> r c p (t q)", c=MROWS, p=2, r=2)
                    for r in range(2):
                        sp.dma_start(Q[a][64 * r + KROWS:64 * r + KROWS + MROWS, r::2, half * 512:(half + 1) * 512],
                                     src[r]).then_inc(m_in[half], 16)
                    wait_apart(sp, m_in[half], pair * 32 + 32, 32)

                load(0, 0)

                def body(i):
                    for a in range(2):
                        g = i * 2 + a
                        if a == 0 and isinstance(i, int) and i == 0:
                            load(1, 1)
                            maxima(0, 0, 0)
                        elif not (isinstance(i, int) and i == NGRP // 2 - 1 and a == 1):
                            load(g + 1, 1 - a)
                        maxima(g, a, 1)
                        if not (isinstance(i, int) and i == NGRP // 2 - 1 and a == 1):
                            maxima(g + 1, 1 - a, 0)

                iterations(sp, body)

            @block.tensor
            def _(pe):
                def a_tile(i, s, t):
                    slot, half, tiles = a_step(s)
                    h, qt = tiles[t]
                    q0 = (half * 4 + qt) * P
                    if s % GSTEPS == 0 and t == 0:
                        pe.wait_ge(group_in[slot], (i + (s // GSTEPS) // 2) * 112 + 112)
                    if beyond(i, s, 1):
                        pe.wait_ge(a_max, i * (2 * BODY) + 2 * s + t - 1)
                    if t == 0 and s % KC == 1 and beyond(i, s, KC):
                        pe.wait_ge(mT_out, unit(i, s))
                    for c in range(2):
                        mm = pe.matmul(psA[t][:, c * 512:(c + 1) * 512], Q[slot][:, h, q0:q0 + P],
                                       KA[slot][:, h // 2, c * 512:(c + 1) * 512], start=True, stop=True)
                    mm.then_inc(a_mm, 1)

                def turn(i, s):
                    pe.wait_ge(m_split, unit(i, s))
                    pe.wait_ge(a_max, i * (2 * BODY) + 2 * s + (1 if exists(i, s) else 0))
                    pe.transpose(psA[0][:].bitcast(BF16)[:, 0:P], mp[:].rearrange("p c m -> p (c m)"),
                                 M.identb[:]).then_inc(m_T, 1)

                def scores(i, s, h):
                    slot, half, kc = (s // GSTEPS) % 2, (s % GSTEPS) // KC, s % KC
                    if kc == 0 and h == 0:
                        pe.wait_ge(m_in[half], group(i, s) * 32 + 32)
                    if known(i, s) is None or known(i, s) * QUAD + h >= 3:
                        pe.wait_ge(exp_done, i * (BODY * QUAD) + s * QUAD + h + 1 - last_use(s, h))
                    pe.matmul(psS[bank(s, h)][:], K[slot][:, h // 2, kc * P:(kc + 1) * P],
                              Q[slot][:, h, half * 512:(half + 1) * 512],
                              start=True, stop=True).then_inc(s_mm, 1)

                def values(i, s):
                    slot, kc = (s // GSTEPS) % 2, s % KC
                    pe.wait_ge(exp_done, i * (BODY * QUAD) + (s + 1) * QUAD)
                    if kc == 0 and beyond(i, s, 1):
                        pe.wait_ge(acc_out, unit(i, s))
                    for h in range(QUAD):
                        mm = pe.matmul(acc[VW * h:VW * (h + 1), :], V[slot][:, kc, h * (HD + 1):h * (HD + 1) + VW],
                                       pt[s % 2][:, h, :], start=(kc == 0), stop=(kc == KC - 1),
                                       tile_position=(0, VW * h), skip_group_check=True)
                    mm.then_inc(pv_done, 1)

                pe.wait_ge(ld_ones, 16 * 8)
                pe.wait_ge(zeroed, 3)
                for s in range(AHEAD):
                    a_tile(0, s, 0)
                    a_tile(0, s, 1)
                    if s % KC == 0 and s > 0:
                        turn(0, s)

                def body(i):
                    for s in range(BODY):
                        more = exists(i, s + AHEAD)
                        if more:
                            a_tile(i, s + AHEAD, 0)
                        scores(i, s, 0)
                        scores(i, s, 1)
                        if more:
                            a_tile(i, s + AHEAD, 1)
                        scores(i, s, 2)
                        scores(i, s, 3)
                        if (s + AHEAD) % KC == 0 and (more or known(i, s + AHEAD) == NSTEPS):
                            turn(i, s + AHEAD)
                        if s > 0:
                            values(i, s - 1)
                        elif beyond(i, s, 1):
                            values(i - 1, BODY - 1)

                iterations(pe, body)
                values(NGRP // 2 - 1, BODY - 1)

            @block.vector
            def _(dve):
                dve.memset(ones[:], 1.0).then_inc(ones_set, 1)
                for k in (*K, *KA):
                    dve.memset(k[:], 0.0).then_inc(k_zero, 1)
                dve.memset(mp[:], 0.0).then_inc(zeroed, 1)
                dve.wait_ge(zeroed, 1)
                for v in V:
                    dve.memset(v[:, :, VC:VC + VW], 0.0).then_inc(zeroed, 1)

                def a_max_tile(i, s, t):
                    slot, half, tiles = a_step(s)
                    h, qt = tiles[t]
                    dve.wait_ge(a_mm, i * (2 * BODY) + 2 * s + t + 1)
                    if s % KC == 0 and t == 0 and beyond(i, s, 1):
                        dve.wait_ge(m_split, unit(i, s))
                    dve.tensor_reduce(mx[:, h, qt:qt + 1], psA[t][:], AX.X, ALU.max).then_inc(a_max, 1)

                def split(i, s):
                    link = Link(dve, dve_step, unit(i, s) * 4)
                    dve.wait_ge(a_max, i * (2 * BODY) + 2 * s + 2)
                    if beyond(i, s, KC):
                        dve.wait_ge(m_T, unit(i, s))
                    m = mx[:].rearrange("p h t -> p (h t)")
                    link(dve.tensor_scalar(mp[:, 0, :], m, -1.0, None, ALU.mult))
                    link(dve.scalar_tensor_tensor(out=mr[:], in0=m, scalar=-1.0, in1=mp[:, 0, :], op0=ALU.mult, op1=ALU.subtract))
                    link(dve.tensor_copy(mp[:, 1, :], mr[:]))
                    link(dve.tensor_tensor(mr[:], mr[:], mp[:, 1, :], ALU.subtract))
                    dve.tensor_copy(mp[:, 2, :], mr[:]).then_inc(m_split, 1)

                def turned(i, s):
                    dve.wait_ge(m_T, unit(i, s))
                    if beyond(i, s, 2 * KC):
                        dve.wait_ge(m_stored, i * (16 * BODY // KC) + (s // KC - 1) * 16)
                    dve.tensor_copy(mT[:], psA[0][:].bitcast(BF16)[0:MROWS * QUAD * 4, 0:P]).then_inc(mT_out, 1)

                def a_part(i, s):
                    if exists(i, s):
                        a_max_tile(i, s, 0)
                        a_max_tile(i, s, 1)
                    if s % KC == 0 and beyond(i, s, 1) and (known(i, s) is None or known(i, s) <= NSTEPS):
                        turned(i, s)
                    if s % KC == KC - 1 and exists(i, s):
                        split(i, s)

                for s in range(AHEAD):
                    a_part(0, s)

                def body(i):
                    for s in range(BODY):
                        a_part(i, s + AHEAD)

                iterations(dve, body)

            @block.scalar
            def _(act):
                def evacuate(u):
                    wait_apart(act, pv_done, (u + 1) * KC)
                    act.activation(M.attn[:, bass.ds(u, 1), :].rearrange("p o q -> p (o q)"), acc[:], ACT.Copy).then_inc(acc_out, 1)

                def body(i):
                    for s in range(BODY):
                        if beyond(i, s, 2):
                            act.wait_ge(pv_done, i * BODY + s - 1)
                        for h in range(QUAD):
                            act.wait_ge(s_mm, i * (BODY * QUAD) + s * QUAD + h + 1)
                            act.activation(pt[s % 2][:, h, :], psS[bank(s, h)][:], ACT.Exp,
                                           scale=INV_SCALE).then_inc(exp_done, 1)
                        if s % KC == 0 and beyond(i, s, 1):
                            evacuate(i * (BODY // KC) + s // KC - 1)

                iterations(act, body)
                evacuate(NSTEPS // KC - 1)


def phase_output1(nc, D, M):
    with Names(nc, "o1_") as n:
        num_T, ctx_ready, ctx_T, ctxT_ready = n.sem("num_T"), n.sem("ctx_ready"), n.sem("ctx_T"), n.sem("ctxT_ready")
        o_mm, added, wog_ready, pool_step, dve_step = n.sem("o_mm"), n.sem("added"), n.sem("wog_ready"), n.sem("pool_step"), n.sem("dve_step")
        bog_added = n.sem("bog_added")
        psN = [n.ps(f"psN{i}", [P, 512]) for i in range(3)]
        psC = [n.ps(f"psC{i}", [P, 512]) for i in range(2)]
        psO = [n.ps(f"psO{i}", [P, 512]) for i in range(2)]
        wog, bog = n.sb("wog", [P, B, P]), n.sb("bog", [P, B, P])
        rden = [n.sb(f"rden{i}", [P, H]) for i in range(2)]
        ctx = [n.sb(f"ctx{i}", [P, P]) for i in range(2)]
        ctxT = [n.sb(f"ctxT{i}", [P, P]) for i in range(2)]
        with nc.Block() as block:
            @block.gpsimd
            def _(pool):
                ga = M.mod[:, 1, :, GA * P:(GA + 1) * P]
                pool.tensor_tensor(wog[:], M.wo1[:].unsqueeze(1).to_broadcast([P, B, P]), ga, ALU.mult).then_inc(wog_ready, 1)
                pool.tensor_tensor(bog[:], M.bo1[:].unsqueeze(1).to_broadcast([P, B, P]), ga, ALU.mult).then_inc(pool_step, 1)
                pool.wait_ge(pool_step, 1)
                for b in range(B):
                    xb = M.x[:, b * TB:(b + 1) * TB, :]
                    pool.tensor_tensor(xb, xb, bog[:, b, :].unsqueeze(1).to_broadcast([P, TB, P]), ALU.add).then_inc(bog_added, 1)

            @block.tensor
            def _(pe):
                pe.wait_ge(wog_ready, 1)
                for k in range(NT + 2):
                    if k < NT:
                        b, half, qt = k // TB, (k % TB) // 4, k % 4
                        if k >= 3:
                            pe.wait_ge(ctx_ready, k - 2)
                        for quad in range(4):
                            u = (b * 4 + quad) * 2 + half
                            mm = pe.transpose(psN[k % 3][:, quad * P:(quad + 1) * P], M.attn[:, u, qt * P:(qt + 1) * P], M.ident[:])
                        mm.then_inc(num_T, 1)
                    if 1 <= k <= NT:
                        i = k - 1
                        pe.wait_ge(ctx_ready, i + 1)
                        if i >= 2:
                            pe.wait_ge(ctxT_ready, i - 1)
                        pe.transpose(psC[i % 2][:, 0:P], ctx[i % 2][:], M.ident[:]).then_inc(ctx_T, 1)
                    if k >= 2:
                        i = k - 2
                        pe.wait_ge(ctxT_ready, i + 1)
                        if i >= 2:
                            pe.wait_ge(added, i - 1)
                        pe.matmul(psO[i % 2][:, 0:P], ctxT[i % 2][:], wog[:, i // TB, :], start=True, stop=True).then_inc(o_mm, 1)

            @block.scalar
            def _(act):
                for i in range(NT):
                    act.wait_ge(ctx_T, i + 1)
                    if i >= 2:
                        act.wait_ge(o_mm, i - 1)
                    act.activation(ctxT[i % 2][:], psC[i % 2][:, 0:P], ACT.Copy).then_inc(ctxT_ready, 1)

            @block.vector
            def _(dve):
                def add(i):
                    dve.wait_ge(o_mm, i + 1)
                    dve.wait_ge(bog_added, i // TB + 1)
                    dve.tensor_tensor(M.x[:, i, :], M.x[:, i, :], psO[i % 2][:, 0:P], ALU.add).then_inc(added, 1)

                def stats(i):
                    dve.wait_ge(added, i + 1)
                    dve.bn_stats(M.stats[:, i, :], M.x[:, i, :])

                for k in range(NT + 3):
                    if k < NT:
                        dve.wait_ge(num_T, k + 1)
                        nd = psN[k % 3][:].rearrange("p (h c) -> p h c", c=VW)
                        if k >= 2:
                            dve.wait_ge(ctx_T, k - 1)
                            dve.wait_ge(ctx_ready, k - 1)
                        dve.reciprocal(rden[k % 2][:].unsqueeze(2), nd[:, :, HD:HD + 1]).then_inc(dve_step, 1)
                        dve.wait_ge(dve_step, k + 1)
                        dve.tensor_tensor(ctx[k % 2][:].rearrange("p (h d) -> p h d", h=H), nd[:, :, 0:HD],
                                          rden[k % 2][:].unsqueeze(2).to_broadcast([P, H, HD]), ALU.mult).then_inc(ctx_ready, 1)
                    if 2 <= k < NT + 2:
                        add(k - 2)
                    if k >= 3:
                        stats(k - 3)


def phase_experts1(nc, D, M):
    S = Steps(NS1, 3)
    U = S.UNROLL
    with Names(nc, "e1_") as n:
        loaded = [n.sem(f"loaded{i}") for i in range(2)]
        x_T, xT_ready, mm1_done, silu_done, g_ready = (n.sem("x_T"), n.sem("xT_ready"), n.sem("mm1_done"),
                                                       n.sem("silu_done"), n.sem("g_ready"))
        g_T, gT_ready, mm2_done, y_ready = n.sem("g_T"), n.sem("gT_ready"), n.sem("mm2_done"), n.sem("y_ready")
        stored = [n.sem(f"stored{i}") for i in range(2)]
        rows = [n.sb(f"rows{i}", [P, GT, P]) for i in range(2)]
        xT = [n.sb(f"xT{i}", [P, GT, P]) for i in range(2)]
        sg = [n.sb(f"sg{i}", [P, F1]) for i in range(2)]
        g = [n.sb(f"g{i}", [P, F1]) for i in range(2)]
        gT = [n.sb(f"gT{i}", [P, P]) for i in range(2)]
        y = [n.sb(f"y{i}", [P, GT, P]) for i in range(2)]
        psX = [n.ps(f"psX{i}", [P, 512]) for i in range(2)]
        ps1 = [n.ps(f"ps1{i}", [P, 512]) for i in range(2)]
        ps2 = [n.ps(f"ps2{i}", [P, 512]) for i in range(2)]
        psY = [n.ps(f"psY{i}", [P, 512]) for i in range(2)]
        src = M.sorted[1].rearrange("(s p) e -> p s e", p=P)
        dst = M.result[1].rearrange("(s p) e -> p s e", p=P)

        with nc.Block() as block:
            @block.sync
            def _(sp):
                move_tiles(sp, NS1, src, dst, rows, y, loaded, stored, x_T, y_ready)

            @block.tensor
            def _(pe):
                def step(i, r):
                    k, gs = i * U + r, r // GT
                    if S.has(k) and r % GT == 0:
                        pe.wait_ge(loaded[gs], i * 16 + 16)
                        if after(k, U):
                            pe.wait_ge(xT_ready, i * 2 + gs - 1)
                        for t in range(GT):
                            mm = pe.transpose(psX[gs][:, t * P:(t + 1) * P], rows[gs][:, t, :], M.ident[:])
                        mm.then_inc(x_T, 1)
                    if S.has(k - 1):
                        j = (r - 1) % U
                        e = pe.value_load(M.expert[0:1, bass.ds(k - 1, 1)], min_val=0, max_val=E1 - 1)
                        if j % GT == 0:
                            pe.wait_ge(xT_ready, i * 2 + (r - 1) // GT + 1)
                        if after(k - 1, 2):
                            pe.wait_ge(g_ready, k - 2)
                        pe.matmul(ps1[j % 2][:, 0:2 * F1], xT[j // GT][:, j % GT, :], M.wgu1[:, bass.ds(e, 1), :], start=True,
                                  stop=True).then_inc(mm1_done, 1)
                    if S.has(k - 2):
                        q = r % 2
                        pe.wait_ge(g_ready, k - 1)
                        if after(k - 2, 2):
                            pe.wait_ge(gT_ready, k - 3)
                        pe.transpose(ps2[q][:, 0:P], g[q][:], M.ident[:]).then_inc(g_T, 1)
                    if S.has(k - 3):
                        q = (r - 3) % 2
                        e = pe.value_load(M.expert[0:1, bass.ds(k - 3, 1)], min_val=0, max_val=E1 - 1)
                        pe.wait_ge(gT_ready, k - 2)
                        if after(k - 3, 2):
                            pe.wait_ge(y_ready, k - 4)
                        pe.matmul(psY[q][:, 0:P], gT[q][:], M.wdn1[:, bass.ds(e, 1), :],
                                  start=True, stop=True).then_inc(mm2_done, 1)

                S.run(pe, step)

            @block.vector
            def _(dve):
                def step(i, r):
                    k, gs = i * U + r, r // GT
                    if S.has(k) and r % GT == 0:
                        dve.wait_ge(x_T, i * 2 + gs + 1)
                        if after(k, U):
                            dve.wait_ge(mm1_done, k - GT)
                        dve.tensor_copy(xT[gs][:].rearrange("p t e -> p (t e)"), psX[gs][:]).then_inc(xT_ready, 1)
                    if S.has(k - 1):
                        q = (r - 1) % 2
                        dve.wait_ge(silu_done, k)
                        if after(k - 1, 2):
                            dve.wait_ge(g_T, k - 2)
                        dve.tensor_tensor(g[q][:], ps1[q][:, F1:2 * F1], sg[q][:], ALU.mult).then_inc(g_ready, 1)
                    if S.has(k - 3):
                        j = (r - 3) % U
                        dve.wait_ge(mm2_done, k - 2)
                        if after(k - 3, U) and j % GT == 0:
                            dve.wait_ge(stored[j // GT], (i if r >= 3 else i - 1) * 16)
                        dve.tensor_copy(y[j // GT][:, j % GT, :], psY[j % 2][:, 0:P]).then_inc(y_ready, 1)

                S.run(dve, step)

            @block.scalar
            def _(act):
                def step(i, r):
                    k = i * U + r
                    if S.has(k - 1):
                        q = (r - 1) % 2
                        act.wait_ge(mm1_done, k)
                        if after(k - 1, 2):
                            act.wait_ge(g_ready, k - 2)
                        act.activation(sg[q][:], ps1[q][:, 0:F1], ACT.Silu).then_inc(silu_done, 1)
                    if S.has(k - 2):
                        q = r % 2
                        act.wait_ge(g_T, k - 1)
                        if after(k - 2, 2):
                            act.wait_ge(mm2_done, k - 3)
                        act.activation(gT[q][:], ps2[q][:, 0:P], ACT.Copy).then_inc(gT_ready, 1)

                S.run(act, step)


def phase_shared1(nc, D, M):
    NC = 2 * B
    with Names(nc, "s1_") as n:
        gathered = [n.sem(f"gathered{i}") for i in range(NC)]
        g_mm, u_mm, silu_done, m_ready = n.sem("g_mm"), n.sem("u_mm"), n.sem("silu_done"), n.sem("m_ready")
        d_mm, summed, scaled, x_done, stored = n.sem("d_mm"), n.sem("summed"), n.sem("scaled"), n.sem("x_done"), n.sem("stored")
        psG = [n.ps(f"psG{i}", [P, 512]) for i in range(2)]
        psU = [n.ps(f"psU{i}", [P, 512]) for i in range(2)]
        psD = [n.ps(f"psD{i}", [P, 512]) for i in range(2)]
        sg = [n.sb(f"sg{i}", [P, 512]) for i in range(2)]
        m = [n.sb(f"m{i}", [P, FCS, 512]) for i in range(2)]
        tot = [n.sb(f"tot{i}", [P, 4, P]) for i in range(2)]
        with nc.Block() as block:
            @block.gpsimd
            def _(pool):
                for i in range(NT):
                    pool.indirect_dma_start(
                        out=M.h[:, i, :], out_offset=None, in_=M.result[1][:, :],
                        in_offset=bass.IndirectOffsetOnAxis(ap=M.slot[:, i:i + 1], axis=0)).then_inc(gathered[i // 4], 16)
                for g in gathered:
                    pool.wait_ge(g, 64)

            @block.tensor
            def _(pe):
                def down(c):
                    if c >= 2:
                        pe.wait_ge(summed, c - 1)
                    for t in range(4):
                        for f in range(FCS):
                            pe.wait_ge(m_ready, c * FCS + f + 1)
                            mm = pe.matmul(psD[c % 2][:, t * P:(t + 1) * P], m[c % 2][:, f, t * P:(t + 1) * P],
                                           M.wsd1[:, f, :], start=(f == 0), stop=(f == FCS - 1))
                    mm.then_inc(d_mm, 1)

                for c in range(NC + 1):
                    if c < NC:
                        for f in range(FCS):
                            k = c * FCS + f
                            if k >= 2:
                                pe.wait_ge(m_ready, k - 1)
                            tok = M.hT[:, c * 512:(c + 1) * 512]
                            pe.matmul(psG[k % 2][:], M.wsg1[:, f * P:(f + 1) * P], tok, start=True, stop=True).then_inc(g_mm, 1)
                            pe.matmul(psU[k % 2][:], M.wsg1[:, FS + f * P:FS + (f + 1) * P], tok, start=True,
                                      stop=True).then_inc(u_mm, 1)
                    if c >= 1:
                        down(c - 1)

            @block.scalar
            def _(act):
                for k in range(NC * FCS):
                    act.wait_ge(g_mm, k + 1)
                    if k >= 2:
                        act.wait_ge(m_ready, k - 1)
                    act.activation(sg[k % 2][:], psG[k % 2][:], ACT.Silu).then_inc(silu_done, 1)

            @block.vector
            def _(dve):
                def finish(c):
                    b = c // 2
                    dve.wait_ge(d_mm, c + 1)
                    dve.wait_ge(gathered[c], 64)
                    if c >= 2:
                        dve.wait_ge(x_done, c - 1)
                    dve.tensor_tensor(tot[c % 2][:], psD[c % 2][:].rearrange("p (t e) -> p t e", t=4),
                                      M.h[:, 4 * c:4 * c + 4, :], ALU.add).then_inc(summed, 1)
                    dve.wait_ge(summed, c + 1)
                    gb = M.mod[:, 1, b, GB * P:(GB + 1) * P].unsqueeze(1).to_broadcast([P, 4, P])
                    dve.tensor_tensor(tot[c % 2][:], tot[c % 2][:], gb, ALU.mult).then_inc(scaled, 1)
                    dve.wait_ge(scaled, c + 1)
                    xc = M.x[:, 4 * c:4 * c + 4, :]
                    dve.tensor_tensor(xc, xc, tot[c % 2][:], ALU.add).then_inc(x_done, 1)

                for c in range(NC + 1):
                    if c < NC:
                        for f in range(FCS):
                            k = c * FCS + f
                            dve.wait_ge(u_mm, k + 1)
                            dve.wait_ge(silu_done, k + 1)
                            if c >= 2 and f == 0:
                                dve.wait_ge(d_mm, c - 1)
                            dve.tensor_tensor(m[c % 2][:, f, :], psU[k % 2][:], sg[k % 2][:], ALU.mult).then_inc(m_ready, 1)
                    if c >= 1:
                        finish(c - 1)

            @block.sync
            def _(sp):
                for c in range(NC):
                    sp.wait_ge(x_done, c + 1)
                    sp.dma_start(D["out"][c // 2].rearrange("(t p) e -> p t e", p=P)[:, 4 * (c % 2):4 * (c % 2) + 4, :],
                                 M.x[:, 4 * c:4 * c + 4, :]).then_inc(stored, 16)
                sp.wait_ge(stored, 16 * NC)


def program(nc, D, out, last=99):
    phases = iter(range(last))
    done = []

    def run(phase, *args):
        if next(phases, None) is not None:
            phase(nc, D, M, *args)
        done.append(phase)

    Names.start(nc)
    with Names(nc) as M:
        declare(nc, M)
        with Names(nc) as layer0:
            declare_experts0(M, layer0)
            run(phase_load)
            run(phase_linear_attention)
            with Names(nc) as rows:
                declare_rows(M, rows, 0)
                run(phase_route, 0)
                run(phase_experts0)
                run(phase_combine0)
        run(phase_project1)
        with Names(nc) as attended:
            M.attn = attended.sb("attn", [P, NGRP * 2, 512])
            run(phase_attention1)
            run(phase_output1)
        with Names(nc) as layer1:
            declare_experts1(M, layer1)
            declare_rows(M, layer1, 1)
            D["out"] = out
            run(phase_route, 1)
            run(phase_experts1)
            run(phase_shared1)
        if last < 99:
            phase_store(nc, M, out)


def phase_store(nc, M, out):
    with Names(nc, "st_") as n:
        stored = n.sem("stored")
        with nc.Block() as block:
            @block.sync
            def _(sp):
                for b in range(B):
                    sp.dma_start(out[b].rearrange("(t p) e -> p t e", p=P),
                                 M.x[:, b * TB:(b + 1) * TB, :]).then_inc(stored, 16)
                sp.wait_ge(stored, 16 * B)


def declare(nc, M):
    M.x = M.sb("x", [P, NT, P])
    M.stats = M.sb("stats", [P, NT, 6])
    M.ln_d, M.ln_v = M.sb("ln_d", [P, NT]), M.sb("ln_v", [P, NT])
    M.mean, M.rstd, M.half = M.sb("mean", [P, NT]), M.sb("rstd", [P, NT]), M.sb("half", [P, NT])
    M.mod = M.sb("mod", [P, 2, B, 6 * P])
    M.modcol = M.sb("modcol", [P, 2, 2, B])
    M.gate, M.zeros = M.sb("gate", [P, NT]), M.sb("zeros", [P, P])
    M.slot, M.expert = M.sb("slot", [P, NT], I32), M.sb("expert", [1, NS1], I32)
    M.sorted = [nc.dram_tensor(f"sorted{l}", [s * P, P], F32).ap() for l, s in enumerate((NS0, NS1))]
    M.result = [nc.dram_tensor(f"result{l}", [s * P, P], F32).ap() for l, s in enumerate((NS0, NS1))]
    M.qk_rows = [nc.dram_tensor(f"{x}_rows", [B * H, KROWS, L], BF16).ap() for x in "qk"]
    M.v_rows = nc.dram_tensor("v_rows", [NGRP, P, KC, VC], F32).ap()
    M.m_rows = nc.dram_tensor("m_rows", [2, MROWS * QUAD * 4, P], BF16).ap()
    M.ident, M.identb = M.sb("ident", [P, P]), M.sb("identb", [P, P], BF16)
    M.wq0, M.wkv0, M.wo0 = M.sb("wq0", [P, P]), M.sb("wkv0", [P, 2 * P]), M.sb("wo0", [P, P])
    M.bq0, M.bkv0, M.bo0 = M.sb("bq0", [P, 1]), M.sb("bkv0", [P, 2 * P]), M.sb("bo0", [P, P])
    M.blockmask, M.headmask = M.sb("blockmask", [P, P]), M.sb("headmask", [P, H])
    M.tri, M.onesm = M.sb("tri", [P, P]), M.sb("onesm", [P, P])
    M.idents, M.tiles = M.sb("idents", [P, E1]), M.sb("tiles", [P, NS1])
    M.wr0, M.br0 = M.sb("wr0", [P, E0]), M.sb("br0", [P, E0])
    M.wd1, M.wuq1, M.wukv1, M.wkr1 = (M.sb("wd1", [P, 2 * DR]), M.sb("wuq1", [DR, 3 * P]),
                                      M.sb("wukv1", [P, 2 * P]), M.sb("wkr1", [P, 2 * P]))
    M.bcol1, M.bv1 = M.sb("bcol1", [P, 8]), M.sb("bv1", [P, P])
    M.wo1, M.bo1 = M.sb("wo1", [P, P]), M.sb("bo1", [P, P])
    M.wr1 = M.sb("wr1", [P, E1])


def declare_experts0(M, n):
    M.w10, M.w20 = n.sb("w10", [P, E0, F0]), n.sb("w20", [P, E0, FC0, P])
    M.b10, M.b20 = n.sb("b10", [P, E0, F0]), n.sb("b20", [P, E0, P])


def declare_experts1(M, n):
    M.wgu1, M.wdn1 = n.sb("wgu1", [P, E1, 2 * F1]), n.sb("wdn1", [P, E1, P])
    M.wsg1, M.wsd1 = n.sb("wsg1", [P, 2 * FS]), n.sb("wsd1", [P, FCS, P])


def declare_rows(M, n, l):
    M.h, M.hT = n.sb(f"h_l{l}", [P, NT, P]), n.sb(f"hT_l{l}", [P, NT * P])


def rope_tables():
    ids = np.arange(P // 2, dtype=np.float32)
    theta = (np.float32(10000.0) ** (np.float32(-2.0) * ids)).astype(np.float32) / np.float32(P // 2)
    r = np.arange(L, dtype=np.float32)[:, None] * theta[None, :]
    cos, sin = np.cos(r), np.sin(r)
    both = np.empty((2, P, L), np.float32)
    both[0, 0::2], both[0, 1::2] = cos.T, cos.T
    both[1, 0::2], both[1, 1::2] = -sin.T, sin.T
    return both


def layout(a):
    row = lambda v: np.ascontiguousarray(v)
    swap = np.arange(P) ^ 1
    r = np.arange(P)
    return {
        "x": a["L0_attn_query"],
        "cT": np.stack([a["L0_c"].T, a["L1_c"].T], 1),
        "wmod": np.stack([a["L0_wmod"], a["L1_wmod"]], 1),
        "ident": np.eye(P, dtype=np.float32),
        "wq0": a["L0_attn_Wq"].T, "wkv0": np.concatenate([a["L0_attn_Wk"].T, a["L0_attn_Wv"].T], 1),
        "wo0": a["L0_attn_Wo"].T, "bq0": a["L0_attn_bq"][:, None],
        "bkv0": np.concatenate([a["L0_attn_bk"], a["L0_attn_bv"]]), "bo0": a["L0_attn_bo"],
        "blockmask": (r[:, None] // HD == r[None, :] // HD).astype(np.float32),
        "headmask": (r[:, None] // HD == np.arange(H)[None, :]).astype(np.float32),
        "tri": (r[:, None] < r[None, :]).astype(np.float32), "onesm": np.ones((P, P), np.float32),
        "idents": np.arange(E1, dtype=np.float32), "tiles": np.arange(NS1, dtype=np.float32),
        "wr0": a["L0_ffn_Wr"], "br0": a["L0_ffn_br"],
        "w10": a["L0_ffn_W1"].transpose(1, 0, 2),
        "w20": a["L0_ffn_W2"].reshape(E0, FC0, P, P).transpose(2, 0, 1, 3),
        "b10": a["L0_ffn_b1"], "b20": a["L0_ffn_b2"],
        "wd1": np.concatenate([a["L1_attn_Wd_q_w"], a["L1_attn_Wd_kv_w"]], 1),
        "wuq1": np.concatenate([a["L1_attn_Wu_q_w"], a["L1_attn_Wq_r_w"], a["L1_attn_Wq_r_w"][:, swap]], 1),
        "wukv1": np.concatenate([np.zeros((DR, 2 * P), np.float32),
                                 np.concatenate([a["L1_attn_Wu_k_w"], a["L1_attn_Wu_v_w"]], 1)], 0),
        "wkr1": np.concatenate([a["L1_attn_Wk_r_w"], a["L1_attn_Wk_r_w"][:, swap]], 1),
        "bcol1": np.stack([np.concatenate([a["L1_attn_Wd_q_b"], a["L1_attn_Wd_kv_b"]]),
                           a["L1_attn_Wu_q_b"], a["L1_attn_Wq_r_b"], a["L1_attn_Wq_r_b"][swap],
                           a["L1_attn_Wu_k_b"], a["L1_attn_Wk_r_b"], a["L1_attn_Wk_r_b"][swap],
                           np.zeros(P, np.float32)], 1),
        "bv1": a["L1_attn_Wu_v_b"], "wo1": a["L1_attn_Wo_w"], "bo1": a["L1_attn_Wo_b"],
        "wr1": a["L1_ffn_router_w"].T,
        "wgu1": a["L1_ffn_gate_up_proj"].transpose(1, 0, 2), "wdn1": a["L1_ffn_down_proj"].transpose(1, 0, 2),
        "wsg1": np.concatenate([a["L1_ffn_shared_gate_w"].T, a["L1_ffn_shared_up_w"].T], 1),
        "wsd1": a["L1_ffn_shared_down_w"].T.reshape(FCS, P, P).transpose(1, 0, 2),
        "rope": rope_tables().transpose(1, 0, 2),
    }


def kernel(**inputs):
    import concourse.bacc as bacc
    from concourse.bass_utils import run_bass_kernel_spmd

    nc = bacc.Bacc("TRN2", target_bir_lowering=False, num_devices=1)
    arrays, D = {}, {}
    for name, a in layout(inputs).items():
        arrays[f"in_{name}"] = np.ascontiguousarray(a)
        D[name] = nc.dram_tensor(f"in_{name}", list(a.shape), F32, kind="ExternalInput").ap()
    out = nc.dram_tensor("out_0", [B, L, P], F32, kind="ExternalOutput").ap()
    program(nc, D, out)
    return run_bass_kernel_spmd(nc, [arrays], core_ids=[0]).results[0]["out_0"]
```

```python
from contextlib import ExitStack

import concourse.bass as bass
import numpy as np
from concourse import mybir

F32, BF16, I32, U32 = mybir.dt.float32, mybir.dt.bfloat16, mybir.dt.int32, mybir.dt.uint32
ALU = mybir.AluOpType
ACT = mybir.ActivationFunctionType
AX = mybir.AxisListType

P = 128
B, L = 4, 1024
TB = L // P
NT = B * TB
H, HD = 16, 8
E0, F0 = 8, 512
E1, F1 = 16, 128
FS = 512
DR = 64
NS0 = NT + E0
NS1 = NT + E1
FC0 = F0 // P
FCS = FS // P
SA, CA, GA, SB, CB, GB = range(6)
LN_EPS = 1e-5
DEN_EPS = 1e-6
INV_SCALE = 1.0 / 12.0
NPART = 6
KROWS = NPART * HD
MROWS = 3
VW = 32


class Link:

    def __init__(self, eng, sem, base=0):
        self.eng, self.sem, self.base, self.n = eng, sem, base, 0

    def __call__(self, ins):
        self.n += 1
        ins.then_inc(self.sem, 1)
        self.eng.wait_ge(self.sem, self.base + self.n)


class Names:

    turn, halves = 0, ()

    @classmethod
    def start(cls, nc):
        free = list(nc.free_semaphores)
        cls.turn, cls.halves = 0, (free[0::2], free[1::2])

    def __init__(self, nc, prefix=""):
        self.nc, self.prefix, self.ctx, self.sems = nc, prefix, ExitStack(), []
        if prefix:
            self.numbers = iter(Names.halves[Names.turn])
            Names.turn = 1 - Names.turn

    def __enter__(self):
        return self

    def __exit__(self, *a):
        if self.sems:
            self.nc.clear_and_free_semaphores(self.sems)
        return self.ctx.__exit__(*a)

    def sb(self, name, shape, dt=F32):
        return self.ctx.enter_context(self.nc.sbuf_tensor(self.prefix + name, shape, dt))

    def ps(self, name, shape, dt=F32):
        return self.ctx.enter_context(self.nc.psum_tensor(self.prefix + name, shape, dt))

    def sem(self, name):
        self.sems.append(self.nc.alloc_semaphore(self.prefix + name, next(self.numbers)))
        return self.sems[-1]


def wait_apart(eng, sem, value, least=1):
    value = value if isinstance(value, int) else eng.to_reg(value)
    eng.wait_ge(sem, least)
    eng.wait_ge(sem, value)


def batches(eng, n, body):
    body(0, True)
    with eng.Fori(1, n) as i:
        body(i, False)


def ends_apart(eng, body):
    body(0, True)
    with eng.Fori(1, B - 1) as b:
        body(b, False)
    body(B - 1, False)


def phase_load(nc, D, M):
    with Names(nc, "ld_") as n:
        ld_x, ld_w = [n.sem(f"ld_x{b}") for b in range(B)], n.sem("ld_w")
        ld_c = n.sem("ld_c")
        act_done, dve_step, sc_ready = n.sem("act_done"), n.sem("dve_step"), n.sem("sc_ready")
        mod_mm, mod_out = n.sem("mod_mm"), n.sem("mod_out")
        col_mm = n.sem("col_mm")
        wmod = n.sb("wmod", [P, 2, 6 * P])
        cT = n.sb("cT", [P, 2, B])
        e = n.sb("sig_e", [P, 2, B])
        sc = n.sb("silu_c", [P, 2, B])
        scb = n.sb("silu_c_bc", [P, 2 * B, P])
        mod_ps = [n.ps(f"mod_ps{i}", [P, 1024]) for i in range(2)]
        col_ps = n.ps("col_ps", [P, 512])
        w_loads = [
            (M.ident, D["ident"]), (M.wq0, D["wq0"]), (M.wkv0, D["wkv0"]), (M.wo0, D["wo0"]),
            (M.bq0, D["bq0"]), (M.bkv0, D["bkv0"].partition_broadcast(P)), (M.bo0, D["bo0"].partition_broadcast(P)),
            (M.blockmask, D["blockmask"]), (M.headmask, D["headmask"]),
        ]
        with nc.Block() as block:
            @block.sync
            def _(sp):
                sp.dma_start(cT[:], D["cT"]).then_inc(ld_c, 16)
                sp.dma_start(wmod[:], D["wmod"]).then_inc(ld_c, 16)
                for b in range(B):
                    sp.dma_start(M.x[:, b * TB:(b + 1) * TB, :],
                                 D["x"][b].rearrange("(t p) e -> p t e", p=P)).then_inc(ld_x[b], 16)
                for dst, src in w_loads:
                    sp.dma_start(dst[:], src).then_inc(ld_w, 16)
                sp.wait_ge(ld_w, 16 * len(w_loads))

            @block.scalar
            def _(act):
                act.wait_ge(ld_c, 32)
                act.activation(e[:], cT[:], ACT.Exp, scale=-1.0).then_inc(act_done, 1)

            @block.tensor
            def _(pe):
                pe.wait_ge(sc_ready, 1)
                for k in range(2 * B):
                    if k >= 2:
                        pe.wait_ge(mod_out, k - 1)
                    for c0, c1 in ((0, 512), (512, 768)):
                        mm = pe.matmul(mod_ps[k % 2][:, c0:c1], scb[:, k, :], wmod[:, k // B, c0:c1],
                                       start=True, stop=True)
                    mm.then_inc(mod_mm, 1)
                for l in range(2):
                    for j in (SA, CA):
                        mm = pe.matmul(col_ps[:, (2 * l + j) * B:(2 * l + j + 1) * B],
                                       wmod[:, l, j * P:(j + 1) * P], sc[:, l, :], start=True, stop=True)
                mm.then_inc(col_mm, 1)

            @block.vector
            def _(dve):
                link = Link(dve, dve_step)
                dve.memset(M.zeros[:], 0.0)
                link(dve.memset(M.half[:], -0.5))
                dve.wait_ge(act_done, 1)
                link(dve.tensor_scalar(e[:], e[:], 1.0, None, ALU.add))
                link(dve.reciprocal(e[:], e[:]))
                link(dve.tensor_tensor(sc[:], cT[:], e[:], ALU.mult))
                dve.tensor_copy(scb[:], sc[:].rearrange("p l b -> p (l b)").unsqueeze(2).to_broadcast([P, 2 * B, P])).then_inc(sc_ready, 1)
                for b in range(B):
                    dve.wait_ge(ld_x[b], 16)
                    for t in range(b * TB, (b + 1) * TB):
                        dve.bn_stats(M.stats[:, t, :], M.x[:, t, :])
                dve.wait_ge(ld_w, 16 * len(w_loads))
                dve.tensor_copy(M.identb[:], M.ident[:])
                for k in range(2 * B):
                    dve.wait_ge(mod_mm, k + 1)
                    dve.tensor_copy(M.mod[:, k // B, k % B, :], mod_ps[k % 2][:, 0:6 * P]).then_inc(mod_out, 1)
                dve.wait_ge(mod_out, 2 * B)
                dve.wait_ge(col_mm, 1)
                link(dve.tensor_copy(M.modcol[:], col_ps[:, 0:4 * B].rearrange("p (l j b) -> p l j b", l=2, j=2)))
                link(dve.tensor_scalar(M.modcol[:, :, 1, :], M.modcol[:, :, 1, :], 1.0, None, ALU.add))
                for l in range(2):
                    cb = M.mod[:, l, :, CB * P:(CB + 1) * P]
                    link(dve.tensor_scalar(cb, cb, 1.0, None, ALU.add))
                    for g in (GA, GB):
                        gv = M.mod[:, l, :, g * P:(g + 1) * P]
                        s = scb[:, 0:B, :]
                        a = scb[:, B:2 * B, :]
                        link(dve.tensor_scalar(s, gv, 0.0, 2.0, ALU.is_ge, ALU.mult))
                        link(dve.tensor_scalar(a, gv, -1.0, None, ALU.mult))
                        link(dve.tensor_tensor(a, a, gv, ALU.max))
                        link(dve.tensor_scalar(a, a, 0.25, None, ALU.max))
                        link(dve.scalar_tensor_tensor(out=gv, in0=s, scalar=-1.0, in1=a, op0=ALU.add, op1=ALU.mult))


def variance_and_mean(dve, link, M, tiles, var_ready):
    st, d, v, mean = M.stats[:, tiles, :], M.ln_d[:, tiles], M.ln_v[:, tiles], M.mean[:, tiles]
    link(dve.tensor_tensor(d, st[:, :, 1], st[:, :, 4], ALU.subtract))
    link(dve.scalar_tensor_tensor(out=v, in0=d, scalar=P / 4.0, in1=d, op0=ALU.mult, op1=ALU.mult))
    link(dve.tensor_tensor(v, v, st[:, :, 2], ALU.add))
    link(dve.tensor_tensor(v, v, st[:, :, 5], ALU.add))
    dve.tensor_scalar(v, v, 1.0 / P, LN_EPS, ALU.mult, ALU.add).then_inc(var_ready, 1)
    link(dve.tensor_tensor(mean, st[:, :, 1], st[:, :, 4], ALU.add))
    link(dve.tensor_scalar(mean, mean, 0.5, None, ALU.mult))


def mean_and_rstd(dve, pool, link, M, var_ready, rstd_ready):
    if dve is not None:
        variance_and_mean(dve, link, M, slice(0, NT), var_ready)
    if pool is not None:
        pool.wait_ge(var_ready, 1)
        pool.tensor_tensor(M.rstd[:], M.ln_v[:], M.half[:], ALU.pow).then_inc(rstd_ready, 1)


def phase_linear_attention(nc, D, M):
    with Names(nc, "la_") as n:
        var_ready, rstd_ready = n.sem("var_ready"), n.sem("rstd_ready")
        dve_ln, dve_step = n.sem("dve_ln"), n.sem("dve_step")
        xn_ready, xn_T, hT_ready = n.sem("xn_ready"), n.sem("xn_T"), n.sem("hT_ready")
        kv_ones = n.sem("kv_ones")
        q_neg, k_neg = n.sem("q_neg"), n.sem("k_neg")
        q_mm, q_act, phiq_ready = n.sem("q_mm"), n.sem("q_act"), n.sem("phiq_ready")
        kv_mm, kv_bias, k_act, phik_ready = n.sem("kv_mm"), n.sem("kv_bias"), n.sem("k_act"), n.sem("phik_ready")
        s_mm, s_ready, num_mm, ctx_ready = n.sem("s_mm"), n.sem("s_ready"), n.sem("num_mm"), n.sem("ctx_ready")
        ctx_T, ctxT_ready, wog_ready, bog_added = n.sem("ctx_T"), n.sem("ctxT_ready"), n.sem("wog_ready"), n.sem("bog_added")
        pool_step, o_mm, x_done = n.sem("pool_step"), n.sem("o_mm"), n.sem("x_done")
        ld_later = n.sem("ld_later")
        psT = n.ps("psT", [P, L])
        psQ = n.ps("psQ", [P, L])
        psKV = n.ps("psKV", [P, 2 * L])
        xn = n.sb("xn", [P, TB, P])
        hT = n.sb("hT", [P, L])
        eq, phiq = n.sb("eq", [P, L]), n.sb("phiq", [P, L])
        ek, phik = n.sb("ek", [P, TB, P]), n.sb("phik", [P, TB, P])
        kvb = n.sb("kvb", [P, TB, 2 * P + 1])
        sm = n.sb("sm", [P, P + H])
        rden = n.sb("rden", [P, TB, H])
        ctx = n.sb("ctx", [P, TB, P])
        ctxT = n.sb("ctxT", [P, L])
        wog, bog = n.sb("wog", [P, P]), n.sb("bog", [P, P])
        NW = P + H
        TPK = 512 // NW
        groups = [(t, min(t + TPK, TB)) for t in range(0, TB, TPK)]

        def num_at(t):
            return psKV[:, (t // TPK) * 512 + (t % TPK) * NW:(t // TPK) * 512 + (t % TPK + 1) * NW]

        NG = len(groups)
        later = [
            (M.tri, D["tri"]), (M.onesm, D["onesm"]), (M.idents, D["idents"].partition_broadcast(P)),
            (M.tiles, D["tiles"].partition_broadcast(P)),
            (M.wr0, D["wr0"]), (M.br0, D["br0"].partition_broadcast(P)),
            (M.w10, D["w10"]), (M.w20, D["w20"]),
            (M.b10, D["b10"].partition_broadcast(P)), (M.b20, D["b20"].partition_broadcast(P)),
            (M.wd1, D["wd1"]), (M.wuq1, D["wuq1"]), (M.wukv1, D["wukv1"]), (M.wkr1, D["wkr1"]),
            (M.bcol1, D["bcol1"]), (M.bv1, D["bv1"].partition_broadcast(P)),
            (M.wo1, D["wo1"]), (M.bo1, D["bo1"].partition_broadcast(P)),
            (M.wr1, D["wr1"]),
        ]

        with nc.Block() as block:
            @block.sync
            def _(sp):
                for dst, src in later:
                    sp.dma_start(dst[:], src).then_inc(ld_later, 16)
                for l, ns in enumerate((NS0, NS1)):
                    sp.dma_start(M.sorted[l].rearrange("(s p) e -> p s e", p=P),
                                 M.zeros[:].unsqueeze(1).to_broadcast([P, ns, P])).then_inc(ld_later, 16)
                sp.wait_ge(ld_later, 16 * (2 + len(later)))

            @block.gpsimd
            def _(pool):
                mean_and_rstd(None, pool, None, M, var_ready, rstd_ready)

                def batch(b, first):
                    if not first:
                        pool.wait_ge(o_mm, b * 2)
                        pool.wait_ge(bog_added, b)
                    ga = M.mod[:, 0, b, GA * P:(GA + 1) * P]
                    pool.tensor_tensor(bog[:], M.bo0[:], ga, ALU.mult).then_inc(pool_step, 1)
                    pool.tensor_tensor(wog[:], M.wo0[:], ga, ALU.mult).then_inc(wog_ready, 1)
                    pool.wait_ge(pool_step, b + 1)
                    pool.wait_ge(k_act, b * 2 + 2)
                    pool.tensor_tensor(phik[:], ek[:], phik[:], ALU.add).then_inc(phik_ready, 1)
                    pool.wait_ge(xn_ready, b * TB + TB)
                    xb = M.x[:, bass.ds(b * TB, TB), :]
                    pool.tensor_tensor(xb, xb, bog[:].unsqueeze(1).to_broadcast([P, TB, P]),
                                       ALU.add).then_inc(bog_added, 1)

                batches(pool, B, batch)

            @block.vector
            def _(dve):
                dve.memset(kvb[:, :, 2 * P:2 * P + 1], 1.0).then_inc(kv_ones, 1)
                mean_and_rstd(dve, None, Link(dve, dve_ln), M, var_ready, rstd_ready)
                dve.wait_ge(rstd_ready, 1)

                def batch(b, first):
                    link = Link(dve, dve_step, b * (2 * NG + 2))
                    if not first:
                        dve.wait_ge(xn_T, b * 2)
                    for t in range(TB):
                        i = b * TB + t
                        dve.tensor_scalar(xn[:, t, :], M.x[:, i, :], M.mean[:, bass.ds(i, 1)],
                                          M.rstd[:, bass.ds(i, 1)], ALU.subtract, ALU.mult).then_inc(xn_ready, 1)
                    if not first:
                        dve.wait_ge(num_mm, b * NG)
                    for j in range(2):
                        dve.wait_ge(q_mm, b * 2 + j + 1)
                        cols = slice(j * 512, (j + 1) * 512)
                        dve.tensor_scalar(eq[:, cols], psQ[:, cols], M.bq0[:, 0:1], 0.0, ALU.add,
                                          ALU.min).then_inc(q_neg, 1)
                    for j in range(4):
                        dve.wait_ge(kv_mm, b * 4 + j + 1)
                        dve.tensor_tensor(kvb[:, 2 * j:2 * j + 2, 0:2 * P],
                                          psKV[:, j * 512:(j + 1) * 512].rearrange("p (t f) -> p t f", t=2),
                                          M.bkv0[:].unsqueeze(1).to_broadcast([P, 2, 2 * P]),
                                          ALU.add).then_inc(kv_bias, 1)
                    dve.wait_ge(kv_bias, b * 4 + 4)
                    dve.tensor_scalar(ek[:], kvb[:, :, 0:P], 0.0, None, ALU.min).then_inc(k_neg, 1)
                    dve.wait_ge(q_act, b * 2 + 2)
                    dve.tensor_tensor(phiq[:], eq[:], phiq[:], ALU.add).then_inc(phiq_ready, 1)
                    dve.wait_ge(s_mm, b + 1)
                    dve.tensor_tensor(sm[:, 0:P], psT[:, 0:P], M.blockmask[:], ALU.mult).then_inc(s_ready, 1)
                    dve.tensor_scalar(sm[:, P:NW], M.headmask[:], psT[:, P:P + 1], None, ALU.mult).then_inc(s_ready, 1)
                    for g, (t0, t1) in enumerate(groups):
                        dve.wait_ge(num_mm, b * NG + g + 1)
                        nd = psKV[:, g * 512:g * 512 + (t1 - t0) * NW].rearrange("p (t f) -> p t f", f=NW)
                        link(dve.tensor_scalar(rden[:, t0:t1, :], nd[:, :, P:NW], DEN_EPS, None, ALU.add))
                        link(dve.reciprocal(rden[:, t0:t1, :], rden[:, t0:t1, :]))
                        dve.tensor_tensor(ctx[:, t0:t1, :].rearrange("p t (h d) -> p t h d", h=H),
                                          nd[:, :, 0:P].rearrange("p t (h d) -> p t h d", h=H),
                                          rden[:, t0:t1, :].unsqueeze(3).to_broadcast([P, t1 - t0, H, HD]),
                                          ALU.mult).then_inc(ctx_ready, 1)
                    dve.wait_ge(bog_added, b + 1)
                    for j in range(2):
                        dve.wait_ge(o_mm, b * 2 + j + 1)
                        xj = M.x[:, bass.ds(b * TB + 4 * j, 4), :]
                        link(dve.tensor_tensor(xj, xj, psT[:, j * 512:(j + 1) * 512].rearrange("p (t f) -> p t f", t=4),
                                               ALU.add))
                        for t in range(4 * j, 4 * j + 4):
                            ins = dve.bn_stats(M.stats[:, b * TB + t, :], M.x[:, b * TB + t, :])
                    ins.then_inc(x_done, 1)

                batches(dve, B, batch)

            @block.scalar
            def _(act):
                def batch(b, first):
                    if not first:
                        act.wait_ge(s_mm, b)
                        act.wait_ge(num_mm, b * NG)
                    for j in range(2):
                        wait_apart(act, xn_T, b * 2 + j + 1)
                        act.activation(hT[:, j * 512:(j + 1) * 512], psT[:, j * 512:(j + 1) * 512], ACT.Identity,
                                       bias=M.modcol[:, 0, 0, bass.ds(b, 1)],
                                       scale=M.modcol[:, 0, 1, bass.ds(b, 1)]).then_inc(hT_ready, 1)
                    for j in range(2):
                        cols = slice(j * 512, (j + 1) * 512)
                        act.wait_ge(q_neg, b * 2 + j + 1)
                        act.activation(phiq[:, cols], psQ[:, cols], ACT.Relu, bias=M.bq0[:, 0:1])
                        act.activation(eq[:, cols], eq[:, cols], ACT.Exp).then_inc(q_act, 1)
                    act.wait_ge(kv_bias, b * 4 + 4)
                    act.activation(phik[:], kvb[:, :, 0:P], ACT.Relu).then_inc(k_act, 1)
                    act.wait_ge(k_neg, b + 1)
                    act.activation(ek[:], ek[:], ACT.Exp).then_inc(k_act, 1)
                    for j in range(2):
                        act.wait_ge(ctx_T, b * 2 + j + 1)
                        act.activation(ctxT[:, j * 512:(j + 1) * 512], psQ[:, j * 512:(j + 1) * 512],
                                       ACT.Copy).then_inc(ctxT_ready, 1)

                batches(act, B, batch)

            @block.tensor
            def _(pe):
                def batch(b, first):
                    if not first:
                        pe.wait_ge(x_done, b)
                    for t in range(TB):
                        pe.wait_ge(xn_ready, b * TB + t + 1)
                        mm = pe.transpose(psT[:, t * P:(t + 1) * P], xn[:, t, :], M.ident[:])
                        if t % 4 == 3:
                            mm.then_inc(xn_T, 1)
                    for j in range(2):
                        pe.wait_ge(hT_ready, b * 2 + j + 1)
                        cols = slice(j * 512, (j + 1) * 512)
                        pe.matmul(psQ[:, cols], M.wq0[:], hT[:, cols], start=True, stop=True).then_inc(q_mm, 1)
                    for t in range(TB):
                        mm = pe.matmul(psKV[:, t * 256:(t + 1) * 256], hT[:, t * P:(t + 1) * P], M.wkv0[:],
                                       start=True, stop=True)
                        if t % 2 == 1:
                            mm.then_inc(kv_mm, 1)
                    pe.wait_ge(phik_ready, b + 1)
                    if first:
                        pe.wait_ge(kv_ones, 1)
                    for t in range(TB):
                        mm = pe.matmul(psT[:, 0:P + 1], phik[:, t, :], kvb[:, t, P:2 * P + 1],
                                       start=(t == 0), stop=(t == TB - 1))
                    mm.then_inc(s_mm, 1)
                    pe.wait_ge(phiq_ready, b + 1)
                    pe.wait_ge(s_ready, b * 2 + 2)
                    for g, (t0, t1) in enumerate(groups):
                        for t in range(t0, t1):
                            mm = pe.matmul(num_at(t), phiq[:, t * P:(t + 1) * P], sm[:], start=True, stop=True)
                        mm.then_inc(num_mm, 1)
                    for t in range(TB):
                        pe.wait_ge(ctx_ready, b * NG + t // TPK + 1)
                        mm = pe.transpose(psQ[:, t * P:(t + 1) * P], ctx[:, t, :], M.ident[:])
                        if t % 4 == 3:
                            mm.then_inc(ctx_T, 1)
                    pe.wait_ge(wog_ready, b + 1)
                    for t in range(TB):
                        pe.wait_ge(ctxT_ready, b * 2 + t // 4 + 1)
                        mm = pe.matmul(psT[:, t * P:(t + 1) * P], ctxT[:, t * P:(t + 1) * P], wog[:],
                                       start=True, stop=True)
                        if t % 4 == 3:
                            mm.then_inc(o_mm, 1)

                batches(pe, B, batch)


def phase_route(nc, D, M, l):
    E, NS, wr = ((E0, NS0, M.wr0), (E1, NS1, M.wr1))[l]
    with Names(nc, f"rt{l}_") as n:
        var_ready, rstd_ready = n.sem("var_ready"), n.sem("rstd_ready")
        dve_ln, dve_step = n.sem("dve_ln"), n.sem("dve_step")
        xn_ready, h_ready, h_T, hT_ready = n.sem("xn_ready"), n.sem("h_ready"), n.sem("h_T"), n.sem("hT_ready")
        lg_mm, lg_out, shifted, exp_done = n.sem("lg_mm"), n.sem("lg_out"), n.sem("shifted"), n.sem("exp_done")
        oh_ready, rank_mm, slot_ready, scattered = n.sem("oh_ready"), n.sem("rank_mm"), n.sem("slot_ready"), n.sem("scattered")
        dve_rt, half_done = n.sem("dve_rt"), n.sem("half_done")
        psT = [n.ps(f"psT{i}", [P, 512]) for i in range(2)]
        psL = [n.ps(f"psL{i}", [P, TB * E]) for i in range(2)]
        psR, psN = n.ps("psR", [P, NT * E]), n.ps("psN", [P, NT * E])
        xn = n.sb("xn", [P, TB, P])
        lg, t1, oh = n.sb("lg", [P, NT, E]), n.sb("t1", [P, NT, E]), n.sb("oh", [P, NT, E])
        scan = [n.sb(f"scan{i}", [P, NT, E]) for i in range(2)]
        tot = n.sb("tot", [P, NT, E])
        r1 = n.sb("r1", [P, NT])
        cnt = [n.sb(f"cnt{i}", [P, E]) for i in range(3)]
        cnti = n.sb("cnti", [P, E], I32)
        cmp, cmps = n.sb("cmp", [1, NS, E]), n.sb("cmps", [1, NS])
        posf = n.sb("posf", [P, NT])

        def per_tile(v):
            return v.unsqueeze(2).to_broadcast([P, NT, E])

        def per_expert(v, k=NT):
            return v.unsqueeze(1).to_broadcast([v.shape[0], k, E])

        ld_experts = n.sem("ld_experts")

        with nc.Block() as block:
            @block.sync
            def _(sp):
                if l == 1:
                    for dst, name in ((M.wgu1, "wgu1"), (M.wdn1, "wdn1"), (M.wsg1, "wsg1"), (M.wsd1, "wsd1")):
                        sp.dma_start(dst[:], D[name]).then_inc(ld_experts, 16)
                    sp.wait_ge(ld_experts, 16 * 4)

            @block.vector
            def _(dve):
                mean_and_rstd(dve, None, Link(dve, dve_ln), M, var_ready, rstd_ready)
                dve.wait_ge(rstd_ready, 1)

                def batch(b, first):
                    link = Link(dve, dve_step, b * (TB + 1))
                    for t in range(TB):
                        i = b * TB + t
                        ins = dve.tensor_scalar(xn[:, t, :], M.x[:, i, :], M.mean[:, bass.ds(i, 1)],
                                                M.rstd[:, bass.ds(i, 1)], ALU.subtract, ALU.mult)
                        ins.then_inc(dve_step, 1)
                        link.n += 1
                    dve.wait_ge(dve_step, link.base + link.n)
                    link(dve.tensor_tensor(xn[:], xn[:], M.mod[:, l, b, CB * P:(CB + 1) * P].unsqueeze(1).to_broadcast([P, TB, P]),
                                           ALU.mult))
                    dve.tensor_tensor(M.h[:, bass.ds(b * TB, TB), :], xn[:],
                                      M.mod[:, l, b, SB * P:(SB + 1) * P].unsqueeze(1).to_broadcast([P, TB, P]),
                                      ALU.add).then_inc(h_ready, 1)

                def batch_all(b, first):
                    if not first:
                        dve.wait_ge(h_ready, b)
                    batch(b, first)

                batches(dve, B, batch_all)
                for b in range(B):
                    dve.wait_ge(lg_mm, b + 1)
                    src = psL[b % 2][:].rearrange("p (t e) -> p t e", e=E)
                    dst = lg[:, b * TB:(b + 1) * TB, :]
                    if l == 0:
                        dve.tensor_tensor(dst, src, per_expert(M.br0[:], TB), ALU.add).then_inc(lg_out, 1)
                    else:
                        dve.tensor_copy(dst, src).then_inc(lg_out, 1)
                dve.wait_ge(lg_out, B)
                link = Link(dve, dve_rt)
                link(dve.tensor_reduce(r1[:], lg[:], AX.X, ALU.max))
                if l == 0:
                    dve.tensor_tensor(t1[:], lg[:], per_tile(r1[:]), ALU.subtract).then_inc(shifted, 1)
                    dve.wait_ge(exp_done, 1)
                    link(dve.tensor_reduce(posf[:], t1[:], AX.X, ALU.add))
                    link(dve.tensor_reduce(r1[:], t1[:], AX.X, ALU.max))
                    link(dve.reciprocal(posf[:], posf[:]))
                    link(dve.tensor_tensor(M.gate[:], r1[:], posf[:], ALU.mult))
                    link(dve.tensor_tensor(oh[:], t1[:], per_tile(r1[:]), ALU.is_equal))
                else:
                    dve.tensor_scalar(posf[:], r1[:], -1.0, 88.0, ALU.mult, ALU.min).then_inc(shifted, 1)
                    dve.wait_ge(exp_done, 1)
                    link(dve.tensor_scalar(posf[:], posf[:], 1.0, None, ALU.add))
                    link(dve.reciprocal(M.gate[:], posf[:]))
                    link(dve.tensor_tensor(oh[:], lg[:], per_tile(r1[:]), ALU.is_equal))
                link(dve.scalar_tensor_tensor(out=t1[:], in0=oh[:], scalar=-64.0, in1=per_expert(M.idents[:, 0:E]),
                                              op0=ALU.mult, op1=ALU.add))
                link(dve.tensor_reduce(r1[:], t1[:], AX.X, ALU.min))
                dve.tensor_tensor(oh[:], t1[:], per_tile(r1[:]), ALU.is_equal).then_inc(oh_ready, 1)
                if l == 1:
                    dve.wait_ge(h_T, 2 * B)
                    for i in range(NT):
                        dve.tensor_scalar(M.h[:, i, :], M.h[:, i, :], M.gate[:, i:i + 1], None, ALU.mult).then_inc(half_done, 1)
                dve.wait_ge(rank_mm, 2)
                link(dve.tensor_copy(tot[:], psN[:].rearrange("p (t e) -> p t e", e=E)))
                src, d, k = tot, 1, 0
                while d < NT:
                    dst = scan[k % 2]
                    link(dve.tensor_copy(dst[:, 0:d, :], src[:, 0:d, :]))
                    link(dve.tensor_tensor(dst[:, d:NT, :], src[:, d:NT, :], src[:, 0:NT - d, :], ALU.add))
                    src, d, k = dst, 2 * d, k + 1
                link(dve.tensor_scalar(cnt[0][:], src[:, NT - 1, :], float(P - 1), None, ALU.add))
                link(dve.tensor_copy(cnti[:], cnt[0][:]))
                link(dve.tensor_scalar(cnti[:], cnti[:], P.bit_length() - 1, None, ALU.arith_shift_right))
                link(dve.tensor_copy(cnt[2][:], cnti[:]))
                ends, d, k = cnt[2], 1, 0
                while d < E:
                    dst = cnt[k % 2]
                    link(dve.tensor_copy(dst[:, 0:d], ends[:, 0:d]))
                    link(dve.tensor_tensor(dst[:, d:E], ends[:, d:E], ends[:, 0:E - d], ALU.add))
                    ends, d, k = dst, 2 * d, k + 1
                starts = cnt[k % 2]
                link(dve.tensor_tensor(starts[:], ends[:], cnt[2][:], ALU.subtract))
                link(dve.tensor_tensor(t1[:], src[:], tot[:], ALU.subtract))
                link(dve.scalar_tensor_tensor(out=t1[:], in0=per_expert(starts[:]), scalar=float(P), in1=t1[:],
                                              op0=ALU.mult, op1=ALU.add))
                link(dve.tensor_tensor(t1[:], t1[:], psR[:].rearrange("p (t e) -> p t e", e=E), ALU.add))
                link(dve.tensor_tensor(t1[:], t1[:], oh[:], ALU.mult))
                link(dve.tensor_reduce(posf[:], t1[:], AX.X, ALU.add))
                dve.tensor_copy(M.slot[:], posf[:]).then_inc(slot_ready, 1)
                link(dve.tensor_tensor(cmp[:], M.tiles[0:1, 0:NS].unsqueeze(2).to_broadcast([1, NS, E]),
                                       per_expert(ends[0:1, :], NS), ALU.is_ge))
                link(dve.tensor_reduce(cmps[:], cmp[:], AX.X, ALU.add))
                link(dve.tensor_scalar(cmps[:], cmps[:], float(E - 1), None, ALU.min))
                link(dve.tensor_copy(M.expert[:, 0:NS], cmps[:]))

            @block.gpsimd
            def _(pool):
                mean_and_rstd(None, pool, None, M, var_ready, rstd_ready)
                pool.wait_ge(slot_ready, 1)
                if l == 1:
                    pool.wait_ge(half_done, NT)
                for i in range(NT):
                    pool.indirect_dma_start(
                        out=M.sorted[l][:, :], out_offset=bass.IndirectOffsetOnAxis(ap=M.slot[:, i:i + 1], axis=0),
                        in_=M.h[:, i, :], in_offset=None).then_inc(scattered, 16)
                pool.wait_ge(scattered, 16 * NT)

            @block.tensor
            def _(pe):
                for b in range(B):
                    pe.wait_ge(h_ready, b + 1)
                    for j in range(2):
                        if b >= 1:
                            pe.wait_ge(hT_ready, 2 * (b - 1) + j + 1)
                        for t in range(4):
                            mm = pe.transpose(psT[j][:, t * P:(t + 1) * P], M.h[:, b * TB + 4 * j + t, :], M.ident[:])
                        mm.then_inc(h_T, 1)
                    if b >= 2:
                        pe.wait_ge(lg_out, b - 1)
                    for t in range(TB):
                        pe.wait_ge(hT_ready, 2 * b + t // 4 + 1)
                        i = b * TB + t
                        mm = pe.matmul(psL[b % 2][:, t * E:(t + 1) * E], M.hT[:, i * P:(i + 1) * P], wr[:],
                                       start=True, stop=True)
                    mm.then_inc(lg_mm, 1)
                pe.wait_ge(oh_ready, 1)
                flat = oh[:].rearrange("p t e -> p (t e)")
                pe.matmul(psR[:], M.tri[:], flat, start=True, stop=True).then_inc(rank_mm, 1)
                pe.matmul(psN[:], M.onesm[:], flat, start=True, stop=True).then_inc(rank_mm, 1)

            @block.scalar
            def _(act):
                for b in range(B):
                    for j in range(2):
                        act.wait_ge(h_T, 2 * b + j + 1)
                        c = (2 * b + j) * 512
                        act.activation(M.hT[:, c:c + 512], psT[j][:], ACT.Copy).then_inc(hT_ready, 1)
                act.wait_ge(shifted, 1)
                v = t1 if l == 0 else posf
                act.activation(v[:], v[:], ACT.Exp).then_inc(exp_done, 1)


class Steps:

    UNROLL = 8

    def __init__(self, n, lag):
        assert n % self.UNROLL == 0
        self.n, self.lag = n, lag

    def run(self, eng, step):
        for r in range(self.UNROLL):
            step(0, r)
        with eng.Fori(1, self.n // self.UNROLL) as i:
            for r in range(self.UNROLL):
                step(i, r)
        for r in range(self.lag):
            step(self.n // self.UNROLL, r)

    def has(self, j):
        return not isinstance(j, int) or 0 <= j < self.n


def after(j, k):
    return not isinstance(j, int) or j >= k


GT = 4
LAG_T, LAG_Y = 2, 4
RING = 4


class Experts:

    def __init__(self, nc, kind, M, n, E):
        self.nc, self.kind, self.M, self.n, self.E, self.known = nc, kind, M, n, E, {}

    def fetch(self, i, r):
        first = {0: -4, 1: 0, 5: 4}.get(r)
        if first is None or (isinstance(i, int) and not 0 <= i * Steps.UNROLL + first < self.n):
            return
        _, values = self.nc.values_load_multi_w_load_instructions(
            self.M.expert[0:1, bass.ds(i * Steps.UNROLL + first, 4)], engines=[self.kind],
            min_val=0, max_val=self.E - 1,
            skip_runtime_bounds_check_because="routing clamps them on chip: counts of experts, at most E - 1")
        for t in range(4):
            self.known[first + t] = values[t]

    def __getitem__(self, offset):
        return self.known[offset]


def move_tiles(sp, n, src, dst, rows, y, loaded, stored, x_T, y_ready):
    ng = n // GT

    def group(g, q):
        if not isinstance(g, int) or g < ng:
            if not isinstance(g, int) or g >= 2:
                wait_apart(sp, x_T, g - 1)
            sp.dma_start(rows[q][:], src[:, bass.ds(g * GT, GT), :]).then_inc(loaded[q], 16)
        if not isinstance(g, int) or g >= 2:
            wait_apart(sp, y_ready, (g - 1) * GT)
            sp.dma_start(dst[:, bass.ds((g - 2) * GT, GT), :], y[q][:]).then_inc(stored[q], 16)

    for q in range(2):
        group(q, q)
    with sp.Fori(1, ng // 2) as i:
        for q in range(2):
            group(i * 2 + q, q)
    for q in range(2):
        group(ng + q, q)
    for q in range(2):
        sp.wait_ge(stored[q], 16 * (ng // 2))


def phase_experts0(nc, D, M):
    S = Steps(NS0, LAG_Y)
    U = S.UNROLL
    with Names(nc, "e0_") as n:
        loaded = [n.sem(f"loaded{i}") for i in range(2)]
        x_T, xT_ready, mm1_done, h1_ready = n.sem("x_T"), n.sem("xT_ready"), n.sem("mm1_done"), n.sem("h1_ready")
        h1_T, h1T_ready, mm2_done, y_ready = n.sem("h1_T"), n.sem("h1T_ready"), n.sem("mm2_done"), n.sem("y_ready")
        stored = [n.sem(f"stored{i}") for i in range(2)]
        rows = [n.sb(f"rows{i}", [P, GT, P]) for i in range(2)]
        xT = [n.sb(f"xT{i}", [P, GT, P]) for i in range(2)]
        h1 = [n.sb(f"h1_{i}", [P, F0]) for i in range(RING)]
        h1T = [n.sb(f"h1T{i}", [P, FC0, P]) for i in range(RING)]
        y = [n.sb(f"y{i}", [P, GT, P]) for i in range(2)]
        psX = [n.ps(f"psX{i}", [P, 512]) for i in range(2)]
        ps1 = [n.ps(f"ps1{i}", [P, 512]) for i in range(2)]
        ps2 = [n.ps(f"ps2{i}", [P, 512]) for i in range(2)]
        psY = [n.ps(f"psY{i}", [P, 512]) for i in range(2)]
        src = M.sorted[0].rearrange("(s p) e -> p s e", p=P)
        dst = M.result[0].rearrange("(s p) e -> p s e", p=P)

        with nc.Block() as block:
            @block.sync
            def _(sp):
                move_tiles(sp, NS0, src, dst, rows, y, loaded, stored, x_T, y_ready)

            @block.tensor
            def _(pe):
                expert = Experts(nc, mybir.EngineType.PE, M, NS0, E0)

                def step(i, r):
                    k, gs = i * U + r, r // GT
                    expert.fetch(i, r)
                    if S.has(k) and r % GT == 0:
                        pe.wait_ge(loaded[gs], i * 16 + 16)
                        if after(k, U):
                            pe.wait_ge(xT_ready, i * 2 + gs - 1)
                        for t in range(GT):
                            mm = pe.transpose(psX[gs][:, t * P:(t + 1) * P], rows[gs][:, t, :], M.ident[:])
                        mm.then_inc(x_T, 1)
                    if S.has(k - 1):
                        j = (r - 1) % U
                        if j % GT == 0:
                            pe.wait_ge(xT_ready, i * 2 + (r - 1) // GT + 1)
                        if after(k - 1, 2):
                            pe.wait_ge(h1_ready, k - 2)
                        pe.matmul(ps1[j % 2][:], xT[j // GT][:, j % GT, :], M.w10[:, bass.ds(expert[r - 1], 1), :], start=True,
                                  stop=True).then_inc(mm1_done, 1)
                    if S.has(k - LAG_T):
                        j, q, o = k - LAG_T, (r - LAG_T) % 2, (r - LAG_T) % RING
                        pe.wait_ge(h1_ready, j + 1)
                        if after(j, 2):
                            pe.wait_ge(h1T_ready, j - 1)
                        for c in range(FC0):
                            mm = pe.transpose(ps2[q][:, c * P:(c + 1) * P], h1[o][:, c * P:(c + 1) * P], M.ident[:])
                        mm.then_inc(h1_T, 1)
                    if S.has(k - LAG_Y):
                        j, q, o = k - LAG_Y, (r - LAG_Y) % 2, (r - LAG_Y) % RING
                        e = expert[r - LAG_Y]
                        pe.wait_ge(h1T_ready, j + 1)
                        if after(j, 2):
                            pe.wait_ge(y_ready, j - 1)
                        for c in range(FC0):
                            mm = pe.matmul(psY[q][:, 0:P], h1T[o][:, c, :], M.w20[:, bass.ds(e, 1), c, :],
                                           start=(c == 0), stop=(c == FC0 - 1))
                        mm.then_inc(mm2_done, 1)

                S.run(pe, step)

            @block.vector
            def _(dve):
                expert = Experts(nc, mybir.EngineType.DVE, M, NS0, E0)

                def step(i, r):
                    k = i * U + r
                    expert.fetch(i, r)
                    if S.has(k - 1):
                        q, e = (r - 1) % 2, expert[r - 1]
                        dve.wait_ge(mm1_done, k)
                        if after(k - 1, RING):
                            dve.wait_ge(h1_T, k - RING)
                        dve.tensor_tensor(h1[(r - 1) % RING][:], ps1[q][:], M.b10[:, bass.ds(e, 1), :].rearrange("p o f -> p (o f)"),
                                          ALU.add).then_inc(h1_ready, 1)
                    if S.has(k - LAG_Y):
                        j = (r - LAG_Y) % U
                        e = expert[r - LAG_Y]
                        dve.wait_ge(mm2_done, k - LAG_Y + 1)
                        if after(k - LAG_Y, U) and j % GT == 0:
                            dve.wait_ge(stored[j // GT], (i if r >= LAG_Y else i - 1) * 16)
                        dve.tensor_tensor(y[j // GT][:, j % GT, :], psY[j % 2][:, 0:P],
                                          M.b20[:, bass.ds(e, 1), :].rearrange("p o f -> p (o f)"),
                                          ALU.add).then_inc(y_ready, 1)

                S.run(dve, step)

            @block.scalar
            def _(act):
                def step(i, r):
                    k, gs = i * U + r, r // GT
                    if S.has(k) and r % GT == 0:
                        act.wait_ge(x_T, i * 2 + gs + 1)
                        if after(k, U):
                            act.wait_ge(mm1_done, k - GT)
                        act.activation(xT[gs][:].rearrange("p t e -> p (t e)"), psX[gs][:], ACT.Copy).then_inc(xT_ready, 1)
                    if S.has(k - LAG_T):
                        j, q, o = k - LAG_T, (r - LAG_T) % 2, (r - LAG_T) % RING
                        act.wait_ge(h1_T, j + 1)
                        if after(j, RING):
                            act.wait_ge(mm2_done, j - RING + 1)
                        act.activation(h1T[o][:].rearrange("p c t -> p (c t)"), ps2[q][:], ACT.Relu).then_inc(h1T_ready, 1)

                S.run(act, step)


QUAD = 4
NGRP = B * H // QUAD
KC = L // P
GSTEPS = 2 * KC
BODY = 2 * GSTEPS
AHEAD = 12
NSTEPS = NGRP * GSTEPS
VC = QUAD * (HD + 1)


def declare_heads(M, n):
    M.Q = [n.sb(f"Q{i}", [P, QUAD, L], BF16) for i in range(2)]
    M.K = [n.sb(f"K{i}", [P, 2, L], BF16) for i in range(2)]
    M.KA = [n.sb(f"KA{i}", [P, 2, L], BF16) for i in range(2)]
    M.V = [n.sb(f"V{i}", [P, KC, VC + VW], F32) for i in range(2)]
    M.mp = n.sb("mp", [P, P // (QUAD * 4), QUAD * 4], BF16)


def phase_project1(nc, D, M):
    with Names(nc, "p1_") as n:
        ld = n.sem("ld_rope")
        var_ready, rstd_ready = n.sem("var_ready"), n.sem("rstd_ready")
        dve_ln, dve_step, dve_add = n.sem("dve_ln"), n.sem("dve_step"), n.sem("dve_add")
        gathered = [n.sem(f"gathered{i}") for i in range(B)]
        weighed = n.sb("weighed", [P, TB, P])
        xn_ready, xn_T, hT_ready = n.sem("xn_ready"), n.sem("xn_T"), n.sem("hT_ready")
        ct_mm, ct_ready, u_mm, rot_read = n.sem("ct_mm"), n.sem("ct_ready"), n.sem("u_mm"), n.sem("rot_read")
        v_mm, v_out, full_ready, part1, rest1, part2, part3 = (n.sem("v_mm"), n.sem("v_out"), n.sem("full_ready"),
            n.sem("part1"), n.sem("rest1"), n.sem("part2"), n.sem("part3"))
        qk_stored, v_stored = [n.sem(f"qk_stored{i}") for i in range(2)], n.sem("v_stored")
        zeroed, ld_ones = n.sem("zeroed"), n.sem("ld_ones")
        rope = n.sb("rope", [P, 2, L])
        ones = n.sb("ones", [MROWS, L], BF16)
        xn = n.sb("xn", [P, 4, P])
        hT, ctT = n.sb("hT", [P, 512]), n.sb("ctT", [P, 512])
        ras = [n.sb(f"ra{i}", [P, 512]) for i in range(2)]
        rbs = [n.sb(f"rb{i}", [P, 512]) for i in range(2)]
        full, rest = n.sb("full", [P, 2, 512]), n.sb("rest", [P, 2, 512])
        parts = [n.sb(f"part{i}", [P, 2, L], BF16) for i in range(3)]
        vout = n.sb("vout", [P, TB, H, HD + 1])
        psT, psC = n.ps("psT", [P, 512]), n.ps("psC", [P, 512])
        psR = [[n.ps(f"psR{i}_{j}", [P, 512]) for j in range(3)] for i in range(2)]
        PARTS = ((0, 0), (0, 1), (1, 0), (1, 1), (0, 2), (2, 0))

        def halves(eng, body):
            def batch(b, first):
                for j in range(2):
                    body(b, j, b * 2 + j, first and j == 0)
            batches(eng, B, batch)

        with nc.Block() as block:
            @block.sync
            def _(sp):
                sp.dma_start(rope[:], D["rope"]).then_inc(ld, 16)
                sp.wait_ge(zeroed, 3)
                for k in M.K:
                    for r in range(2):
                        for p in range(2):
                            sp.dma_start(k[64 * r + KROWS:64 * r + KROWS + MROWS, p, :], ones[0:MROWS, :]).then_inc(ld_ones, 16)
                sp.wait_ge(ld_ones, 16 * 8)

                def batch(b, first):
                    wait_apart(sp, v_out, b * 2 + 3)
                    for q in range(4):
                        sp.dma_start(M.v_rows[bass.ds(b * 4 + q, 1), :, :, :].rearrange("o p t c -> (o p) t c"),
                                     vout[:, :, 4 * q:4 * q + 4, :].rearrange("p t h c -> p t (h c)")).then_inc(v_stored, 16)
                    for qk in range(2):
                        wait_apart(sp, part3, b * 4 + 3 + qk)
                        for c, which in enumerate(PARTS):
                            dst = M.qk_rows[qk][bass.ds(b * H, H), c * HD:(c + 1) * HD, :]
                            sp.dma_start(dst, parts[which[qk]][:, qk, :]).then_inc(qk_stored[qk], 16)

                batches(sp, B, batch)
                for qk in range(2):
                    sp.wait_ge(qk_stored[qk], 16 * NPART * B)
                sp.wait_ge(v_stored, 16 * 4 * B)

            @block.gpsimd
            def _(pool):
                def gather(b):
                    for i in range(b * TB, (b + 1) * TB):
                        pool.indirect_dma_start(
                            out=M.h[:, i, :], out_offset=None, in_=M.result[0][:, :],
                            in_offset=bass.IndirectOffsetOnAxis(ap=M.slot[:, i:i + 1], axis=0)).then_inc(gathered[b], 16)

                def rstd(b):
                    pool.wait_ge(var_ready, b + 1)
                    tiles = bass.ds(b * TB, TB)
                    pool.tensor_tensor(M.rstd[:, tiles], M.ln_v[:, tiles], M.half[:, 0:TB], ALU.pow).then_inc(rstd_ready, 1)

                gather(0)
                gather(1)
                rstd(0)
                gather(2)

                def half(b, j, m, first):
                    cols = slice(j * 512, (j + 1) * 512)
                    for qk in range(2):
                        pool.wait_ge(part1, m * 2 + qk + 1)
                        if not first:
                            pool.wait_ge(part3, m * 2 - 1 + qk)
                        pool.tensor_tensor(rest[:, qk, :], full[:, qk, :], parts[0][:, qk, cols],
                                           ALU.subtract).then_inc(rest1, 1)
                        pool.wait_ge(part2, m * 2 + qk + 1)
                        pool.tensor_tensor(parts[2][:, qk, cols], rest[:, qk, :], parts[1][:, qk, cols],
                                           ALU.subtract).then_inc(part3, 1)

                for b in range(B):
                    for j in range(2):
                        half(b, j, b * 2 + j, b == 0 and j == 0)
                        if j == 0 and b < B - 1:
                            rstd(b + 1)
                    if b == 0:
                        gather(3)

            @block.vector
            def _(dve):
                dve.memset(vout[:, :, :, HD:HD + 1], 1.0).then_inc(v_out, 1)
                dve.memset(ones[:], 1.0).then_inc(zeroed, 1)
                for k in M.K:
                    dve.memset(k[:], 0.0).then_inc(zeroed, 1)
                for z in (*M.KA, *M.Q, M.mp):
                    dve.memset(z[:], 0.0)
                for v in M.V:
                    dve.memset(v[:, :, VC:VC + VW], 0.0)
                dve.wait_ge(ld, 16)
                dve.wait_ge(v_out, 1)

                def combine(b):
                    add = Link(dve, dve_add, b * 3)
                    for t in range(TB):
                        i = b * TB + t
                        if t == 0:
                            dve.wait_ge(gathered[b], 16 * TB)
                        ins = dve.tensor_scalar(weighed[:, t, :], M.h[:, bass.ds(i, 1), :].rearrange("p o e -> p (o e)"),
                                                M.gate[:, bass.ds(i, 1)], None, ALU.mult)
                    add(ins)
                    add(dve.tensor_tensor(weighed[:], weighed[:], M.mod[:, 0, bass.ds(b, 1), GB * P:(GB + 1) * P].to_broadcast([P, TB, P]),
                                          ALU.mult))
                    xb = M.x[:, bass.ds(b * TB, TB), :]
                    add(dve.tensor_tensor(xb, xb, weighed[:], ALU.add))
                    for t in range(TB):
                        i = b * TB + t
                        ins = dve.bn_stats(M.stats[:, bass.ds(i, 1), :].rearrange("p o e -> p (o e)"),
                                           M.x[:, bass.ds(i, 1), :].rearrange("p o e -> p (o e)"))
                    link = Link(dve, dve_ln, b * 7)
                    link(ins)
                    variance_and_mean(dve, link, M, bass.ds(b * TB, TB), var_ready)

                def normalise(m):
                    for t in range(4):
                        i = m * 4 + t
                        dve.tensor_scalar(xn[:, t, :], M.x[:, bass.ds(i, 1), :].rearrange("p o e -> p (o e)"), M.mean[:, bass.ds(i, 1)],
                                          M.rstd[:, bass.ds(i, 1)], ALU.subtract, ALU.mult).then_inc(xn_ready, 1)

                combine(0)
                dve.wait_ge(rstd_ready, 1)
                normalise(0)

                def half(b, j, m, first):
                    link = Link(dve, dve_step, m * 6)
                    dve.wait_ge(v_mm, m + 1)
                    if not first and j == 0:
                        dve.wait_ge(v_stored, b * 64)
                    dve.tensor_tensor(vout[:, 4 * j:4 * j + 4, :, 0:HD], psC[:].rearrange("p (t h d) -> p t h d", t=4, h=H),
                                      M.bv1[:].rearrange("p (h d) -> p h d", h=H).unsqueeze(1).to_broadcast([P, 4, H, HD]),
                                      ALU.add).then_inc(v_out, 1)
                    if not (isinstance(m, int) and m == 2 * B - 1):
                        if j == 1:
                            dve.wait_ge(rstd_ready, b + 2)
                        dve.wait_ge(xn_T, m + 1)
                        normalise(m + 1)
                    for qk in range(2):
                        u, a, s = psR[qk]
                        bu = 1 + 3 * qk
                        ra, rb = ras[qk], rbs[qk]
                        dve.wait_ge(u_mm, m * 2 + qk + 1)
                        dve.scalar_tensor_tensor(out=ra[:], in0=a[:], scalar=M.bcol1[:, bu + 1:bu + 2],
                                                 in1=rope[:, 0, j * 512:(j + 1) * 512], op0=ALU.add, op1=ALU.mult).then_inc(dve_step, 1)
                        link.n += 1
                        link(dve.scalar_tensor_tensor(out=rb[:], in0=s[:], scalar=M.bcol1[:, bu + 2:bu + 3],
                                                      in1=rope[:, 1, j * 512:(j + 1) * 512], op0=ALU.add, op1=ALU.mult))
                        link(dve.tensor_tensor(ra[:], ra[:], rb[:], ALU.add))
                        if not first:
                            dve.wait_ge(rest1, m * 2 - 1 + qk)
                        dve.scalar_tensor_tensor(out=full[:, qk, :], in0=u[:], scalar=M.bcol1[:, bu:bu + 1],
                                                 in1=ra[:], op0=ALU.add, op1=ALU.add).then_inc(full_ready, 1)
                    if j == 0 and b < B - 1:
                        combine(b + 1)

                def batch(b, first):
                    for j in range(2):
                        half(b, j, b * 2 + j, first and j == 0)

                for b in range(B):
                    batch(b, b == 0)

            @block.scalar
            def _(act):
                def project(m, b):
                    if not (isinstance(m, int) and m == 0):
                        act.wait_ge(u_mm, m * 2)
                    wait_apart(act, xn_T, m + 1)
                    act.activation(hT[:], psT[:], ACT.Identity, bias=M.modcol[:, 1, 0, bass.ds(b, 1)],
                                   scale=M.modcol[:, 1, 1, bass.ds(b, 1)]).then_inc(hT_ready, 1)
                    act.wait_ge(ct_mm, m + 1)
                    act.activation(ctT[:], psC[:], ACT.Identity, bias=M.bcol1[:, 0:1]).then_inc(ct_ready, 1)

                project(0, 0)

                def half(b, j, m, first):
                    if not (isinstance(m, int) and m == 2 * B - 1):
                        project(m + 1, b + j)
                    cols = slice(j * 512, (j + 1) * 512)
                    for qk in range(2):
                        act.wait_ge(full_ready, m * 2 + qk + 1)
                        if not first and j == 0:
                            act.wait_ge(qk_stored[qk], b * NPART * 16)
                        act.activation(parts[0][:, qk, cols], full[:, qk, :], ACT.Copy).then_inc(part1, 1)
                        act.wait_ge(rest1, m * 2 + qk + 1)
                        act.activation(parts[1][:, qk, cols], rest[:, qk, :], ACT.Copy).then_inc(part2, 1)

                def batch(b, first):
                    for j in range(2):
                        half(b, j, b * 2 + j, first and j == 0)

                ends_apart(act, batch)

            @block.tensor
            def _(pe):
                def half(b, j, m, first):
                    for t in range(4):
                        pe.wait_ge(xn_ready, m * 4 + t + 1)
                        if t == 0 and not first:
                            pe.wait_ge(hT_ready, m)
                        mm = pe.transpose(psT[:, t * P:(t + 1) * P], xn[:, t, :], M.ident[:])
                    mm.then_inc(xn_T, 1)
                    pe.wait_ge(hT_ready, m + 1)
                    if not first:
                        pe.wait_ge(v_out, m + 1)
                    pe.matmul(psC[:], M.wd1[:], hT[:], start=True, stop=True).then_inc(ct_mm, 1)
                    if not first:
                        pe.wait_ge(full_ready, m * 2 - 1)
                    pe.wait_ge(ct_ready, m + 1)
                    for k in range(3):
                        mm = pe.matmul(psR[0][k][:], M.wuq1[:, k * P:(k + 1) * P], ctT[:], start=True, stop=True)
                    mm.then_inc(u_mm, 1)
                    for t in range(4):
                        mm = pe.matmul(psC[:, t * P:(t + 1) * P], ctT[:, t * P:(t + 1) * P], M.wukv1[:, P:2 * P],
                                       start=True, stop=True)
                    mm.then_inc(v_mm, 1)
                    if not first:
                        pe.wait_ge(full_ready, m * 2)
                    for k in range(2):
                        pe.matmul(psR[1][1 + k][:], M.wkr1[:, k * P:(k + 1) * P], hT[:], start=True, stop=True)
                    pe.matmul(psR[1][0][:], M.wukv1[:, 0:P], ctT[:], start=True, stop=True).then_inc(u_mm, 1)

                halves(pe, half)


def phase_attention1(nc, D, M):
    with Names(nc, "at_") as n:
        group_in = [n.sem(f"group_in{i}") for i in range(2)]
        a_mm, a_max, m_split, m_T, mT_out = n.sem("a_mm"), n.sem("a_max"), n.sem("m_split"), n.sem("m_T"), n.sem("mT_out")
        m_stored, m_in = n.sem("m_stored"), [n.sem(f"m_in{i}") for i in range(2)]
        s_mm, exp_done, pv_done, acc_out = n.sem("s_mm"), n.sem("exp_done"), n.sem("pv_done"), n.sem("acc_out")
        dve_step = n.sem("dve_step")
        Q, K, KA, V, mp = M.Q, M.K, M.KA, M.V, M.mp
        pt = [n.sb(f"pt{i}", [P, QUAD, 512]) for i in range(2)]
        mx = n.sb("mx", [P, QUAD, 4])
        mr = n.sb("mr", [P, QUAD * 4])
        mT = n.sb("mT", [MROWS * QUAD * 4, P], BF16)
        psA = [n.ps(f"psA{i}", [P, L]) for i in range(2)]
        psS = [n.ps(f"psS{i}", [P, 512]) for i in range(3)]
        acc = n.ps("acc", [P, 512])

        def a_step(s):
            w = s % GSTEPS
            half, kk = w // KC, w % KC
            return (s // GSTEPS) % 2, half, [(kk // 2, 2 * (kk % 2) + t) for t in range(2)]

        def bank(s, h):
            return ((s % GSTEPS) * QUAD + h) % 3

        def last_use(s, h):
            k, in_group = (s % GSTEPS) * QUAD + h, GSTEPS * QUAD
            return next(d for d in range(1, 8) if (k - d) % in_group % 3 == k % 3)

        def known(i, s):
            return i * BODY + s if isinstance(i, int) else None

        def beyond(i, s, n):
            return known(i, s) is None or known(i, s) >= n

        def exists(i, s):
            return known(i, s) is None or known(i, s) < NSTEPS

        def unit(i, s):
            return i * (BODY // KC) + s // KC

        def group(i, s):
            return i * (BODY // GSTEPS) + s // GSTEPS

        def iterations(eng, body):
            body(0)
            with eng.Fori(1, NGRP // 2 - 1) as i:
                body(i)
            body(NGRP // 2 - 1)

        with nc.Block() as block:
            @block.sync
            def _(sp):
                def load(g, a):
                    if not (isinstance(g, int) and g < 2):
                        wait_apart(sp, pv_done, (g - 1) * GSTEPS)
                    for r in range(2):
                        for rows, dst in ((M.qk_rows[0], Q[a][:, r::2, :]), (M.qk_rows[1], KA[a]), (M.qk_rows[1], K[a])):
                            src = rows[bass.ds(g * QUAD, QUAD), :, :].rearrange("(p r) c t -> r c p t", r=2)[r]
                            sp.dma_start(dst[64 * r:64 * r + KROWS, :, :], src).then_inc(group_in[a], 16)
                    sp.dma_start(V[a][:, :, 0:VC], M.v_rows[bass.ds(g, 1), :, :, :].rearrange("o p t c -> (o p) t c")).then_inc(group_in[a], 16)

                def maxima(pair, a, half):
                    u = pair * 2 + half
                    wait_apart(sp, mT_out, u + 1)
                    sp.dma_start(M.m_rows[half], mT[:]).then_inc(m_stored, 16)
                    wait_apart(sp, m_stored, (u + 1) * 16, 16)
                    src = M.m_rows[half].rearrange("(c p r t) q -> r c p (t q)", c=MROWS, p=2, r=2)
                    for r in range(2):
                        sp.dma_start(Q[a][64 * r + KROWS:64 * r + KROWS + MROWS, r::2, half * 512:(half + 1) * 512],
                                     src[r]).then_inc(m_in[half], 16)
                    wait_apart(sp, m_in[half], pair * 32 + 32, 32)

                load(0, 0)

                def body(i):
                    for a in range(2):
                        g = i * 2 + a
                        if a == 0 and isinstance(i, int) and i == 0:
                            load(1, 1)
                            maxima(0, 0, 0)
                        elif not (isinstance(i, int) and i == NGRP // 2 - 1 and a == 1):
                            load(g + 1, 1 - a)
                        maxima(g, a, 1)
                        if not (isinstance(i, int) and i == NGRP // 2 - 1 and a == 1):
                            maxima(g + 1, 1 - a, 0)

                iterations(sp, body)

            @block.tensor
            def _(pe):
                def a_tile(i, s, t):
                    slot, half, tiles = a_step(s)
                    h, qt = tiles[t]
                    q0 = (half * 4 + qt) * P
                    if s % GSTEPS == 0 and t == 0:
                        pe.wait_ge(group_in[slot], (i + (s // GSTEPS) // 2) * 112 + 112)
                    if beyond(i, s, 1):
                        pe.wait_ge(a_max, i * (2 * BODY) + 2 * s + t - 1)
                    if t == 0 and s % KC == 1 and beyond(i, s, KC):
                        pe.wait_ge(mT_out, unit(i, s))
                    for c in range(2):
                        mm = pe.matmul(psA[t][:, c * 512:(c + 1) * 512], Q[slot][:, h, q0:q0 + P],
                                       KA[slot][:, h // 2, c * 512:(c + 1) * 512], start=True, stop=True)
                    mm.then_inc(a_mm, 1)

                def turn(i, s):
                    pe.wait_ge(m_split, unit(i, s))
                    pe.wait_ge(a_max, i * (2 * BODY) + 2 * s + (1 if exists(i, s) else 0))
                    pe.transpose(psA[0][:].bitcast(BF16)[:, 0:P], mp[:].rearrange("p c m -> p (c m)"),
                                 M.identb[:]).then_inc(m_T, 1)

                def scores(i, s, h):
                    slot, half, kc = (s // GSTEPS) % 2, (s % GSTEPS) // KC, s % KC
                    if kc == 0 and h == 0:
                        pe.wait_ge(m_in[half], group(i, s) * 32 + 32)
                    if known(i, s) is None or known(i, s) * QUAD + h >= 3:
                        pe.wait_ge(exp_done, i * (BODY * QUAD) + s * QUAD + h + 1 - last_use(s, h))
                    pe.matmul(psS[bank(s, h)][:], K[slot][:, h // 2, kc * P:(kc + 1) * P],
                              Q[slot][:, h, half * 512:(half + 1) * 512],
                              start=True, stop=True).then_inc(s_mm, 1)

                def values(i, s):
                    slot, kc = (s // GSTEPS) % 2, s % KC
                    pe.wait_ge(exp_done, i * (BODY * QUAD) + (s + 1) * QUAD)
                    if kc == 0 and beyond(i, s, 1):
                        pe.wait_ge(acc_out, unit(i, s))
                    for h in range(QUAD):
                        mm = pe.matmul(acc[VW * h:VW * (h + 1), :], V[slot][:, kc, h * (HD + 1):h * (HD + 1) + VW],
                                       pt[s % 2][:, h, :], start=(kc == 0), stop=(kc == KC - 1),
                                       tile_position=(0, VW * h), skip_group_check=True)
                    mm.then_inc(pv_done, 1)

                for s in range(AHEAD):
                    a_tile(0, s, 0)
                    a_tile(0, s, 1)
                    if s % KC == 0 and s > 0:
                        turn(0, s)

                def body(i):
                    for s in range(BODY):
                        more = exists(i, s + AHEAD)
                        if more:
                            a_tile(i, s + AHEAD, 0)
                        scores(i, s, 0)
                        scores(i, s, 1)
                        if more:
                            a_tile(i, s + AHEAD, 1)
                        scores(i, s, 2)
                        scores(i, s, 3)
                        if (s + AHEAD) % KC == 0 and (more or known(i, s + AHEAD) == NSTEPS):
                            turn(i, s + AHEAD)
                        if s > 0:
                            values(i, s - 1)
                        elif beyond(i, s, 1):
                            values(i - 1, BODY - 1)

                iterations(pe, body)
                values(NGRP // 2 - 1, BODY - 1)

            @block.vector
            def _(dve):
                def a_max_tile(i, s, t):
                    slot, half, tiles = a_step(s)
                    h, qt = tiles[t]
                    dve.wait_ge(a_mm, i * (2 * BODY) + 2 * s + t + 1)
                    if s % KC == 0 and t == 0 and beyond(i, s, 1):
                        dve.wait_ge(m_split, unit(i, s))
                    dve.tensor_reduce(mx[:, h, qt:qt + 1], psA[t][:], AX.X, ALU.max).then_inc(a_max, 1)

                def split(i, s):
                    link = Link(dve, dve_step, unit(i, s) * 4)
                    dve.wait_ge(a_max, i * (2 * BODY) + 2 * s + 2)
                    if beyond(i, s, KC):
                        dve.wait_ge(m_T, unit(i, s))
                    m = mx[:].rearrange("p h t -> p (h t)")
                    link(dve.tensor_scalar(mp[:, 0, :], m, -1.0, None, ALU.mult))
                    link(dve.scalar_tensor_tensor(out=mr[:], in0=m, scalar=-1.0, in1=mp[:, 0, :], op0=ALU.mult, op1=ALU.subtract))
                    link(dve.tensor_copy(mp[:, 1, :], mr[:]))
                    link(dve.tensor_tensor(mr[:], mr[:], mp[:, 1, :], ALU.subtract))
                    dve.tensor_copy(mp[:, 2, :], mr[:]).then_inc(m_split, 1)

                def turned(i, s):
                    dve.wait_ge(m_T, unit(i, s))
                    if beyond(i, s, 2 * KC):
                        dve.wait_ge(m_stored, i * (16 * BODY // KC) + (s // KC - 1) * 16)
                    dve.tensor_copy(mT[:], psA[0][:].bitcast(BF16)[0:MROWS * QUAD * 4, 0:P]).then_inc(mT_out, 1)

                def a_part(i, s):
                    if exists(i, s):
                        a_max_tile(i, s, 0)
                        a_max_tile(i, s, 1)
                    if s % KC == 0 and beyond(i, s, 1) and (known(i, s) is None or known(i, s) <= NSTEPS):
                        turned(i, s)
                    if s % KC == KC - 1 and exists(i, s):
                        split(i, s)

                for s in range(AHEAD):
                    a_part(0, s)

                def body(i):
                    for s in range(BODY):
                        a_part(i, s + AHEAD)

                iterations(dve, body)

            @block.scalar
            def _(act):
                def evacuate(u):
                    wait_apart(act, pv_done, (u + 1) * KC)
                    act.activation(M.attn[:, bass.ds(u, 1), :].rearrange("p o q -> p (o q)"), acc[:], ACT.Copy).then_inc(acc_out, 1)

                def body(i):
                    for s in range(BODY):
                        if beyond(i, s, 2):
                            act.wait_ge(pv_done, i * BODY + s - 1)
                        for h in range(QUAD):
                            act.wait_ge(s_mm, i * (BODY * QUAD) + s * QUAD + h + 1)
                            act.activation(pt[s % 2][:, h, :], psS[bank(s, h)][:], ACT.Exp,
                                           scale=INV_SCALE).then_inc(exp_done, 1)
                        if s % KC == 0 and beyond(i, s, 1):
                            evacuate(i * (BODY // KC) + s // KC - 1)

                iterations(act, body)
                evacuate(NSTEPS // KC - 1)


def phase_output1(nc, D, M):
    with Names(nc, "o1_") as n:
        num_T, ctx_ready, ctx_T, ctxT_ready = n.sem("num_T"), n.sem("ctx_ready"), n.sem("ctx_T"), n.sem("ctxT_ready")
        o_mm, added, wog_ready, pool_step, dve_step = n.sem("o_mm"), n.sem("added"), n.sem("wog_ready"), n.sem("pool_step"), n.sem("dve_step")
        bog_added = n.sem("bog_added")
        psN = [n.ps(f"psN{i}", [P, 512]) for i in range(3)]
        psC = [n.ps(f"psC{i}", [P, 512]) for i in range(2)]
        psO = [n.ps(f"psO{i}", [P, 512]) for i in range(2)]
        wog, bog = n.sb("wog", [P, B, P]), n.sb("bog", [P, B, P])
        rden = [n.sb(f"rden{i}", [P, H]) for i in range(2)]
        ctx = [n.sb(f"ctx{i}", [P, P]) for i in range(2)]
        ctxT = [n.sb(f"ctxT{i}", [P, P]) for i in range(2)]
        with nc.Block() as block:
            @block.gpsimd
            def _(pool):
                ga = M.mod[:, 1, :, GA * P:(GA + 1) * P]
                pool.tensor_tensor(wog[:], M.wo1[:].unsqueeze(1).to_broadcast([P, B, P]), ga, ALU.mult).then_inc(wog_ready, 1)
                pool.tensor_tensor(bog[:], M.bo1[:].unsqueeze(1).to_broadcast([P, B, P]), ga, ALU.mult).then_inc(pool_step, 1)
                pool.wait_ge(pool_step, 1)
                for b in range(B):
                    xb = M.x[:, b * TB:(b + 1) * TB, :]
                    pool.tensor_tensor(xb, xb, bog[:, b, :].unsqueeze(1).to_broadcast([P, TB, P]), ALU.add).then_inc(bog_added, 1)

            @block.tensor
            def _(pe):
                pe.wait_ge(wog_ready, 1)
                for k in range(NT + 2):
                    if k < NT:
                        b, half, qt = k // TB, (k % TB) // 4, k % 4
                        if k >= 3:
                            pe.wait_ge(ctx_ready, k - 2)
                        for quad in range(4):
                            u = (b * 4 + quad) * 2 + half
                            mm = pe.transpose(psN[k % 3][:, quad * P:(quad + 1) * P], M.attn[:, u, qt * P:(qt + 1) * P], M.ident[:])
                        mm.then_inc(num_T, 1)
                    if 1 <= k <= NT:
                        i = k - 1
                        pe.wait_ge(ctx_ready, i + 1)
                        if i >= 2:
                            pe.wait_ge(ctxT_ready, i - 1)
                        pe.transpose(psC[i % 2][:, 0:P], ctx[i % 2][:], M.ident[:]).then_inc(ctx_T, 1)
                    if k >= 2:
                        i = k - 2
                        pe.wait_ge(ctxT_ready, i + 1)
                        if i >= 2:
                            pe.wait_ge(added, i - 1)
                        pe.matmul(psO[i % 2][:, 0:P], ctxT[i % 2][:], wog[:, i // TB, :], start=True, stop=True).then_inc(o_mm, 1)

            @block.scalar
            def _(act):
                for i in range(NT):
                    act.wait_ge(ctx_T, i + 1)
                    if i >= 2:
                        act.wait_ge(o_mm, i - 1)
                    act.activation(ctxT[i % 2][:], psC[i % 2][:, 0:P], ACT.Copy).then_inc(ctxT_ready, 1)

            @block.vector
            def _(dve):
                def add(i):
                    dve.wait_ge(o_mm, i + 1)
                    dve.wait_ge(bog_added, i // TB + 1)
                    dve.tensor_tensor(M.x[:, i, :], M.x[:, i, :], psO[i % 2][:, 0:P], ALU.add).then_inc(added, 1)

                def stats(i):
                    dve.wait_ge(added, i + 1)
                    dve.bn_stats(M.stats[:, i, :], M.x[:, i, :])

                for k in range(NT + 3):
                    if k < NT:
                        dve.wait_ge(num_T, k + 1)
                        nd = psN[k % 3][:].rearrange("p (h c) -> p h c", c=VW)
                        if k >= 2:
                            dve.wait_ge(ctx_T, k - 1)
                            dve.wait_ge(ctx_ready, k - 1)
                        dve.reciprocal(rden[k % 2][:].unsqueeze(2), nd[:, :, HD:HD + 1]).then_inc(dve_step, 1)
                        dve.wait_ge(dve_step, k + 1)
                        dve.tensor_tensor(ctx[k % 2][:].rearrange("p (h d) -> p h d", h=H), nd[:, :, 0:HD],
                                          rden[k % 2][:].unsqueeze(2).to_broadcast([P, H, HD]), ALU.mult).then_inc(ctx_ready, 1)
                    if 2 <= k < NT + 2:
                        add(k - 2)
                    if k >= 3:
                        stats(k - 3)


def phase_experts1(nc, D, M):
    S = Steps(NS1, LAG_Y)
    U = S.UNROLL
    with Names(nc, "e1_") as n:
        loaded = [n.sem(f"loaded{i}") for i in range(2)]
        x_T, xT_ready, mm1_done, silu_done, g_ready = (n.sem("x_T"), n.sem("xT_ready"), n.sem("mm1_done"),
                                                       n.sem("silu_done"), n.sem("g_ready"))
        g_T, gT_ready, mm2_done, y_ready = n.sem("g_T"), n.sem("gT_ready"), n.sem("mm2_done"), n.sem("y_ready")
        stored = [n.sem(f"stored{i}") for i in range(2)]
        rows = [n.sb(f"rows{i}", [P, GT, P]) for i in range(2)]
        xT = [n.sb(f"xT{i}", [P, GT, P]) for i in range(2)]
        sg = [n.sb(f"sg{i}", [P, F1]) for i in range(2)]
        g = [n.sb(f"g{i}", [P, F1]) for i in range(RING)]
        gT = [n.sb(f"gT{i}", [P, P]) for i in range(RING)]
        y = [n.sb(f"y{i}", [P, GT, P]) for i in range(2)]
        psX = [n.ps(f"psX{i}", [P, 512]) for i in range(2)]
        ps1 = [n.ps(f"ps1{i}", [P, 512]) for i in range(2)]
        ps2 = [n.ps(f"ps2{i}", [P, 512]) for i in range(2)]
        psY = [n.ps(f"psY{i}", [P, 512]) for i in range(2)]
        src = M.sorted[1].rearrange("(s p) e -> p s e", p=P)
        dst = M.result[1].rearrange("(s p) e -> p s e", p=P)

        with nc.Block() as block:
            @block.sync
            def _(sp):
                move_tiles(sp, NS1, src, dst, rows, y, loaded, stored, x_T, y_ready)

            @block.tensor
            def _(pe):
                expert = Experts(nc, mybir.EngineType.PE, M, NS1, E1)

                def step(i, r):
                    k, gs = i * U + r, r // GT
                    expert.fetch(i, r)
                    if S.has(k) and r % GT == 0:
                        pe.wait_ge(loaded[gs], i * 16 + 16)
                        if after(k, U):
                            pe.wait_ge(xT_ready, i * 2 + gs - 1)
                        for t in range(GT):
                            mm = pe.transpose(psX[gs][:, t * P:(t + 1) * P], rows[gs][:, t, :], M.ident[:])
                        mm.then_inc(x_T, 1)
                    if S.has(k - 1):
                        j = (r - 1) % U
                        if j % GT == 0:
                            pe.wait_ge(xT_ready, i * 2 + (r - 1) // GT + 1)
                        if after(k - 1, 2):
                            pe.wait_ge(g_ready, k - 2)
                        pe.matmul(ps1[j % 2][:, 0:2 * F1], xT[j // GT][:, j % GT, :], M.wgu1[:, bass.ds(expert[r - 1], 1), :], start=True,
                                  stop=True).then_inc(mm1_done, 1)
                    if S.has(k - LAG_T):
                        j, q, o = k - LAG_T, (r - LAG_T) % 2, (r - LAG_T) % RING
                        pe.wait_ge(g_ready, j + 1)
                        if after(j, 2):
                            pe.wait_ge(gT_ready, j - 1)
                        pe.transpose(ps2[q][:, 0:P], g[o][:], M.ident[:]).then_inc(g_T, 1)
                    if S.has(k - LAG_Y):
                        j, q, o = k - LAG_Y, (r - LAG_Y) % 2, (r - LAG_Y) % RING
                        e = expert[r - LAG_Y]
                        pe.wait_ge(gT_ready, j + 1)
                        if after(j, 2):
                            pe.wait_ge(y_ready, j - 1)
                        pe.matmul(psY[q][:, 0:P], gT[o][:], M.wdn1[:, bass.ds(e, 1), :],
                                  start=True, stop=True).then_inc(mm2_done, 1)

                S.run(pe, step)

            @block.vector
            def _(dve):
                def step(i, r):
                    k, gs = i * U + r, r // GT
                    if S.has(k) and r % GT == 0:
                        dve.wait_ge(x_T, i * 2 + gs + 1)
                        if after(k, U):
                            dve.wait_ge(mm1_done, k - GT)
                        dve.tensor_copy(xT[gs][:].rearrange("p t e -> p (t e)"), psX[gs][:]).then_inc(xT_ready, 1)
                    if S.has(k - 1):
                        q = (r - 1) % 2
                        dve.wait_ge(silu_done, k)
                        if after(k - 1, RING):
                            dve.wait_ge(g_T, k - RING)
                        dve.tensor_tensor(g[(r - 1) % RING][:], ps1[q][:, F1:2 * F1], sg[q][:], ALU.mult).then_inc(g_ready, 1)
                    if S.has(k - LAG_Y):
                        j = (r - LAG_Y) % U
                        dve.wait_ge(mm2_done, k - LAG_Y + 1)
                        if after(k - LAG_Y, U) and j % GT == 0:
                            dve.wait_ge(stored[j // GT], (i if r >= LAG_Y else i - 1) * 16)
                        dve.tensor_copy(y[j // GT][:, j % GT, :], psY[j % 2][:, 0:P]).then_inc(y_ready, 1)

                S.run(dve, step)

            @block.scalar
            def _(act):
                def step(i, r):
                    k = i * U + r
                    if S.has(k - 1):
                        q = (r - 1) % 2
                        act.wait_ge(mm1_done, k)
                        if after(k - 1, 2):
                            act.wait_ge(g_ready, k - 2)
                        act.activation(sg[q][:], ps1[q][:, 0:F1], ACT.Silu).then_inc(silu_done, 1)
                    if S.has(k - LAG_T):
                        j, q, o = k - LAG_T, (r - LAG_T) % 2, (r - LAG_T) % RING
                        act.wait_ge(g_T, j + 1)
                        if after(j, RING):
                            act.wait_ge(mm2_done, j - RING + 1)
                        act.activation(gT[o][:], ps2[q][:, 0:P], ACT.Copy).then_inc(gT_ready, 1)

                S.run(act, step)


def phase_shared1(nc, D, M):
    NC = 2 * B
    with Names(nc, "s1_") as n:
        gathered = [n.sem(f"gathered{i}") for i in range(NC)]
        g_mm, u_mm, silu_done, m_ready = n.sem("g_mm"), n.sem("u_mm"), n.sem("silu_done"), n.sem("m_ready")
        d_mm, summed, scaled, x_done, stored = n.sem("d_mm"), n.sem("summed"), n.sem("scaled"), n.sem("x_done"), n.sem("stored")
        psG = [n.ps(f"psG{i}", [P, 512]) for i in range(2)]
        psU = [n.ps(f"psU{i}", [P, 512]) for i in range(2)]
        psD = [n.ps(f"psD{i}", [P, 512]) for i in range(2)]
        sg = [n.sb(f"sg{i}", [P, 512]) for i in range(2)]
        m = [n.sb(f"m{i}", [P, FCS, 512]) for i in range(2)]
        tot = [n.sb(f"tot{i}", [P, 4, P]) for i in range(2)]
        with nc.Block() as block:
            @block.gpsimd
            def _(pool):
                for i in range(NT):
                    pool.indirect_dma_start(
                        out=M.h[:, i, :], out_offset=None, in_=M.result[1][:, :],
                        in_offset=bass.IndirectOffsetOnAxis(ap=M.slot[:, i:i + 1], axis=0)).then_inc(gathered[i // 4], 16)
                for g in gathered:
                    pool.wait_ge(g, 64)

            @block.tensor
            def _(pe):
                def down(c):
                    if c >= 2:
                        pe.wait_ge(summed, c - 1)
                    for t in range(4):
                        for f in range(FCS):
                            pe.wait_ge(m_ready, c * FCS + f + 1)
                            mm = pe.matmul(psD[c % 2][:, t * P:(t + 1) * P], m[c % 2][:, f, t * P:(t + 1) * P],
                                           M.wsd1[:, f, :], start=(f == 0), stop=(f == FCS - 1))
                    mm.then_inc(d_mm, 1)

                for c in range(NC + 1):
                    if c < NC:
                        for f in range(FCS):
                            k = c * FCS + f
                            if k >= 2:
                                pe.wait_ge(m_ready, k - 1)
                            tok = M.hT[:, c * 512:(c + 1) * 512]
                            pe.matmul(psG[k % 2][:], M.wsg1[:, f * P:(f + 1) * P], tok, start=True, stop=True).then_inc(g_mm, 1)
                            pe.matmul(psU[k % 2][:], M.wsg1[:, FS + f * P:FS + (f + 1) * P], tok, start=True,
                                      stop=True).then_inc(u_mm, 1)
                    if c >= 1:
                        down(c - 1)

            @block.scalar
            def _(act):
                for k in range(NC * FCS):
                    act.wait_ge(g_mm, k + 1)
                    if k >= 2:
                        act.wait_ge(m_ready, k - 1)
                    act.activation(sg[k % 2][:], psG[k % 2][:], ACT.Silu).then_inc(silu_done, 1)

            @block.vector
            def _(dve):
                def finish(c):
                    b = c // 2
                    dve.wait_ge(d_mm, c + 1)
                    dve.wait_ge(gathered[c], 64)
                    if c >= 2:
                        dve.wait_ge(x_done, c - 1)
                    dve.tensor_tensor(tot[c % 2][:], psD[c % 2][:].rearrange("p (t e) -> p t e", t=4),
                                      M.h[:, 4 * c:4 * c + 4, :], ALU.add).then_inc(summed, 1)
                    dve.wait_ge(summed, c + 1)
                    gb = M.mod[:, 1, b, GB * P:(GB + 1) * P].unsqueeze(1).to_broadcast([P, 4, P])
                    dve.tensor_tensor(tot[c % 2][:], tot[c % 2][:], gb, ALU.mult).then_inc(scaled, 1)
                    dve.wait_ge(scaled, c + 1)
                    xc = M.x[:, 4 * c:4 * c + 4, :]
                    dve.tensor_tensor(xc, xc, tot[c % 2][:], ALU.add).then_inc(x_done, 1)

                for c in range(NC + 1):
                    if c < NC:
                        for f in range(FCS):
                            k = c * FCS + f
                            dve.wait_ge(u_mm, k + 1)
                            dve.wait_ge(silu_done, k + 1)
                            if c >= 2 and f == 0:
                                dve.wait_ge(d_mm, c - 1)
                            dve.tensor_tensor(m[c % 2][:, f, :], psU[k % 2][:], sg[k % 2][:], ALU.mult).then_inc(m_ready, 1)
                    if c >= 1:
                        finish(c - 1)

            @block.sync
            def _(sp):
                for c in range(NC):
                    sp.wait_ge(x_done, c + 1)
                    sp.dma_start(D["out"][c // 2].rearrange("(t p) e -> p t e", p=P)[:, 4 * (c % 2):4 * (c % 2) + 4, :],
                                 M.x[:, 4 * c:4 * c + 4, :]).then_inc(stored, 16)
                sp.wait_ge(stored, 16 * NC)


def program(nc, D, out, last=99):
    phases = iter(range(last))
    done = []

    def run(phase, *args):
        if next(phases, None) is not None:
            phase(nc, D, M, *args)
        done.append(phase)

    Names.start(nc)
    with Names(nc) as M:
        declare(nc, M)
        with Names(nc) as heads:
            declare_heads(M, heads)
            with Names(nc) as rows:
                M.h = rows.sb("h_l0", [P, NT, P])
                with Names(nc) as layer0:
                    declare_experts0(M, layer0)
                    run(phase_load)
                    run(phase_linear_attention)
                    with Names(nc) as turned:
                        M.hT = turned.sb("hT_l0", [P, NT * P])
                        run(phase_route, 0)
                    run(phase_experts0)
                run(phase_project1)
            with Names(nc) as attended:
                M.attn = attended.sb("attn", [P, NGRP * 2, 512])
                run(phase_attention1)
                run(phase_output1)
        with Names(nc) as layer1:
            declare_experts1(M, layer1)
            declare_rows(M, layer1, 1)
            D["out"] = out
            run(phase_route, 1)
            run(phase_experts1)
            run(phase_shared1)
        if last < 99:
            phase_store(nc, M, out)


def phase_store(nc, M, out):
    with Names(nc, "st_") as n:
        stored = n.sem("stored")
        with nc.Block() as block:
            @block.sync
            def _(sp):
                for b in range(B):
                    sp.dma_start(out[b].rearrange("(t p) e -> p t e", p=P),
                                 M.x[:, b * TB:(b + 1) * TB, :]).then_inc(stored, 16)
                sp.wait_ge(stored, 16 * B)


def declare(nc, M):
    M.x = M.sb("x", [P, NT, P])
    M.stats = M.sb("stats", [P, NT, 6])
    M.ln_d, M.ln_v = M.sb("ln_d", [P, NT]), M.sb("ln_v", [P, NT])
    M.mean, M.rstd, M.half = M.sb("mean", [P, NT]), M.sb("rstd", [P, NT]), M.sb("half", [P, NT])
    M.mod = M.sb("mod", [P, 2, B, 6 * P])
    M.modcol = M.sb("modcol", [P, 2, 2, B])
    M.gate, M.zeros = M.sb("gate", [P, NT]), M.sb("zeros", [P, P])
    M.slot, M.expert = M.sb("slot", [P, NT], I32), M.sb("expert", [1, NS1], I32)
    M.sorted = [nc.dram_tensor(f"sorted{l}", [s * P, P], F32).ap() for l, s in enumerate((NS0, NS1))]
    M.result = [nc.dram_tensor(f"result{l}", [s * P, P], F32).ap() for l, s in enumerate((NS0, NS1))]
    M.qk_rows = [nc.dram_tensor(f"{x}_rows", [B * H, KROWS, L], BF16).ap() for x in "qk"]
    M.v_rows = nc.dram_tensor("v_rows", [NGRP, P, KC, VC], F32).ap()
    M.m_rows = nc.dram_tensor("m_rows", [2, MROWS * QUAD * 4, P], BF16).ap()
    M.ident, M.identb = M.sb("ident", [P, P]), M.sb("identb", [P, P], BF16)
    M.wq0, M.wkv0, M.wo0 = M.sb("wq0", [P, P]), M.sb("wkv0", [P, 2 * P]), M.sb("wo0", [P, P])
    M.bq0, M.bkv0, M.bo0 = M.sb("bq0", [P, 1]), M.sb("bkv0", [P, 2 * P]), M.sb("bo0", [P, P])
    M.blockmask, M.headmask = M.sb("blockmask", [P, P]), M.sb("headmask", [P, H])
    M.tri, M.onesm = M.sb("tri", [P, P]), M.sb("onesm", [P, P])
    M.idents, M.tiles = M.sb("idents", [P, E1]), M.sb("tiles", [P, NS1])
    M.wr0, M.br0 = M.sb("wr0", [P, E0]), M.sb("br0", [P, E0])
    M.wd1, M.wuq1, M.wukv1, M.wkr1 = (M.sb("wd1", [P, 2 * DR]), M.sb("wuq1", [P, 3 * P]),
                                      M.sb("wukv1", [P, 2 * P]), M.sb("wkr1", [P, 2 * P]))
    M.bcol1, M.bv1 = M.sb("bcol1", [P, 8]), M.sb("bv1", [P, P])
    M.wo1, M.bo1 = M.sb("wo1", [P, P]), M.sb("bo1", [P, P])
    M.wr1 = M.sb("wr1", [P, E1])


def declare_experts0(M, n):
    M.w10, M.w20 = n.sb("w10", [P, E0, F0]), n.sb("w20", [P, E0, FC0, P])
    M.b10, M.b20 = n.sb("b10", [P, E0, F0]), n.sb("b20", [P, E0, P])


def declare_experts1(M, n):
    M.wgu1, M.wdn1 = n.sb("wgu1", [P, E1, 2 * F1]), n.sb("wdn1", [P, E1, P])
    M.wsg1, M.wsd1 = n.sb("wsg1", [P, 2 * FS]), n.sb("wsd1", [P, FCS, P])


def declare_rows(M, n, l):
    M.h, M.hT = n.sb(f"h_l{l}", [P, NT, P]), n.sb(f"hT_l{l}", [P, NT * P])


def rope_tables():
    ids = np.arange(P // 2, dtype=np.float32)
    theta = (np.float32(10000.0) ** (np.float32(-2.0) * ids)).astype(np.float32) / np.float32(P // 2)
    r = np.arange(L, dtype=np.float32)[:, None] * theta[None, :]
    cos, sin = np.cos(r), np.sin(r)
    both = np.empty((2, P, L), np.float32)
    both[0, 0::2], both[0, 1::2] = cos.T, cos.T
    both[1, 0::2], both[1, 1::2] = -sin.T, sin.T
    return both


def layout(a):
    row = lambda v: np.ascontiguousarray(v)
    swap = np.arange(P) ^ 1
    r = np.arange(P)
    return {
        "x": a["L0_attn_query"],
        "cT": np.stack([a["L0_c"].T, a["L1_c"].T], 1),
        "wmod": np.stack([a["L0_wmod"], a["L1_wmod"]], 1),
        "ident": np.eye(P, dtype=np.float32),
        "wq0": a["L0_attn_Wq"].T, "wkv0": np.concatenate([a["L0_attn_Wk"].T, a["L0_attn_Wv"].T], 1),
        "wo0": a["L0_attn_Wo"].T, "bq0": a["L0_attn_bq"][:, None],
        "bkv0": np.concatenate([a["L0_attn_bk"], a["L0_attn_bv"]]), "bo0": a["L0_attn_bo"],
        "blockmask": (r[:, None] // HD == r[None, :] // HD).astype(np.float32),
        "headmask": (r[:, None] // HD == np.arange(H)[None, :]).astype(np.float32),
        "tri": (r[:, None] < r[None, :]).astype(np.float32), "onesm": np.ones((P, P), np.float32),
        "idents": np.arange(E1, dtype=np.float32), "tiles": np.arange(NS1, dtype=np.float32),
        "wr0": a["L0_ffn_Wr"], "br0": a["L0_ffn_br"],
        "w10": a["L0_ffn_W1"].transpose(1, 0, 2),
        "w20": a["L0_ffn_W2"].reshape(E0, FC0, P, P).transpose(2, 0, 1, 3),
        "b10": a["L0_ffn_b1"], "b20": a["L0_ffn_b2"],
        "wd1": np.concatenate([a["L1_attn_Wd_q_w"], a["L1_attn_Wd_kv_w"]], 1),
        "wuq1": np.concatenate([np.concatenate([a["L1_attn_Wu_q_w"], a["L1_attn_Wq_r_w"], a["L1_attn_Wq_r_w"][:, swap]], 1),
                                np.zeros((DR, 3 * P), np.float32)], 0),
        "wukv1": np.concatenate([np.zeros((DR, 2 * P), np.float32),
                                 np.concatenate([a["L1_attn_Wu_k_w"], a["L1_attn_Wu_v_w"]], 1)], 0),
        "wkr1": np.concatenate([a["L1_attn_Wk_r_w"], a["L1_attn_Wk_r_w"][:, swap]], 1),
        "bcol1": np.stack([np.concatenate([a["L1_attn_Wd_q_b"], a["L1_attn_Wd_kv_b"]]),
                           a["L1_attn_Wu_q_b"], a["L1_attn_Wq_r_b"], a["L1_attn_Wq_r_b"][swap],
                           a["L1_attn_Wu_k_b"], a["L1_attn_Wk_r_b"], a["L1_attn_Wk_r_b"][swap],
                           np.zeros(P, np.float32)], 1),
        "bv1": a["L1_attn_Wu_v_b"], "wo1": a["L1_attn_Wo_w"], "bo1": a["L1_attn_Wo_b"],
        "wr1": a["L1_ffn_router_w"].T,
        "wgu1": a["L1_ffn_gate_up_proj"].transpose(1, 0, 2), "wdn1": a["L1_ffn_down_proj"].transpose(1, 0, 2),
        "wsg1": np.concatenate([a["L1_ffn_shared_gate_w"].T, a["L1_ffn_shared_up_w"].T], 1),
        "wsd1": a["L1_ffn_shared_down_w"].T.reshape(FCS, P, P).transpose(1, 0, 2),
        "rope": rope_tables().transpose(1, 0, 2),
    }


def kernel(**inputs):
    import concourse.bacc as bacc
    from concourse.bass_utils import run_bass_kernel_spmd

    nc = bacc.Bacc("TRN2", target_bir_lowering=False, num_devices=1)
    arrays, D = {}, {}
    for name, a in layout(inputs).items():
        arrays[f"in_{name}"] = np.ascontiguousarray(a)
        D[name] = nc.dram_tensor(f"in_{name}", list(a.shape), F32, kind="ExternalInput").ap()
    out = nc.dram_tensor("out_0", [B, L, P], F32, kind="ExternalOutput").ap()
    program(nc, D, out)
    return run_bass_kernel_spmd(nc, [arrays], core_ids=[0]).results[0]["out_0"]
```

```python
from contextlib import ExitStack

import concourse.bass as bass
import numpy as np
from concourse import mybir

F32, BF16, I32 = mybir.dt.float32, mybir.dt.bfloat16, mybir.dt.int32
ALU = mybir.AluOpType
ACT = mybir.ActivationFunctionType
AX = mybir.AxisListType

P = 128
B, L = 4, 1024
TB = L // P
NT = B * TB
H, HD = 16, 8
E0, F0 = 8, 512
E1, F1 = 16, 128
FS = 512
DR = 64
NS0 = NT + E0
NS1 = NT + E1
FC0 = F0 // P
FCS = FS // P
SA, CA, GA, SB, CB, GB = range(6)
LN_EPS = 1e-5
DEN_EPS = 1e-6
INV_SCALE = 1.0 / 12.0
NPART = 6
KROWS = NPART * HD
MROWS = 3
VW = 32


class Link:

    def __init__(self, eng, sem, base=0):
        self.eng, self.sem, self.base, self.n = eng, sem, base, 0

    def __call__(self, ins):
        self.n += 1
        ins.then_inc(self.sem, 1)
        self.eng.wait_ge(self.sem, self.base + self.n)


LASTING = 5


class Names:

    turn, halves, lasting = 0, (), ()

    @classmethod
    def start(cls, nc):
        free = list(nc.free_semaphores)
        cls.turn, cls.halves, cls.lasting = 0, (free[LASTING::2], free[LASTING + 1::2]), free[:LASTING]

    def __init__(self, nc, prefix=""):
        self.nc, self.prefix, self.ctx, self.sems = nc, prefix, ExitStack(), []
        if prefix:
            self.numbers = iter(Names.halves[Names.turn])
            Names.turn = 1 - Names.turn
        else:
            self.numbers = iter(Names.lasting)

    def __enter__(self):
        return self

    def __exit__(self, *a):
        if self.sems:
            self.nc.clear_and_free_semaphores(self.sems)
        return self.ctx.__exit__(*a)

    def sb(self, name, shape, dt=F32):
        return self.ctx.enter_context(self.nc.sbuf_tensor(self.prefix + name, shape, dt))

    def ps(self, name, shape, dt=F32):
        return self.ctx.enter_context(self.nc.psum_tensor(self.prefix + name, shape, dt))

    def sem(self, name):
        self.sems.append(self.nc.alloc_semaphore(self.prefix + name, next(self.numbers)))
        return self.sems[-1]


def wait_apart(eng, sem, value, least=1):
    value = value if isinstance(value, int) else eng.to_reg(value)
    eng.wait_ge(sem, least)
    eng.wait_ge(sem, value)


def batches(eng, n, body):
    body(0, True)
    with eng.Fori(1, n) as i:
        body(i, False)


def ends_apart(eng, body):
    body(0, True)
    with eng.Fori(1, B - 1) as b:
        body(b, False)
    body(B - 1, False)


def phase_load(nc, D, M):
    with Names(nc, "ld_") as n:
        ld_x, ld_w = [n.sem(f"ld_x{b}") for b in range(B)], n.sem("ld_w")
        ld_c = n.sem("ld_c")
        act_done, dve_step, sc_ready = n.sem("act_done"), n.sem("dve_step"), n.sem("sc_ready")
        mod_mm, mod_out = n.sem("mod_mm"), n.sem("mod_out")
        col_mm = n.sem("col_mm")
        wmod = [n.sb("wmod0", [P, 6 * P]), M.wmod1]
        cT = n.sb("cT", [P, 2, B])
        e = n.sb("sig_e", [P, 2, B])
        sc = n.sb("silu_c", [P, 2, B])
        scb = [n.sb("silu_c_bc", [P, B, P]), M.scb1]
        tmp = n.sb("tmp", [P, 2 * B, P])
        mod_ps = [n.ps(f"mod_ps{i}", [P, 1024]) for i in range(2)]
        col_ps = n.ps("col_ps", [P, 512])
        w_loads = [
            (M.ident, D["ident"]), (M.wq0, D["wq0"]), (M.wkv0, D["wkv0"]), (M.wo0, D["wo0"]),
            (M.bq0, D["bq0"]), (M.bkv0, D["bkv0"].partition_broadcast(P)), (M.bo0, D["bo0"].partition_broadcast(P)),
            (M.blockmask, D["blockmask"]), (M.headmask, D["headmask"]),
        ]
        with nc.Block() as block:
            @block.sync
            def _(sp):
                sp.dma_start(cT[:], D["cT"]).then_inc(ld_c, 16)
                for l in range(2):
                    sp.dma_start(wmod[l][:], D["wmod"][:, l, :]).then_inc(ld_c, 16)
                for b in range(B):
                    sp.dma_start(M.x[:, b * TB:(b + 1) * TB, :],
                                 D["x"][b].rearrange("(t p) e -> p t e", p=P)).then_inc(ld_x[b], 16)
                for dst, src in w_loads:
                    sp.dma_start(dst[:], src).then_inc(ld_w, 16)
                sp.wait_ge(ld_w, 16 * len(w_loads))

            @block.scalar
            def _(act):
                act.wait_ge(ld_c, 48)
                act.activation(e[:], cT[:], ACT.Exp, scale=-1.0).then_inc(act_done, 1)
                take_modulation(act, M, 0, mod_ps, mod_mm, mod_out)

            @block.tensor
            def _(pe):
                pe.wait_ge(sc_ready, 2)
                modulation(pe, scb[0], wmod[0], mod_ps, mod_mm, mod_out)
                for l in range(2):
                    for j in (SA, CA):
                        mm = pe.matmul(col_ps[:, (2 * l + j) * B:(2 * l + j + 1) * B],
                                       wmod[l][:, j * P:(j + 1) * P], sc[:, l, :], start=True, stop=True)
                mm.then_inc(col_mm, 1)

            @block.vector
            def _(dve):
                link = Link(dve, dve_step)
                dve.memset(M.zeros[:], 0.0)
                link(dve.memset(M.half[:], -0.5))
                dve.wait_ge(act_done, 1)
                link(dve.tensor_scalar(e[:], e[:], 1.0, None, ALU.add))
                link(dve.reciprocal(e[:], e[:]))
                link(dve.tensor_tensor(sc[:], cT[:], e[:], ALU.mult))
                for l in range(2):
                    dve.tensor_copy(scb[l][:], sc[:, l, :].unsqueeze(2).to_broadcast([P, B, P])).then_inc(sc_ready, 1)
                for b in range(B):
                    dve.wait_ge(ld_x[b], 16)
                    for t in range(b * TB, (b + 1) * TB):
                        dve.bn_stats(M.stats[:, t, :], M.x[:, t, :])
                dve.wait_ge(ld_w, 16 * len(w_loads))
                dve.tensor_copy(M.identb[:], M.ident[:])
                dve.wait_ge(col_mm, 1)
                link(dve.tensor_copy(M.modcol[:], col_ps[:, 0:4 * B].rearrange("p (l j b) -> p l j b", l=2, j=2)))
                link(dve.tensor_scalar(M.modcol[:, :, 1, :], M.modcol[:, :, 1, :], 1.0, None, ALU.add))
                dve.wait_ge(mod_out, B)
                cb = M.mod[:, 0, :, CB * P:(CB + 1) * P]
                link(dve.tensor_scalar(cb, cb, 1.0, None, ALU.add))
                bounded_gate(dve, link, M, tmp, 0, GA)


def modulation(pe, scb, wmod, mod_ps, mod_mm, mod_out):
    for b in range(B):
        if b >= len(mod_ps):
            pe.wait_ge(mod_out, b - len(mod_ps) + 1)
        for c0, c1 in ((0, 512), (512, 6 * P)):
            mm = pe.matmul(mod_ps[b % len(mod_ps)][:, c0:c1], scb[:, b, :], wmod[:, c0:c1], start=True, stop=True)
        mm.then_inc(mod_mm, 1)


def take_modulation(act, M, l, mod_ps, mod_mm, mod_out):
    for b in range(B):
        act.wait_ge(mod_mm, b + 1)
        act.activation(M.mod[:, l, b, :], mod_ps[b % len(mod_ps)][:, 0:6 * P], ACT.Copy).then_inc(mod_out, 1)


def bounded_gate(dve, link, M, tmp, l, g):
    gv, s, a = M.mod[:, l, :, g * P:(g + 1) * P], tmp[:, 0:B, :], tmp[:, B:2 * B, :]
    link(dve.tensor_scalar(s, gv, 0.0, 2.0, ALU.is_ge, ALU.mult))
    link(dve.tensor_scalar(a, gv, -1.0, None, ALU.mult))
    link(dve.tensor_tensor(a, a, gv, ALU.max))
    link(dve.tensor_scalar(a, a, 0.25, None, ALU.max))
    link(dve.scalar_tensor_tensor(out=gv, in0=s, scalar=-1.0, in1=a, op0=ALU.add, op1=ALU.mult))


def variance_and_mean(dve, link, M, tiles, var_ready):
    st, d, v, mean = M.stats[:, tiles, :], M.ln_d[:, tiles], M.ln_v[:, tiles], M.mean[:, tiles]
    link(dve.tensor_tensor(d, st[:, :, 1], st[:, :, 4], ALU.subtract))
    link(dve.scalar_tensor_tensor(out=v, in0=d, scalar=P / 4.0, in1=d, op0=ALU.mult, op1=ALU.mult))
    link(dve.tensor_tensor(v, v, st[:, :, 2], ALU.add))
    link(dve.tensor_tensor(v, v, st[:, :, 5], ALU.add))
    dve.tensor_scalar(v, v, 1.0 / P, LN_EPS, ALU.mult, ALU.add).then_inc(var_ready, 1)
    link(dve.tensor_tensor(mean, st[:, :, 1], st[:, :, 4], ALU.add))
    link(dve.tensor_scalar(mean, mean, 0.5, None, ALU.mult))


def mean_and_rstd(dve, pool, link, M, var_ready, rstd_ready):
    if dve is not None:
        variance_and_mean(dve, link, M, slice(0, NT), var_ready)
    if pool is not None:
        pool.wait_ge(var_ready, 1)
        for b in range(B):
            tiles = slice(b * TB, (b + 1) * TB)
            pool.tensor_tensor(M.rstd[:, tiles], M.ln_v[:, tiles], M.half[:, tiles], ALU.pow).then_inc(rstd_ready, 1)


def phase_linear_attention(nc, D, M):
    with Names(nc, "la_") as n:
        var_ready, rstd_ready = n.sem("var_ready"), n.sem("rstd_ready")
        dve_ln, dve_step = n.sem("dve_ln"), n.sem("dve_step")
        xn_ready, xn_T, hT_ready = n.sem("xn_ready"), n.sem("xn_T"), n.sem("hT_ready")
        kv_ones = n.sem("kv_ones")
        q_neg, k_neg = n.sem("q_neg"), n.sem("k_neg")
        q_mm, q_act, phiq_ready = n.sem("q_mm"), n.sem("q_act"), n.sem("phiq_ready")
        kv_mm, kv_bias, k_act, phik_ready = n.sem("kv_mm"), n.sem("kv_bias"), n.sem("k_act"), n.sem("phik_ready")
        s_mm, s_ready, num_mm, ctx_ready = n.sem("s_mm"), n.sem("s_ready"), n.sem("num_mm"), n.sem("ctx_ready")
        ctx_T, ctxT_ready, wog_ready, bog_added = n.sem("ctx_T"), n.sem("ctxT_ready"), n.sem("wog_ready"), n.sem("bog_added")
        pool_step, o_mm = n.sem("pool_step"), n.sem("o_mm")
        ld_later = n.sem("ld_later")
        psT = n.ps("psT", [P, L])
        psQ = n.ps("psQ", [P, L])
        psKV = n.ps("psKV", [P, 2 * L])
        xn = n.sb("xn", [P, TB, P])
        hT = n.sb("hT", [P, L])
        eq, phiq = n.sb("eq", [P, L]), n.sb("phiq", [P, L])
        ek, phik = n.sb("ek", [P, TB, P]), n.sb("phik", [P, TB, P])
        kvb = n.sb("kvb", [P, TB, 2 * P + 1])
        sm = n.sb("sm", [P, P + H])
        rden = n.sb("rden", [P, TB, H])
        ctx = n.sb("ctx", [P, TB, P])
        ctxT = n.sb("ctxT", [P, L])
        wog, bog = n.sb("wog", [P, P]), n.sb("bog", [P, P])
        NW = P + H
        TPK = 512 // NW
        groups = [(t, min(t + TPK, TB)) for t in range(0, TB, TPK)]

        def num_at(t):
            return psKV[:, (t // TPK) * 512 + (t % TPK) * NW:(t // TPK) * 512 + (t % TPK + 1) * NW]

        NG = len(groups)
        S_AT = NG * 512
        assert S_AT + P + 1 <= 2 * L
        later = [
            (M.tri, D["tri"]), (M.onesm, D["onesm"]), (M.idents, D["idents"].partition_broadcast(P)),
            (M.tiles, D["tiles"].partition_broadcast(P)),
            (M.wr0, D["wr0"]), (M.br0, D["br0"].partition_broadcast(P)),
            (M.w10, D["w10"]), (M.w20, D["w20"]),
            (M.b10, D["b10"].partition_broadcast(P)), (M.b20, D["b20"].partition_broadcast(P)),
            (M.wd1, D["wd1"]), (M.wuq1, D["wuq1"]), (M.wukv1, D["wukv1"]), (M.wkr1, D["wkr1"]),
            (M.bcol1, D["bcol1"]), (M.bv1, D["bv1"].partition_broadcast(P)),
            (M.wo1, D["wo1"]), (M.bo1, D["bo1"].partition_broadcast(P)),
            (M.wr1, D["wr1"]),
        ]

        with nc.Block() as block:
            @block.sync
            def _(sp):
                for dst, src in later:
                    sp.dma_start(dst[:], src).then_inc(ld_later, 16)
                for l, ns in enumerate((NS0, NS1)):
                    sp.dma_start(M.sorted[l].rearrange("(s p) e -> p s e", p=P),
                                 M.zeros[:].unsqueeze(1).to_broadcast([P, ns, P])).then_inc(ld_later, 16)
                sp.wait_ge(ld_later, 16 * (2 + len(later)))

            @block.gpsimd
            def _(pool):
                mean_and_rstd(None, pool, None, M, var_ready, rstd_ready)

                def batch(b, first):
                    if not first:
                        pool.wait_ge(o_mm, b * 2)
                        pool.wait_ge(bog_added, b)
                    ga = M.mod[:, 0, b, GA * P:(GA + 1) * P]
                    pool.tensor_tensor(bog[:], M.bo0[:], ga, ALU.mult).then_inc(pool_step, 1)
                    pool.tensor_tensor(wog[:], M.wo0[:], ga, ALU.mult).then_inc(wog_ready, 1)
                    pool.wait_ge(pool_step, b + 1)
                    pool.wait_ge(xn_ready, b * TB + TB)
                    xb = M.x[:, bass.ds(b * TB, TB), :]
                    pool.tensor_tensor(xb, xb, bog[:].unsqueeze(1).to_broadcast([P, TB, P]),
                                       ALU.add).then_inc(bog_added, 1)

                batches(pool, B, batch)

            @block.vector
            def _(dve):
                dve.memset(kvb[:, :, 2 * P:2 * P + 1], 1.0).then_inc(kv_ones, 1)
                mean_and_rstd(dve, None, Link(dve, dve_ln), M, var_ready, rstd_ready)

                def normalise(b):
                    dve.wait_ge(rstd_ready, b + 1)
                    if not (isinstance(b, int) and b == 0):
                        dve.wait_ge(xn_T, b * 2)
                    for t in range(TB):
                        i = b * TB + t
                        dve.tensor_scalar(xn[:, t, :], M.x[:, i, :], M.mean[:, bass.ds(i, 1)],
                                          M.rstd[:, bass.ds(i, 1)], ALU.subtract, ALU.mult).then_inc(xn_ready, 1)

                normalise(0)

                def batch(b, first):
                    link = Link(dve, dve_step, b * (2 * NG + 2))
                    if not first:
                        dve.wait_ge(num_mm, b * NG)
                    for j in range(2):
                        dve.wait_ge(q_mm, b * 2 + j + 1)
                        cols = slice(j * 512, (j + 1) * 512)
                        dve.tensor_scalar(eq[:, cols], psQ[:, cols], M.bq0[:, 0:1], 0.0, ALU.add,
                                          ALU.min).then_inc(q_neg, 1)
                    for j in range(4):
                        dve.wait_ge(kv_mm, b * 4 + j + 1)
                        dve.tensor_tensor(kvb[:, 2 * j:2 * j + 2, 0:2 * P],
                                          psKV[:, j * 512:(j + 1) * 512].rearrange("p (t f) -> p t f", t=2),
                                          M.bkv0[:].unsqueeze(1).to_broadcast([P, 2, 2 * P]),
                                          ALU.add).then_inc(kv_bias, 1)
                        if j % 2 == 1:
                            dve.wait_ge(kv_bias, b * 4 + j + 1)
                            half = slice(4 * (j // 2), 4 * (j // 2) + 4)
                            dve.tensor_scalar(ek[:, half, :], kvb[:, half, 0:P], 0.0, None, ALU.min).then_inc(k_neg, 1)
                    for j in range(2):
                        half = slice(4 * j, 4 * j + 4)
                        dve.wait_ge(k_act, b * 4 + 2 * j + 2)
                        dve.tensor_tensor(phik[:, half, :], ek[:, half, :], phik[:, half, :], ALU.add).then_inc(phik_ready, 1)
                        if j == 0:
                            dve.wait_ge(q_act, b * 2 + 2)
                            dve.tensor_tensor(phiq[:], eq[:], phiq[:], ALU.add).then_inc(phiq_ready, 1)
                    if not (isinstance(b, int) and b == B - 1):
                        normalise(b + 1)
                    dve.wait_ge(s_mm, b + 1)
                    dve.tensor_tensor(sm[:, 0:P], psKV[:, S_AT:S_AT + P], M.blockmask[:], ALU.mult).then_inc(s_ready, 1)
                    dve.tensor_scalar(sm[:, P:NW], M.headmask[:], psKV[:, S_AT + P:S_AT + P + 1], None, ALU.mult).then_inc(s_ready, 1)
                    for g, (t0, t1) in enumerate(groups):
                        dve.wait_ge(num_mm, b * NG + g + 1)
                        nd = psKV[:, g * 512:g * 512 + (t1 - t0) * NW].rearrange("p (t f) -> p t f", f=NW)
                        link(dve.tensor_scalar(rden[:, t0:t1, :], nd[:, :, P:NW], DEN_EPS, None, ALU.add))
                        link(dve.reciprocal(rden[:, t0:t1, :], rden[:, t0:t1, :]))
                        dve.tensor_tensor(ctx[:, t0:t1, :].rearrange("p t (h d) -> p t h d", h=H),
                                          nd[:, :, 0:P].rearrange("p t (h d) -> p t h d", h=H),
                                          rden[:, t0:t1, :].unsqueeze(3).to_broadcast([P, t1 - t0, H, HD]),
                                          ALU.mult).then_inc(ctx_ready, 1)
                    dve.wait_ge(bog_added, b + 1)
                    for j in range(2):
                        dve.wait_ge(o_mm, b * 2 + j + 1)
                        xj = M.x[:, bass.ds(b * TB + 4 * j, 4), :]
                        link(dve.tensor_tensor(xj, xj, psKV[:, j * 512:(j + 1) * 512].rearrange("p (t f) -> p t f", t=4),
                                               ALU.add))
                    for t in range(TB):
                        dve.bn_stats(M.stats[:, b * TB + t, :], M.x[:, b * TB + t, :])

                ends_apart(dve, batch)

            @block.scalar
            def _(act):
                def modulate(b):
                    if not (isinstance(b, int) and b == 0):
                        act.wait_ge(s_mm, b)
                    for j in range(2):
                        wait_apart(act, xn_T, b * 2 + j + 1)
                        act.activation(hT[:, j * 512:(j + 1) * 512], psT[:, j * 512:(j + 1) * 512], ACT.Identity,
                                       bias=M.modcol[:, 0, 0, bass.ds(b, 1)],
                                       scale=M.modcol[:, 0, 1, bass.ds(b, 1)]).then_inc(hT_ready, 1)

                modulate(0)

                def batch(b, first):
                    if not first:
                        act.wait_ge(num_mm, b * NG)
                    for j in range(2):
                        cols = slice(j * 512, (j + 1) * 512)
                        act.wait_ge(q_neg, b * 2 + j + 1)
                        act.activation(phiq[:, cols], psQ[:, cols], ACT.Relu, bias=M.bq0[:, 0:1])
                        act.activation(eq[:, cols], eq[:, cols], ACT.Exp).then_inc(q_act, 1)
                    for j in range(2):
                        half = slice(4 * j, 4 * j + 4)
                        act.wait_ge(kv_bias, b * 4 + 2 * j + 2)
                        act.activation(phik[:, half, :], kvb[:, half, 0:P], ACT.Relu).then_inc(k_act, 1)
                        act.wait_ge(k_neg, b * 2 + j + 1)
                        act.activation(ek[:, half, :], ek[:, half, :], ACT.Exp).then_inc(k_act, 1)
                    if not (isinstance(b, int) and b == B - 1):
                        modulate(b + 1)
                    for j in range(2):
                        act.wait_ge(ctx_T, b * 2 + j + 1)
                        act.activation(ctxT[:, j * 512:(j + 1) * 512], psQ[:, j * 512:(j + 1) * 512],
                                       ACT.Copy).then_inc(ctxT_ready, 1)

                ends_apart(act, batch)

            @block.tensor
            def _(pe):
                def turn(b):
                    for t in range(TB):
                        pe.wait_ge(xn_ready, b * TB + t + 1)
                        mm = pe.transpose(psT[:, t * P:(t + 1) * P], xn[:, t, :], M.ident[:])
                        if t % 4 == 3:
                            mm.then_inc(xn_T, 1)

                turn(0)

                def batch(b, first):
                    for j in range(2):
                        pe.wait_ge(hT_ready, b * 2 + j + 1)
                        cols = slice(j * 512, (j + 1) * 512)
                        pe.matmul(psQ[:, cols], M.wq0[:], hT[:, cols], start=True, stop=True).then_inc(q_mm, 1)
                    if not first:
                        pe.wait_ge(dve_step, b * (2 * NG + 2))
                    for t in range(TB):
                        mm = pe.matmul(psKV[:, t * 256:(t + 1) * 256], hT[:, t * P:(t + 1) * P], M.wkv0[:],
                                       start=True, stop=True)
                        if t % 2 == 1:
                            mm.then_inc(kv_mm, 1)
                    if first:
                        pe.wait_ge(kv_ones, 1)
                    for t in range(TB):
                        if t % 4 == 0:
                            pe.wait_ge(phik_ready, b * 2 + t // 4 + 1)
                        mm = pe.matmul(psKV[:, S_AT:S_AT + P + 1], phik[:, t, :], kvb[:, t, P:2 * P + 1],
                                       start=(t == 0), stop=(t == TB - 1))
                    mm.then_inc(s_mm, 1)
                    if not (isinstance(b, int) and b == B - 1):
                        turn(b + 1)
                    pe.wait_ge(phiq_ready, b + 1)
                    pe.wait_ge(s_ready, b * 2 + 2)
                    for g, (t0, t1) in enumerate(groups):
                        for t in range(t0, t1):
                            mm = pe.matmul(num_at(t), phiq[:, t * P:(t + 1) * P], sm[:], start=True, stop=True)
                        mm.then_inc(num_mm, 1)
                    for t in range(TB):
                        pe.wait_ge(ctx_ready, b * NG + t // TPK + 1)
                        mm = pe.transpose(psQ[:, t * P:(t + 1) * P], ctx[:, t, :], M.ident[:])
                        if t % 4 == 3:
                            mm.then_inc(ctx_T, 1)
                    pe.wait_ge(wog_ready, b + 1)
                    for t in range(TB):
                        pe.wait_ge(ctxT_ready, b * 2 + t // 4 + 1)
                        mm = pe.matmul(psKV[:, t * P:(t + 1) * P], ctxT[:, t * P:(t + 1) * P], wog[:],
                                       start=True, stop=True)
                        if t % 4 == 3:
                            mm.then_inc(o_mm, 1)

                ends_apart(pe, batch)


SHARED_EARLY = B


class SharedExpert:

    def __init__(self, n, M, chunks, psG, psU):
        self.M, self.chunks, self.psG, self.psU = M, list(chunks), psG, psU
        self.g_mm, self.u_mm, self.silu_done = n.sem("g_mm"), n.sem("u_mm"), n.sem("silu_done")
        self.m_ready, self.d_mm, self.scaled, self.x_added = n.sem("m_ready"), n.sem("d_mm"), n.sem("scaled"), n.sem("x_added")
        self.psD = [n.ps(f"psD{i}", [P, 512]) for i in range(2)]
        self.sg = [n.sb(f"sg{i}", [P, 512]) for i in range(2)]
        self.m = [n.sb(f"m{i}", [P, FCS, 512]) for i in range(2)]
        self.t = [n.sb(f"part{i}", [P, 4, P]) for i in range(2)]
        self.finished = 0

    def up(self, pe, i, f):
        M, c, k = self.M, self.chunks[i], i * FCS + f
        if k >= 2:
            pe.wait_ge(self.m_ready, k - 1)
        tok = M.hT[:, c * 512:(c + 1) * 512]
        pe.matmul(self.psG[k % 2][:, 0:512], M.wsg1[:, f * P:(f + 1) * P], tok, start=True, stop=True).then_inc(self.g_mm, 1)
        pe.matmul(self.psU[k % 2][:, 0:512], M.wsg1[:, FS + f * P:FS + (f + 1) * P], tok, start=True,
                  stop=True).then_inc(self.u_mm, 1)

    def down(self, pe, i):
        if i >= 2:
            pe.wait_ge(self.scaled, i - 1)
        for t in range(4):
            for f in range(FCS):
                pe.wait_ge(self.m_ready, i * FCS + f + 1)
                mm = pe.matmul(self.psD[i % 2][:, t * P:(t + 1) * P], self.m[i % 2][:, f, t * P:(t + 1) * P],
                               self.M.wsd1[:, f, :], start=(f == 0), stop=(f == FCS - 1))
        mm.then_inc(self.d_mm, 1)

    def silu(self, act):
        for k in range(len(self.chunks) * FCS):
            act.wait_ge(self.g_mm, k + 1)
            if k >= 2:
                act.wait_ge(self.m_ready, k - 1)
            act.activation(self.sg[k % 2][:], self.psG[k % 2][:, 0:512], ACT.Silu).then_inc(self.silu_done, 1)

    def gate(self, dve, i):
        for f in range(FCS):
            k = i * FCS + f
            dve.wait_ge(self.u_mm, k + 1)
            dve.wait_ge(self.silu_done, k + 1)
            if i >= 2 and f == 0:
                dve.wait_ge(self.d_mm, i - 1)
            dve.tensor_tensor(self.m[i % 2][:, f, :], self.psU[k % 2][:, 0:512], self.sg[k % 2][:], ALU.mult).then_inc(self.m_ready, 1)

    def finish(self, dve, i):
        M, c = self.M, self.chunks[i]
        dve.wait_ge(self.d_mm, i + 1)
        if i >= 2:
            dve.wait_ge(self.x_added, i - 1)
        gb = M.mod[:, 1, c // 2, GB * P:(GB + 1) * P].unsqueeze(1).to_broadcast([P, 4, P])
        dve.tensor_tensor(self.t[i % 2][:], self.psD[i % 2][:].rearrange("p (t e) -> p t e", t=4), gb, ALU.mult).then_inc(self.scaled, 1)
        dve.wait_ge(self.scaled, i + 1)
        xc = M.x[:, 4 * c:4 * c + 4, :]
        dve.tensor_tensor(xc, xc, self.t[i % 2][:], ALU.add).then_inc(self.x_added, 1)
        self.finished = i + 1


def phase_route(nc, D, M, l):
    E, NS, wr = ((E0, NS0, M.wr0), (E1, NS1, M.wr1))[l]
    with Names(nc, f"rt{l}_") as n:
        var_ready, rstd_ready = n.sem("var_ready"), n.sem("rstd_ready")
        dve_ln, dve_step = n.sem("dve_ln"), n.sem("dve_step")
        xn_ready, h_ready, h_T, hT_ready = n.sem("xn_ready"), n.sem("h_ready"), n.sem("h_T"), n.sem("hT_ready")
        lg_mm, lg_out, shifted, exp_done = n.sem("lg_mm"), n.sem("lg_out"), n.sem("shifted"), n.sem("exp_done")
        oh_ready, rank_mm, slot_ready, scattered = n.sem("oh_ready"), n.sem("rank_mm"), n.sem("slot_ready"), n.sem("scattered")
        dve_rt, half_done = n.sem("dve_rt"), n.sem("half_done")
        psT = [n.ps(f"psT{i}", [P, 512]) for i in range(2)]
        psL = n.ps("psL", [P, 512])
        psV = n.ps("psV", [P, 512])
        shared = SharedExpert(n, M, range(SHARED_EARLY), psT, [psV, psL]) if l == 1 else None
        psR, psN = n.ps("psR", [P, NT * E]), n.ps("psN", [P, NT * E])
        xn = n.sb("xn", [P, TB, P])
        lg, t1, oh = n.sb("lg", [P, NT, E]), n.sb("t1", [P, NT, E]), n.sb("oh", [P, NT, E])
        scan = [n.sb(f"scan{i}", [P, NT, E]) for i in range(2)]
        tot = n.sb("tot", [P, NT, E])
        r1 = n.sb("r1", [P, NT])
        cnt = [n.sb(f"cnt{i}", [P, E]) for i in range(3)]
        cnti = n.sb("cnti", [P, E], I32)
        cmp, cmps = n.sb("cmp", [1, NS, E]), n.sb("cmps", [1, NS])
        posf = n.sb("posf", [P, NT])
        if l == 0:
            tmp, mod_ps = n.sb("tmp", [P, 2 * B, P]), [n.ps("mod_ps", [P, 1024])]
            mod_mm, mod_out = n.sem("mod_mm"), n.sem("mod_out")

        def per_tile(v):
            return v.unsqueeze(2).to_broadcast([P, NT, E])

        def per_expert(v, k=NT):
            return v.unsqueeze(1).to_broadcast([v.shape[0], k, E])

        ld_experts = n.sem("ld_experts")

        with nc.Block() as block:
            @block.sync
            def _(sp):
                if l == 1:
                    for dst, name in ((M.wgu1, "wgu1"), (M.wdn1, "wdn1"), (M.wsg1, "wsg1"), (M.wsd1, "wsd1")):
                        sp.dma_start(dst[:], D[name]).then_inc(ld_experts, 16)
                    sp.wait_ge(ld_experts, 16 * 4)

            @block.vector
            def _(dve):
                mean_and_rstd(dve, None, Link(dve, dve_ln), M, var_ready, rstd_ready)

                def batch(b, first):
                    dve.wait_ge(rstd_ready, b + 1)
                    link = Link(dve, dve_step, b * (TB + 1))
                    for t in range(TB):
                        i = b * TB + t
                        ins = dve.tensor_scalar(xn[:, t, :], M.x[:, i, :], M.mean[:, bass.ds(i, 1)],
                                                M.rstd[:, bass.ds(i, 1)], ALU.subtract, ALU.mult)
                        ins.then_inc(dve_step, 1)
                        link.n += 1
                    dve.wait_ge(dve_step, link.base + link.n)
                    link(dve.tensor_tensor(xn[:], xn[:], M.mod[:, l, b, CB * P:(CB + 1) * P].unsqueeze(1).to_broadcast([P, TB, P]),
                                           ALU.mult))
                    dve.tensor_tensor(M.h[:, bass.ds(b * TB, TB), :], xn[:],
                                      M.mod[:, l, b, SB * P:(SB + 1) * P].unsqueeze(1).to_broadcast([P, TB, P]),
                                      ALU.add).then_inc(h_ready, 1)

                def batch_all(b, first):
                    if not first:
                        dve.wait_ge(h_ready, b)
                    batch(b, first)

                batches(dve, B, batch_all)
                dve.wait_ge(lg_mm, 1)
                src = psL[:, 0:NT * E].rearrange("p (t e) -> p t e", e=E)
                if l == 0:
                    dve.tensor_tensor(lg[:], src, per_expert(M.br0[:]), ALU.add).then_inc(lg_out, 1)
                else:
                    dve.tensor_copy(lg[:], src).then_inc(lg_out, 1)
                dve.wait_ge(lg_out, 1)
                link = Link(dve, dve_rt)
                link(dve.tensor_reduce(r1[:], lg[:], AX.X, ALU.max))
                if l == 0:
                    dve.tensor_tensor(t1[:], lg[:], per_tile(r1[:]), ALU.subtract).then_inc(shifted, 1)
                    dve.wait_ge(exp_done, 1)
                    link(dve.tensor_reduce(posf[:], t1[:], AX.X, ALU.add))
                    link(dve.tensor_reduce(r1[:], t1[:], AX.X, ALU.max))
                    link(dve.reciprocal(posf[:], posf[:]))
                    link(dve.tensor_tensor(M.gate[:], r1[:], posf[:], ALU.mult))
                    link(dve.tensor_tensor(oh[:], t1[:], per_tile(r1[:]), ALU.is_equal))
                else:
                    dve.tensor_scalar(posf[:], r1[:], -1.0, 88.0, ALU.mult, ALU.min).then_inc(shifted, 1)
                    dve.wait_ge(exp_done, 1)
                    link(dve.tensor_scalar(posf[:], posf[:], 1.0, None, ALU.add))
                    link(dve.reciprocal(M.gate[:], posf[:]))
                    link(dve.tensor_tensor(oh[:], lg[:], per_tile(r1[:]), ALU.is_equal))
                link(dve.scalar_tensor_tensor(out=t1[:], in0=oh[:], scalar=-64.0, in1=per_expert(M.idents[:, 0:E]),
                                              op0=ALU.mult, op1=ALU.add))
                link(dve.tensor_reduce(r1[:], t1[:], AX.X, ALU.min))
                dve.tensor_tensor(oh[:], t1[:], per_tile(r1[:]), ALU.is_equal).then_inc(oh_ready, 1)
                dve.wait_ge(rank_mm, 2)
                link(dve.tensor_copy(tot[:], psN[:].rearrange("p (t e) -> p t e", e=E)))
                src, d, k = tot, 1, 0
                while d < NT:
                    dst = scan[k % 2]
                    link(dve.tensor_copy(dst[:, 0:d, :], src[:, 0:d, :]))
                    link(dve.tensor_tensor(dst[:, d:NT, :], src[:, d:NT, :], src[:, 0:NT - d, :], ALU.add))
                    src, d, k = dst, 2 * d, k + 1
                link(dve.tensor_scalar(cnt[0][:], src[:, NT - 1, :], float(P - 1), None, ALU.add))
                link(dve.tensor_copy(cnti[:], cnt[0][:]))
                link(dve.tensor_scalar(cnti[:], cnti[:], P.bit_length() - 1, None, ALU.arith_shift_right))
                link(dve.tensor_copy(cnt[2][:], cnti[:]))
                ends, d, k = cnt[2], 1, 0
                while d < E:
                    dst = cnt[k % 2]
                    link(dve.tensor_copy(dst[:, 0:d], ends[:, 0:d]))
                    link(dve.tensor_tensor(dst[:, d:E], ends[:, d:E], ends[:, 0:E - d], ALU.add))
                    ends, d, k = dst, 2 * d, k + 1
                starts = cnt[k % 2]
                link(dve.tensor_tensor(starts[:], ends[:], cnt[2][:], ALU.subtract))
                link(dve.tensor_tensor(t1[:], src[:], tot[:], ALU.subtract))
                link(dve.scalar_tensor_tensor(out=t1[:], in0=per_expert(starts[:]), scalar=float(P), in1=t1[:],
                                              op0=ALU.mult, op1=ALU.add))
                link(dve.tensor_tensor(t1[:], t1[:], psR[:].rearrange("p (t e) -> p t e", e=E), ALU.add))
                link(dve.tensor_tensor(t1[:], t1[:], oh[:], ALU.mult))
                link(dve.tensor_reduce(posf[:], t1[:], AX.X, ALU.add))
                dve.tensor_copy(M.slot[:], posf[:]).then_inc(slot_ready, 1)
                link(dve.tensor_tensor(cmp[:], M.tiles[0:1, 0:NS].unsqueeze(2).to_broadcast([1, NS, E]),
                                       per_expert(ends[0:1, :], NS), ALU.is_ge))
                link(dve.tensor_reduce(cmps[:], cmp[:], AX.X, ALU.add))
                link(dve.tensor_scalar(cmps[:], cmps[:], float(E - 1), None, ALU.min))
                link(dve.tensor_copy(M.expert[:, 0:NS], cmps[:]))
                if l == 0:
                    clear_heads(dve, M)
                    bounded_gate(dve, link, M, tmp, 0, GB)
                    dve.wait_ge(mod_out, B)
                    cb = M.mod[:, 1, :, CB * P:(CB + 1) * P]
                    link(dve.tensor_scalar(cb, cb, 1.0, None, ALU.add))
                    bounded_gate(dve, link, M, tmp, 1, GA)
                    bounded_gate(dve, link, M, tmp, 1, GB)
                if shared:
                    for i in range(SHARED_EARLY + 1):
                        if i < SHARED_EARLY:
                            shared.gate(dve, i)
                        if i >= 1:
                            shared.finish(dve, i - 1)

            @block.gpsimd
            def _(pool):
                mean_and_rstd(None, pool, None, M, var_ready, rstd_ready)
                pool.wait_ge(slot_ready, 1)
                if l == 1:
                    pool.wait_ge(half_done, NT)
                for i in range(NT):
                    pool.indirect_dma_start(
                        out=M.sorted[l][:, :], out_offset=bass.IndirectOffsetOnAxis(ap=M.slot[:, i:i + 1], axis=0),
                        in_=M.h[:, i, :], in_offset=None).then_inc(scattered, 16)
                pool.wait_ge(scattered, 16 * NT)

            @block.tensor
            def _(pe):
                for b in range(B):
                    pe.wait_ge(h_ready, b + 1)
                    for j in range(2):
                        if b >= 1:
                            pe.wait_ge(hT_ready, 2 * (b - 1) + j + 1)
                        for t in range(4):
                            mm = pe.transpose(psT[j][:, t * P:(t + 1) * P], M.h[:, b * TB + 4 * j + t, :], M.ident[:])
                        mm.then_inc(h_T, 1)
                    for t in range(TB):
                        pe.wait_ge(hT_ready, 2 * b + t // 4 + 1)
                        i = b * TB + t
                        mm = pe.matmul(psL[:, i * E:(i + 1) * E], M.hT[:, i * P:(i + 1) * P], wr[:],
                                       start=True, stop=True)
                mm.then_inc(lg_mm, 1)
                if shared:
                    pe.wait_ge(ld_experts, 16 * 4)
                    shared.up(pe, 0, 0)
                pe.wait_ge(oh_ready, 1)
                flat = oh[:].rearrange("p t e -> p (t e)")
                pe.matmul(psR[:], M.tri[:], flat, start=True, stop=True).then_inc(rank_mm, 1)
                pe.matmul(psN[:], M.onesm[:], flat, start=True, stop=True).then_inc(rank_mm, 1)
                if l == 0:
                    modulation(pe, M.scb1, M.wmod1, mod_ps, mod_mm, mod_out)
                if shared:
                    for i in range(SHARED_EARLY + 1):
                        if i < SHARED_EARLY:
                            for f in range(1 if i == 0 else 0, FCS):
                                shared.up(pe, i, f)
                        if i >= 1:
                            shared.down(pe, i - 1)

            @block.scalar
            def _(act):
                for b in range(B):
                    for j in range(2):
                        act.wait_ge(h_T, 2 * b + j + 1)
                        c = (2 * b + j) * 512
                        act.activation(M.hT[:, c:c + 512], psT[j][:], ACT.Copy).then_inc(hT_ready, 1)
                act.wait_ge(shifted, 1)
                v = t1 if l == 0 else posf
                act.activation(v[:], v[:], ACT.Exp).then_inc(exp_done, 1)
                if l == 0:
                    take_modulation(act, M, 1, mod_ps, mod_mm, mod_out)
                if shared:
                    act.wait_ge(oh_ready, 1)
                    act.wait_ge(h_T, 2 * B)
                    for i in range(NT):
                        act.activation(M.h[:, i, :], M.h[:, i, :], ACT.Copy, scale=M.gate[:, i:i + 1]).then_inc(half_done, 1)
                    shared.silu(act)


class Steps:

    UNROLL = 8

    def __init__(self, n, lag):
        assert n % self.UNROLL == 0
        self.n, self.lag = n, lag

    def run(self, eng, step):
        for r in range(self.UNROLL):
            step(0, r)
        with eng.Fori(1, self.n // self.UNROLL) as i:
            for r in range(self.UNROLL):
                step(i, r)
        for r in range(self.lag):
            step(self.n // self.UNROLL, r)

    def has(self, j):
        return not isinstance(j, int) or 0 <= j < self.n


def after(j, k):
    return not isinstance(j, int) or j >= k


GT = 4
LAG_T, LAG_Y = 3, 4
RING = 4


class Experts:

    def __init__(self, nc, kind, M, n, E):
        self.nc, self.kind, self.M, self.n, self.E, self.known = nc, kind, M, n, E, {}

    def fetch(self, i, r):
        first = {0: -4, 1: 0, 5: 4}.get(r)
        if first is None or (isinstance(i, int) and not 0 <= i * Steps.UNROLL + first < self.n):
            return
        _, values = self.nc.values_load_multi_w_load_instructions(
            self.M.expert[0:1, bass.ds(i * Steps.UNROLL + first, 4)], engines=[self.kind],
            min_val=0, max_val=self.E - 1,
            skip_runtime_bounds_check_because="routing clamps them on chip: counts of experts, at most E - 1")
        for t in range(4):
            self.known[first + t] = values[t]

    def __getitem__(self, offset):
        return self.known[offset]


def move_tiles(sp, n, src, dst, rows, y, loaded, stored, x_T, y_ready):
    ng = n // GT

    def group(g, q):
        if not isinstance(g, int) or g < ng:
            if not isinstance(g, int) or g >= 2:
                wait_apart(sp, x_T, g - 1)
            sp.dma_start(rows[q][:], src[:, bass.ds(g * GT, GT), :]).then_inc(loaded[q], 16)
        if not isinstance(g, int) or g >= 2:
            wait_apart(sp, y_ready, (g - 1) * GT)
            sp.dma_start(dst[:, bass.ds((g - 2) * GT, GT), :], y[q][:]).then_inc(stored[q], 16)

    for q in range(2):
        group(q, q)
    with sp.Fori(1, ng // 2) as i:
        for q in range(2):
            group(i * 2 + q, q)
    for q in range(2):
        group(ng + q, q)
    for q in range(2):
        sp.wait_ge(stored[q], 16 * (ng // 2))


def phase_experts0(nc, D, M):
    S = Steps(NS0, LAG_Y)
    U = S.UNROLL
    with Names(nc, "e0_") as n:
        loaded = [n.sem(f"loaded{i}") for i in range(2)]
        x_T, xT_ready, mm1_done, h1_ready = n.sem("x_T"), n.sem("xT_ready"), n.sem("mm1_done"), n.sem("h1_ready")
        h1_T, h1T_ready, mm2_done, y_ready = n.sem("h1_T"), n.sem("h1T_ready"), n.sem("mm2_done"), n.sem("y_ready")
        stored = [n.sem(f"stored{i}") for i in range(2)]
        rows = [n.sb(f"rows{i}", [P, GT, P]) for i in range(2)]
        xT = [n.sb(f"xT{i}", [P, GT, P]) for i in range(2)]
        h1 = [n.sb(f"h1_{i}", [P, F0]) for i in range(RING)]
        h1T = [n.sb(f"h1T{i}", [P, FC0, P]) for i in range(RING)]
        y = [n.sb(f"y{i}", [P, GT, P]) for i in range(2)]
        psX = [n.ps(f"psX{i}", [P, 512]) for i in range(2)]
        ps1 = [n.ps(f"ps1{i}", [P, 512]) for i in range(2)]
        ps2 = [n.ps(f"ps2{i}", [P, 512]) for i in range(2)]
        psY = [n.ps(f"psY{i}", [P, 512]) for i in range(2)]
        src = M.sorted[0].rearrange("(s p) e -> p s e", p=P)
        dst = M.result[0].rearrange("(s p) e -> p s e", p=P)

        with nc.Block() as block:
            @block.sync
            def _(sp):
                move_tiles(sp, NS0, src, dst, rows, y, loaded, stored, x_T, y_ready)

            @block.tensor
            def _(pe):
                expert = Experts(nc, mybir.EngineType.PE, M, NS0, E0)

                def step(i, r):
                    k, gs = i * U + r, r // GT
                    expert.fetch(i, r)
                    if S.has(k) and r % GT == 0:
                        pe.wait_ge(loaded[gs], i * 16 + 16)
                        if after(k, U):
                            pe.wait_ge(xT_ready, i * 2 + gs - 1)
                        for t in range(GT):
                            mm = pe.transpose(psX[gs][:, t * P:(t + 1) * P], rows[gs][:, t, :], M.ident[:])
                        mm.then_inc(x_T, 1)
                    if S.has(k - 1):
                        j = (r - 1) % U
                        if j % GT == 0:
                            pe.wait_ge(xT_ready, i * 2 + (r - 1) // GT + 1)
                        if after(k - 1, 2):
                            pe.wait_ge(h1_ready, k - 2)
                        pe.matmul(ps1[j % 2][:], xT[j // GT][:, j % GT, :], M.w10[:, bass.ds(expert[r - 1], 1), :], start=True,
                                  stop=True).then_inc(mm1_done, 1)
                    if S.has(k - LAG_T):
                        j, q, o = k - LAG_T, (r - LAG_T) % 2, (r - LAG_T) % RING
                        pe.wait_ge(h1_ready, j + 1)
                        if after(j, 2):
                            pe.wait_ge(h1T_ready, j - 1)
                        for c in range(FC0):
                            mm = pe.transpose(ps2[q][:, c * P:(c + 1) * P], h1[o][:, c * P:(c + 1) * P], M.ident[:])
                        mm.then_inc(h1_T, 1)
                    if S.has(k - LAG_Y):
                        j, q, o = k - LAG_Y, (r - LAG_Y) % 2, (r - LAG_Y) % RING
                        e = expert[r - LAG_Y]
                        pe.wait_ge(h1T_ready, j + 1)
                        if after(j, 2):
                            pe.wait_ge(y_ready, j - 1)
                        for c in range(FC0):
                            mm = pe.matmul(psY[q][:, 0:P], h1T[o][:, c, :], M.w20[:, bass.ds(e, 1), c, :],
                                           start=(c == 0), stop=(c == FC0 - 1))
                        mm.then_inc(mm2_done, 1)

                S.run(pe, step)

            @block.vector
            def _(dve):
                expert = Experts(nc, mybir.EngineType.DVE, M, NS0, E0)

                def step(i, r):
                    k = i * U + r
                    expert.fetch(i, r)
                    if S.has(k - 1):
                        q, e = (r - 1) % 2, expert[r - 1]
                        dve.wait_ge(mm1_done, k)
                        if after(k - 1, RING):
                            dve.wait_ge(h1_T, k - RING)
                        dve.tensor_tensor(h1[(r - 1) % RING][:], ps1[q][:], M.b10[:, bass.ds(e, 1), :].rearrange("p o f -> p (o f)"),
                                          ALU.add).then_inc(h1_ready, 1)
                    if S.has(k - LAG_Y):
                        j = (r - LAG_Y) % U
                        e = expert[r - LAG_Y]
                        dve.wait_ge(mm2_done, k - LAG_Y + 1)
                        if after(k - LAG_Y, U) and j % GT == 0:
                            dve.wait_ge(stored[j // GT], (i if r >= LAG_Y else i - 1) * 16)
                        dve.tensor_tensor(y[j // GT][:, j % GT, :], psY[j % 2][:, 0:P],
                                          M.b20[:, bass.ds(e, 1), :].rearrange("p o f -> p (o f)"),
                                          ALU.add).then_inc(y_ready, 1)

                S.run(dve, step)

            @block.scalar
            def _(act):
                def step(i, r):
                    k, gs = i * U + r, r // GT
                    if S.has(k) and r % GT == 0:
                        act.wait_ge(x_T, i * 2 + gs + 1)
                        if after(k, U):
                            act.wait_ge(mm1_done, k - GT)
                        act.activation(xT[gs][:].rearrange("p t e -> p (t e)"), psX[gs][:], ACT.Copy).then_inc(xT_ready, 1)
                    if S.has(k - LAG_T):
                        j, q, o = k - LAG_T, (r - LAG_T) % 2, (r - LAG_T) % RING
                        act.wait_ge(h1_T, j + 1)
                        if after(j, RING):
                            act.wait_ge(mm2_done, j - RING + 1)
                        act.activation(h1T[o][:].rearrange("p c t -> p (c t)"), ps2[q][:], ACT.Relu).then_inc(h1T_ready, 1)

                S.run(act, step)


QUAD = 4
NGRP = B * H // QUAD
KC = L // P
GSTEPS = 2 * KC
BODY = 2 * GSTEPS
AHEAD = 12
NSTEPS = NGRP * GSTEPS
VC = QUAD * (HD + 1)


STORES = (3, 4)


def clear_heads(eng, M):
    for z in (*M.Q, *M.K, *M.KA, M.mp):
        eng.memset(z[:], 0.0)
    for v in M.V:
        eng.memset(v[:, :, VC:VC + VW], 0.0)


def load_group(sp, M, g, a):
    for r in range(2):
        for rows, dst in ((M.qk_rows[0], M.Q[a][:, r::2, :]), (M.qk_rows[1], M.KA[a]), (M.qk_rows[1], M.K[a])):
            src = rows[bass.ds(g * QUAD, QUAD), :, :].rearrange("(p r) c t -> r c p t", r=2)[r]
            sp.dma_start(dst[64 * r:64 * r + KROWS, :, :], src).then_inc(M.group_in[a], 16)
    sp.dma_start(M.V[a][:, :, 0:VC], M.v_rows[bass.ds(g, 1), :, :, :].rearrange("o p t c -> (o p) t c")).then_inc(M.group_in[a], 16)


def declare_heads(M, n):
    M.Q = [n.sb(f"Q{i}", [P, QUAD, L], BF16) for i in range(2)]
    M.K = [n.sb(f"K{i}", [P, 2, L], BF16) for i in range(2)]
    M.KA = [n.sb(f"KA{i}", [P, 2, L], BF16) for i in range(2)]
    M.V = [n.sb(f"V{i}", [P, KC, VC + VW], F32) for i in range(2)]
    M.mx = [n.sb(f"mx{i}", [P, QUAD, 4]) for i in range(2)]
    M.mr = n.sb("mr", [P, QUAD * 4])
    M.mp = n.sb("mp", [P, P // (QUAD * 4), QUAD * 4], BF16)


def phase_project1(nc, D, M):
    with Names(nc, "p1_") as n:
        ld = n.sem("ld_rope")
        var_ready, rstd_ready = n.sem("var_ready"), n.sem("rstd_ready")
        dve_ln, dve_step, dve_add = n.sem("dve_ln"), n.sem("dve_step"), n.sem("dve_add")
        gathered = [n.sem(f"gathered{i}") for i in range(B)]
        weighed = n.sb("weighed", [P, TB, P])
        xn_ready, xn_T, hT_ready = n.sem("xn_ready"), n.sem("xn_T"), n.sem("hT_ready")
        ct_mm, ct_ready, u_mm = n.sem("ct_mm"), n.sem("ct_ready"), n.sem("u_mm")
        v_mm, v_out, full_ready, part1, rest1, part2, part3 = (n.sem("v_mm"), n.sem("v_out"), n.sem("full_ready"),
            n.sem("part1"), n.sem("rest1"), n.sem("part2"), n.sem("part3"))
        qk_stored, v_stored = M.qk_stored, M.v_stored
        ones_set, ld_ones = n.sem("ones_set"), n.sem("ld_ones")
        rope = n.sb("rope", [P, 2, L])
        ones = n.sb("ones", [MROWS, L], BF16)
        xn = n.sb("xn", [P, 4, P])
        hT, ctT = n.sb("hT", [P, 512]), n.sb("ctT", [P, 512])
        ras = [n.sb(f"ra{i}", [P, 512]) for i in range(2)]
        rbs = [n.sb(f"rb{i}", [P, 512]) for i in range(2)]
        full, rest = n.sb("full", [P, 2, 512]), n.sb("rest", [P, 2, 512])
        parts = [n.sb(f"part{i}", [P, 2, L], BF16) for i in range(3)]
        vout = n.sb("vout", [P, TB, H, HD + 1])
        psT, psC = n.ps("psT", [P, 512]), n.ps("psC", [P, 512])
        psR = [[n.ps(f"psR{i}_{j}", [P, 512]) for j in range(3)] for i in range(2)]
        RUNS = (((0, 0, 1, 3), (1, 3, 1, 2), (2, 5, 1, 1)),
                ((0, 0, 3, 2), (0, 5, 1, 1), (1, 1, 3, 2), (2, 2, 1, 1)))

        def halves(eng, body):
            def batch(b, first):
                for j in range(2):
                    body(b, j, b * 2 + j, first and j == 0)
            batches(eng, B, batch)

        with nc.Block() as block:
            @block.sync
            def _(sp):
                sp.dma_start(rope[:], D["rope"]).then_inc(ld, 16)
                sp.wait_ge(ones_set, 1)
                for k in M.K:
                    for r in range(2):
                        for p in range(2):
                            sp.dma_start(k[64 * r + KROWS:64 * r + KROWS + MROWS, p, :], ones[0:MROWS, :]).then_inc(ld_ones, 16)
                sp.wait_ge(ld_ones, 16 * 8)

                def batch(b, first):
                    if isinstance(b, int) and b == B - 1:
                        for qk in range(2):
                            sp.wait_ge(qk_stored[qk], 16 * STORES[qk] * b)
                        sp.wait_ge(v_stored, 16 * 4 * b)
                        for a in range(2):
                            load_group(sp, M, a, a)
                    wait_apart(sp, v_out, b * 2 + 3)
                    for q in range(4):
                        sp.dma_start(M.v_rows[bass.ds(b * 4 + q, 1), :, :, :].rearrange("o p t c -> (o p) t c"),
                                     vout[:, :, 4 * q:4 * q + 4, :].rearrange("p t h c -> p t (h c)")).then_inc(v_stored, 16)
                    for qk in range(2):
                        wait_apart(sp, part3, b * 4 + 3 + qk)
                        blocks = M.qk_rows[qk][bass.ds(b * H, H), :, :].rearrange("h (d c) t -> (h d) c t", d=HD)
                        for part, c0, step, count in RUNS[qk]:
                            sp.dma_start(blocks[:, c0:c0 + step * (count - 1) + 1:step, :],
                                         parts[part][:, qk, :].unsqueeze(1).to_broadcast([P, count, L])).then_inc(qk_stored[qk], 16)

                ends_apart(sp, batch)

            @block.gpsimd
            def _(pool):
                def gather(b):
                    for i in range(b * TB, (b + 1) * TB):
                        pool.indirect_dma_start(
                            out=M.h[:, i, :], out_offset=None, in_=M.result[0][:, :],
                            in_offset=bass.IndirectOffsetOnAxis(ap=M.slot[:, i:i + 1], axis=0)).then_inc(gathered[b], 16)

                def rstd(b):
                    pool.wait_ge(var_ready, b + 1)
                    tiles = bass.ds(b * TB, TB)
                    pool.tensor_tensor(M.rstd[:, tiles], M.ln_v[:, tiles], M.half[:, 0:TB], ALU.pow).then_inc(rstd_ready, 1)

                gather(0)
                rstd(0)
                gather(1)
                gather(2)

                def half(b, j, m, first):
                    cols = slice(j * 512, (j + 1) * 512)
                    for qk in range(2):
                        pool.wait_ge(part1, m * 2 + qk + 1)
                        if not first:
                            pool.wait_ge(part3, m * 2 - 1 + qk)
                        pool.tensor_tensor(rest[:, qk, :], full[:, qk, :], parts[0][:, qk, cols],
                                           ALU.subtract).then_inc(rest1, 1)
                        pool.wait_ge(part2, m * 2 + qk + 1)
                        pool.tensor_tensor(parts[2][:, qk, cols], rest[:, qk, :], parts[1][:, qk, cols],
                                           ALU.subtract).then_inc(part3, 1)

                for b in range(B):
                    for j in range(2):
                        half(b, j, b * 2 + j, b == 0 and j == 0)
                        if j == 0 and b < B - 1:
                            rstd(b + 1)
                    if b == 0:
                        gather(3)

            @block.vector
            def _(dve):
                dve.memset(vout[:, :, :, HD:HD + 1], 1.0).then_inc(v_out, 1)
                dve.memset(ones[:], 1.0).then_inc(ones_set, 1)
                dve.wait_ge(ld, 16)
                dve.wait_ge(v_out, 1)

                def combine(b):
                    add = Link(dve, dve_add, b * 2)
                    tiles = range(b * TB, (b + 1) * TB)
                    dve.wait_ge(gathered[b], 16 * TB)
                    for i in tiles:
                        ins = dve.scalar_tensor_tensor(out=weighed[:, i % TB, :], in0=M.h[:, i, :], scalar=M.gate[:, i:i + 1],
                                                       in1=M.mod[:, 0, b, GB * P:(GB + 1) * P], op0=ALU.mult, op1=ALU.mult)
                    add(ins)
                    xb = M.x[:, tiles[0]:tiles[-1] + 1, :]
                    add(dve.tensor_tensor(xb, xb, weighed[:], ALU.add))
                    for i in tiles:
                        ins = dve.bn_stats(M.stats[:, i, :], M.x[:, i, :])
                    link = Link(dve, dve_ln, b * 7)
                    link(ins)
                    variance_and_mean(dve, link, M, slice(tiles[0], tiles[-1] + 1), var_ready)

                def normalise(m):
                    for t in range(4):
                        i = m * 4 + t
                        dve.tensor_scalar(xn[:, t, :], M.x[:, bass.ds(i, 1), :].rearrange("p o e -> p (o e)"), M.mean[:, bass.ds(i, 1)],
                                          M.rstd[:, bass.ds(i, 1)], ALU.subtract, ALU.mult).then_inc(xn_ready, 1)

                combine(0)
                dve.wait_ge(rstd_ready, 1)
                normalise(0)

                def half(b, j, m, first):
                    link = Link(dve, dve_step, m * 6)
                    dve.wait_ge(v_mm, m + 1)
                    if not first and j == 0:
                        dve.wait_ge(v_stored, b * 64)
                    dve.tensor_tensor(vout[:, 4 * j:4 * j + 4, :, 0:HD], psC[:].rearrange("p (t h d) -> p t h d", t=4, h=H),
                                      M.bv1[:].rearrange("p (h d) -> p h d", h=H).unsqueeze(1).to_broadcast([P, 4, H, HD]),
                                      ALU.add).then_inc(v_out, 1)
                    if not (isinstance(m, int) and m == 2 * B - 1):
                        if j == 1:
                            dve.wait_ge(rstd_ready, b + 2)
                        dve.wait_ge(xn_T, m + 1)
                        normalise(m + 1)
                    for qk in range(2):
                        u, a, s = psR[qk]
                        bu = 1 + 3 * qk
                        ra, rb = ras[qk], rbs[qk]
                        dve.wait_ge(u_mm, m * 2 + qk + 1)
                        dve.scalar_tensor_tensor(out=ra[:], in0=a[:], scalar=M.bcol1[:, bu + 1:bu + 2],
                                                 in1=rope[:, 0, j * 512:(j + 1) * 512], op0=ALU.add, op1=ALU.mult).then_inc(dve_step, 1)
                        link.n += 1
                        link(dve.scalar_tensor_tensor(out=rb[:], in0=s[:], scalar=M.bcol1[:, bu + 2:bu + 3],
                                                      in1=rope[:, 1, j * 512:(j + 1) * 512], op0=ALU.add, op1=ALU.mult))
                        link(dve.tensor_tensor(ra[:], ra[:], rb[:], ALU.add))
                        if not first:
                            dve.wait_ge(rest1, m * 2 - 1 + qk)
                        dve.scalar_tensor_tensor(out=full[:, qk, :], in0=u[:], scalar=M.bcol1[:, bu:bu + 1],
                                                 in1=ra[:], op0=ALU.add, op1=ALU.add).then_inc(full_ready, 1)
                    if j == 0 and b < B - 1:
                        combine(b + 1)

                def batch(b, first):
                    for j in range(2):
                        half(b, j, b * 2 + j, first and j == 0)

                for b in range(B):
                    batch(b, b == 0)

            @block.scalar
            def _(act):
                def project(m, b):
                    if not (isinstance(m, int) and m == 0):
                        act.wait_ge(u_mm, m * 2)
                    wait_apart(act, xn_T, m + 1)
                    act.activation(hT[:], psT[:], ACT.Identity, bias=M.modcol[:, 1, 0, bass.ds(b, 1)],
                                   scale=M.modcol[:, 1, 1, bass.ds(b, 1)]).then_inc(hT_ready, 1)
                    act.wait_ge(ct_mm, m + 1)
                    act.activation(ctT[:], psC[:], ACT.Identity, bias=M.bcol1[:, 0:1]).then_inc(ct_ready, 1)

                project(0, 0)

                def half(b, j, m, first):
                    if not (isinstance(m, int) and m == 2 * B - 1):
                        project(m + 1, b + j)
                    cols = slice(j * 512, (j + 1) * 512)
                    for qk in range(2):
                        act.wait_ge(full_ready, m * 2 + qk + 1)
                        if not first and j == 0:
                            act.wait_ge(qk_stored[qk], b * STORES[qk] * 16)
                        act.activation(parts[0][:, qk, cols], full[:, qk, :], ACT.Copy).then_inc(part1, 1)
                        act.wait_ge(rest1, m * 2 + qk + 1)
                        act.activation(parts[1][:, qk, cols], rest[:, qk, :], ACT.Copy).then_inc(part2, 1)

                def batch(b, first):
                    for j in range(2):
                        half(b, j, b * 2 + j, first and j == 0)

                ends_apart(act, batch)

            @block.tensor
            def _(pe):
                def half(b, j, m, first):
                    for t in range(4):
                        pe.wait_ge(xn_ready, m * 4 + t + 1)
                        if t == 0 and not first:
                            pe.wait_ge(hT_ready, m)
                        mm = pe.transpose(psT[:, t * P:(t + 1) * P], xn[:, t, :], M.ident[:])
                    mm.then_inc(xn_T, 1)
                    pe.wait_ge(hT_ready, m + 1)
                    if not first:
                        pe.wait_ge(v_out, m + 1)
                    pe.matmul(psC[:], M.wd1[:], hT[:], start=True, stop=True).then_inc(ct_mm, 1)
                    if not first:
                        pe.wait_ge(full_ready, m * 2 - 1)
                    pe.wait_ge(ct_ready, m + 1)
                    for k in range(3):
                        mm = pe.matmul(psR[0][k][:], M.wuq1[:, k * P:(k + 1) * P], ctT[:], start=True, stop=True)
                    mm.then_inc(u_mm, 1)
                    for t in range(4):
                        mm = pe.matmul(psC[:, t * P:(t + 1) * P], ctT[:, t * P:(t + 1) * P], M.wukv1[:, P:2 * P],
                                       start=True, stop=True)
                    mm.then_inc(v_mm, 1)
                    if not first:
                        pe.wait_ge(full_ready, m * 2)
                    for k in range(2):
                        pe.matmul(psR[1][1 + k][:], M.wkr1[:, k * P:(k + 1) * P], hT[:], start=True, stop=True)
                    pe.matmul(psR[1][0][:], M.wukv1[:, 0:P], ctT[:], start=True, stop=True).then_inc(u_mm, 1)

                halves(pe, half)


def phase_attention1(nc, D, M):
    with Names(nc, "at_") as n:
        group_in = M.group_in
        a_mm, a_max, m_split, m_T, mT_out = n.sem("a_mm"), n.sem("a_max"), n.sem("m_split"), n.sem("m_T"), n.sem("mT_out")
        m_stored, m_in = n.sem("m_stored"), [n.sem(f"m_in{i}") for i in range(2)]
        s_mm, exp_done, pv_done, acc_out = n.sem("s_mm"), n.sem("exp_done"), n.sem("pv_done"), n.sem("acc_out")
        pool_step = n.sem("pool_step")
        Q, K, KA, V, mp = M.Q, M.K, M.KA, M.V, M.mp
        pt = [n.sb(f"pt{i}", [P, QUAD, 512]) for i in range(2)]
        mx, mr = M.mx, M.mr
        mT = n.sb("mT", [MROWS * QUAD * 4, P], BF16)
        psA = [n.ps(f"psA{i}", [P, L]) for i in range(2)]
        psS = [n.ps(f"psS{i}", [P, 512]) for i in range(3)]
        acc = n.ps("acc", [P, 512])

        def a_step(s):
            w = s % GSTEPS
            half, kk = w // KC, w % KC
            return (s // GSTEPS) % 2, half, [(kk // 2, 2 * (kk % 2) + t) for t in range(2)]

        def bank(s, h):
            return ((s % GSTEPS) * QUAD + h) % 3

        def last_use(s, h):
            k, in_group = (s % GSTEPS) * QUAD + h, GSTEPS * QUAD
            return next(d for d in range(1, 8) if (k - d) % in_group % 3 == k % 3)

        def known(i, s):
            return i * BODY + s if isinstance(i, int) else None

        def beyond(i, s, n):
            return known(i, s) is None or known(i, s) >= n

        def exists(i, s):
            return known(i, s) is None or known(i, s) < NSTEPS

        def unit(i, s):
            return i * (BODY // KC) + s // KC

        def group(i, s):
            return i * (BODY // GSTEPS) + s // GSTEPS

        def iterations(eng, body):
            body(0)
            with eng.Fori(1, NGRP // 2 - 1) as i:
                body(i)
            body(NGRP // 2 - 1)

        with nc.Block() as block:
            @block.sync
            def _(sp):
                def load(g, a):
                    wait_apart(sp, pv_done, (g - 1) * GSTEPS)
                    load_group(sp, M, g, a)

                def maxima(pair, a, half):
                    u = pair * 2 + half
                    wait_apart(sp, mT_out, u + 1)
                    sp.dma_start(M.m_rows[half], mT[:]).then_inc(m_stored, 16)
                    wait_apart(sp, m_stored, (u + 1) * 16, 16)
                    src = M.m_rows[half].rearrange("(c p r t) q -> r c p (t q)", c=MROWS, p=2, r=2)
                    for r in range(2):
                        sp.dma_start(Q[a][64 * r + KROWS:64 * r + KROWS + MROWS, r::2, half * 512:(half + 1) * 512],
                                     src[r]).then_inc(m_in[half], 16)
                    wait_apart(sp, m_in[half], pair * 32 + 32, 32)

                for qk in range(2):
                    sp.wait_ge(M.qk_stored[qk], 16 * STORES[qk] * B)
                sp.wait_ge(M.v_stored, 16 * 4 * B)

                def body(i):
                    for a in range(2):
                        g = i * 2 + a
                        if a == 0 and isinstance(i, int) and i == 0:
                            maxima(0, 0, 0)
                        elif not (isinstance(i, int) and i == NGRP // 2 - 1 and a == 1):
                            load(g + 1, 1 - a)
                        maxima(g, a, 1)
                        if not (isinstance(i, int) and i == NGRP // 2 - 1 and a == 1):
                            maxima(g + 1, 1 - a, 0)

                iterations(sp, body)

            @block.tensor
            def _(pe):
                def a_tile(i, s, t):
                    slot, half, tiles = a_step(s)
                    h, qt = tiles[t]
                    q0 = (half * 4 + qt) * P
                    if s % GSTEPS == 0 and t == 0:
                        pe.wait_ge(group_in[slot], (i + (s // GSTEPS) // 2) * 112 + 112)
                    if beyond(i, s, 1):
                        pe.wait_ge(a_max, i * (2 * BODY) + 2 * s + t - 1)
                    if t == 0 and s % KC == 1 and beyond(i, s, KC):
                        pe.wait_ge(mT_out, unit(i, s))
                    for c in range(2):
                        mm = pe.matmul(psA[t][:, c * 512:(c + 1) * 512], Q[slot][:, h, q0:q0 + P],
                                       KA[slot][:, h // 2, c * 512:(c + 1) * 512], start=True, stop=True)
                    mm.then_inc(a_mm, 1)

                def turn(i, s):
                    pe.wait_ge(m_split, unit(i, s))
                    pe.wait_ge(a_max, i * (2 * BODY) + 2 * s + (1 if exists(i, s) else 0))
                    pe.transpose(psA[0][:].bitcast(BF16)[:, 0:P], mp[:].rearrange("p c m -> p (c m)"),
                                 M.identb[:]).then_inc(m_T, 1)

                def scores(i, s, h):
                    slot, half, kc = (s // GSTEPS) % 2, (s % GSTEPS) // KC, s % KC
                    if kc == 0 and h == 0:
                        pe.wait_ge(m_in[half], group(i, s) * 32 + 32)
                    if known(i, s) is None or known(i, s) * QUAD + h >= 3:
                        pe.wait_ge(exp_done, i * (BODY * QUAD) + s * QUAD + h + 1 - last_use(s, h))
                    pe.matmul(psS[bank(s, h)][:], K[slot][:, h // 2, kc * P:(kc + 1) * P],
                              Q[slot][:, h, half * 512:(half + 1) * 512],
                              start=True, stop=True).then_inc(s_mm, 1)

                def values(i, s):
                    slot, kc = (s // GSTEPS) % 2, s % KC
                    pe.wait_ge(exp_done, i * (BODY * QUAD) + (s + 1) * QUAD)
                    if kc == 0 and beyond(i, s, 1):
                        pe.wait_ge(acc_out, unit(i, s))
                    for h in range(QUAD):
                        mm = pe.matmul(acc[VW * h:VW * (h + 1), :], V[slot][:, kc, h * (HD + 1):h * (HD + 1) + VW],
                                       pt[s % 2][:, h, :], start=(kc == 0), stop=(kc == KC - 1),
                                       tile_position=(0, VW * h), skip_group_check=True)
                    mm.then_inc(pv_done, 1)

                for s in range(AHEAD):
                    a_tile(0, s, 0)
                    a_tile(0, s, 1)
                    if s % KC == 0 and s > 0:
                        turn(0, s)

                def body(i):
                    for s in range(BODY):
                        more = exists(i, s + AHEAD)
                        if more:
                            a_tile(i, s + AHEAD, 0)
                        scores(i, s, 0)
                        scores(i, s, 1)
                        if more:
                            a_tile(i, s + AHEAD, 1)
                        scores(i, s, 2)
                        scores(i, s, 3)
                        if (s + AHEAD) % KC == 0 and (more or known(i, s + AHEAD) == NSTEPS):
                            turn(i, s + AHEAD)
                        if s > 0:
                            values(i, s - 1)
                        elif beyond(i, s, 1):
                            values(i - 1, BODY - 1)

                iterations(pe, body)
                values(NGRP // 2 - 1, BODY - 1)

            @block.vector
            def _(dve):
                def a_max_tile(i, s, t):
                    slot, half, tiles = a_step(s)
                    h, qt = tiles[t]
                    dve.wait_ge(a_mm, i * (2 * BODY) + 2 * s + t + 1)
                    if s % KC == 0 and t == 0 and beyond(i, s, KC + 1):
                        dve.wait_ge(m_split, unit(i, s) - 1)
                    dve.tensor_reduce(mx[s // KC % 2][:, h, qt:qt + 1], psA[t][:], AX.X, ALU.max).then_inc(a_max, 1)

                def turned(i, s):
                    dve.wait_ge(m_T, unit(i, s))
                    if beyond(i, s, 2 * KC):
                        dve.wait_ge(m_stored, i * (16 * BODY // KC) + (s // KC - 1) * 16)
                    dve.tensor_copy(mT[:], psA[0][:].bitcast(BF16)[0:MROWS * QUAD * 4, 0:P]).then_inc(mT_out, 1)

                def a_part(i, s):
                    if exists(i, s):
                        a_max_tile(i, s, 0)
                        a_max_tile(i, s, 1)
                    if s % KC == 0 and beyond(i, s, 1) and (known(i, s) is None or known(i, s) <= NSTEPS):
                        turned(i, s)

                for s in range(AHEAD):
                    a_part(0, s)

                def body(i):
                    for s in range(BODY):
                        a_part(i, s + AHEAD)

                iterations(dve, body)

            @block.gpsimd
            def _(pool):
                def split(i, s):
                    link = Link(pool, pool_step, unit(i, s) * 4)
                    pool.wait_ge(a_max, i * (2 * BODY) + 2 * s + 2)
                    if beyond(i, s, KC):
                        pool.wait_ge(m_T, unit(i, s))
                    m = mx[s // KC % 2][:].rearrange("p h t -> p (h t)")
                    zero = M.zeros[:, 0:QUAD * 4]
                    link(pool.tensor_tensor(mr[:], zero, m, ALU.subtract))
                    link(pool.tensor_tensor(mp[:, 0, :], mr[:], zero, ALU.add))
                    link(pool.tensor_tensor(mr[:], mr[:], mp[:, 0, :], ALU.subtract))
                    link(pool.tensor_tensor(mp[:, 1, :], mr[:], zero, ALU.add))
                    pool.tensor_tensor(mp[:, 2, :], mr[:], mp[:, 1, :], ALU.subtract).then_inc(m_split, 1)

                def units(i, steps):
                    for s in steps:
                        if s % KC == KC - 1 and exists(i, s):
                            split(i, s)

                units(0, range(AHEAD))
                iterations(pool, lambda i: units(i, range(AHEAD, AHEAD + BODY)))

            @block.scalar
            def _(act):
                def evacuate(u):
                    wait_apart(act, pv_done, (u + 1) * KC)
                    act.activation(M.attn[:, bass.ds(u, 1), :].rearrange("p o q -> p (o q)"), acc[:], ACT.Copy).then_inc(acc_out, 1)

                def body(i):
                    for s in range(BODY):
                        if beyond(i, s, 2):
                            act.wait_ge(pv_done, i * BODY + s - 1)
                        for h in range(QUAD):
                            act.wait_ge(s_mm, i * (BODY * QUAD) + s * QUAD + h + 1)
                            act.activation(pt[s % 2][:, h, :], psS[bank(s, h)][:], ACT.Exp,
                                           scale=INV_SCALE).then_inc(exp_done, 1)
                        if s % KC == 0 and beyond(i, s, 1):
                            evacuate(i * (BODY // KC) + s // KC - 1)

                iterations(act, body)
                evacuate(NSTEPS // KC - 1)


def phase_output1(nc, D, M):
    with Names(nc, "o1_") as n:
        num_T, ctx_ready, ctx_T, ctxT_ready = n.sem("num_T"), n.sem("ctx_ready"), n.sem("ctx_T"), n.sem("ctxT_ready")
        o_mm, added, wog_ready, pool_step, dve_step = n.sem("o_mm"), n.sem("added"), n.sem("wog_ready"), n.sem("pool_step"), n.sem("dve_step")
        bog_added = n.sem("bog_added")
        psN = [n.ps(f"psN{i}", [P, 512]) for i in range(3)]
        psC = [n.ps(f"psC{i}", [P, 512]) for i in range(2)]
        psO = [n.ps(f"psO{i}", [P, 512]) for i in range(2)]
        wog, bog = n.sb("wog", [P, B, P]), n.sb("bog", [P, B, P])
        rden = [n.sb(f"rden{i}", [P, H]) for i in range(2)]
        ctx = [n.sb(f"ctx{i}", [P, P]) for i in range(2)]
        ctxT = [n.sb(f"ctxT{i}", [P, P]) for i in range(2)]
        with nc.Block() as block:
            @block.gpsimd
            def _(pool):
                ga = M.mod[:, 1, :, GA * P:(GA + 1) * P]
                pool.tensor_tensor(wog[:], M.wo1[:].unsqueeze(1).to_broadcast([P, B, P]), ga, ALU.mult).then_inc(wog_ready, 1)
                pool.tensor_tensor(bog[:], M.bo1[:].unsqueeze(1).to_broadcast([P, B, P]), ga, ALU.mult).then_inc(pool_step, 1)
                pool.wait_ge(pool_step, 1)
                for b in range(B):
                    xb = M.x[:, b * TB:(b + 1) * TB, :]
                    pool.tensor_tensor(xb, xb, bog[:, b, :].unsqueeze(1).to_broadcast([P, TB, P]), ALU.add).then_inc(bog_added, 1)

            @block.tensor
            def _(pe):
                for k in range(NT + 2):
                    if k < NT:
                        b, half, qt = k // TB, (k % TB) // 4, k % 4
                        if k >= 3:
                            pe.wait_ge(ctx_ready, k - 2)
                        for quad in range(4):
                            u = (b * 4 + quad) * 2 + half
                            mm = pe.transpose(psN[k % 3][:, quad * P:(quad + 1) * P], M.attn[:, u, qt * P:(qt + 1) * P], M.ident[:])
                        mm.then_inc(num_T, 1)
                    if 1 <= k <= NT:
                        i = k - 1
                        pe.wait_ge(ctx_ready, i + 1)
                        if i >= 2:
                            pe.wait_ge(ctxT_ready, i - 1)
                        pe.transpose(psC[i % 2][:, 0:P], ctx[i % 2][:], M.ident[:]).then_inc(ctx_T, 1)
                    if k >= 2:
                        i = k - 2
                        if i == 0:
                            pe.wait_ge(wog_ready, 1)
                        pe.wait_ge(ctxT_ready, i + 1)
                        if i >= 2:
                            pe.wait_ge(added, i - 1)
                        pe.matmul(psO[i % 2][:, 0:P], ctxT[i % 2][:], wog[:, i // TB, :], start=True, stop=True).then_inc(o_mm, 1)

            @block.scalar
            def _(act):
                for i in range(NT):
                    act.wait_ge(ctx_T, i + 1)
                    if i >= 2:
                        act.wait_ge(o_mm, i - 1)
                    act.activation(ctxT[i % 2][:], psC[i % 2][:, 0:P], ACT.Copy).then_inc(ctxT_ready, 1)

            @block.vector
            def _(dve):
                def add(i):
                    dve.wait_ge(o_mm, i + 1)
                    dve.wait_ge(bog_added, i // TB + 1)
                    dve.tensor_tensor(M.x[:, i, :], M.x[:, i, :], psO[i % 2][:, 0:P], ALU.add).then_inc(added, 1)

                def stats(i):
                    dve.wait_ge(added, i + 1)
                    dve.bn_stats(M.stats[:, i, :], M.x[:, i, :])

                for k in range(NT + 3):
                    if k < NT:
                        dve.wait_ge(num_T, k + 1)
                        nd = psN[k % 3][:].rearrange("p (h c) -> p h c", c=VW)
                        if k >= 2:
                            dve.wait_ge(ctx_T, k - 1)
                            dve.wait_ge(ctx_ready, k - 1)
                        dve.reciprocal(rden[k % 2][:].unsqueeze(2), nd[:, :, HD:HD + 1]).then_inc(dve_step, 1)
                        dve.wait_ge(dve_step, k + 1)
                        dve.tensor_tensor(ctx[k % 2][:].rearrange("p (h d) -> p h d", h=H), nd[:, :, 0:HD],
                                          rden[k % 2][:].unsqueeze(2).to_broadcast([P, H, HD]), ALU.mult).then_inc(ctx_ready, 1)
                    if 2 <= k < NT + 2:
                        add(k - 2)
                    if k >= 3:
                        stats(k - 3)


def phase_experts1(nc, D, M):
    S = Steps(NS1, LAG_Y)
    U = S.UNROLL
    with Names(nc, "e1_") as n:
        loaded = [n.sem(f"loaded{i}") for i in range(2)]
        x_T, xT_ready, mm1_done, silu_done, g_ready = (n.sem("x_T"), n.sem("xT_ready"), n.sem("mm1_done"),
                                                       n.sem("silu_done"), n.sem("g_ready"))
        g_T, gT_ready, mm2_done, y_ready = n.sem("g_T"), n.sem("gT_ready"), n.sem("mm2_done"), n.sem("y_ready")
        stored = [n.sem(f"stored{i}") for i in range(2)]
        rows = [n.sb(f"rows{i}", [P, GT, P]) for i in range(2)]
        xT = [n.sb(f"xT{i}", [P, GT, P]) for i in range(2)]
        sg = [n.sb(f"sg{i}", [P, F1]) for i in range(2)]
        g = [n.sb(f"g{i}", [P, F1]) for i in range(RING)]
        gT = [n.sb(f"gT{i}", [P, P]) for i in range(RING)]
        y = [n.sb(f"y{i}", [P, GT, P]) for i in range(2)]
        psX = [n.ps(f"psX{i}", [P, 512]) for i in range(2)]
        ps1 = [n.ps(f"ps1{i}", [P, 512]) for i in range(2)]
        ps2 = [n.ps(f"ps2{i}", [P, 512]) for i in range(2)]
        psY = [n.ps(f"psY{i}", [P, 512]) for i in range(2)]
        src = M.sorted[1].rearrange("(s p) e -> p s e", p=P)
        dst = M.result[1].rearrange("(s p) e -> p s e", p=P)

        with nc.Block() as block:
            @block.sync
            def _(sp):
                move_tiles(sp, NS1, src, dst, rows, y, loaded, stored, x_T, y_ready)

            @block.tensor
            def _(pe):
                expert = Experts(nc, mybir.EngineType.PE, M, NS1, E1)

                def step(i, r):
                    k, gs = i * U + r, r // GT
                    expert.fetch(i, r)
                    if S.has(k) and r % GT == 0:
                        pe.wait_ge(loaded[gs], i * 16 + 16)
                        if after(k, U):
                            pe.wait_ge(xT_ready, i * 2 + gs - 1)
                        for t in range(GT):
                            mm = pe.transpose(psX[gs][:, t * P:(t + 1) * P], rows[gs][:, t, :], M.ident[:])
                        mm.then_inc(x_T, 1)
                    if S.has(k - 1):
                        j = (r - 1) % U
                        if j % GT == 0:
                            pe.wait_ge(xT_ready, i * 2 + (r - 1) // GT + 1)
                        if after(k - 1, 2):
                            pe.wait_ge(g_ready, k - 2)
                        pe.matmul(ps1[j % 2][:, 0:2 * F1], xT[j // GT][:, j % GT, :], M.wgu1[:, bass.ds(expert[r - 1], 1), :], start=True,
                                  stop=True).then_inc(mm1_done, 1)
                    if S.has(k - LAG_T):
                        j, q, o = k - LAG_T, (r - LAG_T) % 2, (r - LAG_T) % RING
                        pe.wait_ge(g_ready, j + 1)
                        if after(j, 2):
                            pe.wait_ge(gT_ready, j - 1)
                        pe.transpose(ps2[q][:, 0:P], g[o][:], M.ident[:]).then_inc(g_T, 1)
                    if S.has(k - LAG_Y):
                        j, q, o = k - LAG_Y, (r - LAG_Y) % 2, (r - LAG_Y) % RING
                        e = expert[r - LAG_Y]
                        pe.wait_ge(gT_ready, j + 1)
                        if after(j, 2):
                            pe.wait_ge(y_ready, j - 1)
                        pe.matmul(psY[q][:, 0:P], gT[o][:], M.wdn1[:, bass.ds(e, 1), :],
                                  start=True, stop=True).then_inc(mm2_done, 1)

                S.run(pe, step)

            @block.vector
            def _(dve):
                def step(i, r):
                    k, gs = i * U + r, r // GT
                    if S.has(k) and r % GT == 0:
                        dve.wait_ge(x_T, i * 2 + gs + 1)
                        if after(k, U):
                            dve.wait_ge(mm1_done, k - GT)
                        dve.tensor_copy(xT[gs][:].rearrange("p t e -> p (t e)"), psX[gs][:]).then_inc(xT_ready, 1)
                    if S.has(k - 1):
                        q = (r - 1) % 2
                        dve.wait_ge(silu_done, k)
                        if after(k - 1, RING):
                            dve.wait_ge(g_T, k - RING)
                        dve.tensor_tensor(g[(r - 1) % RING][:], ps1[q][:, F1:2 * F1], sg[q][:], ALU.mult).then_inc(g_ready, 1)
                    if S.has(k - LAG_Y):
                        j = (r - LAG_Y) % U
                        dve.wait_ge(mm2_done, k - LAG_Y + 1)
                        if after(k - LAG_Y, U) and j % GT == 0:
                            dve.wait_ge(stored[j // GT], (i if r >= LAG_Y else i - 1) * 16)
                        dve.tensor_copy(y[j // GT][:, j % GT, :], psY[j % 2][:, 0:P]).then_inc(y_ready, 1)

                S.run(dve, step)

            @block.scalar
            def _(act):
                def step(i, r):
                    k = i * U + r
                    if S.has(k - 1):
                        q = (r - 1) % 2
                        act.wait_ge(mm1_done, k)
                        if after(k - 1, 2):
                            act.wait_ge(g_ready, k - 2)
                        act.activation(sg[q][:], ps1[q][:, 0:F1], ACT.Silu).then_inc(silu_done, 1)
                    if S.has(k - LAG_T):
                        j, q, o = k - LAG_T, (r - LAG_T) % 2, (r - LAG_T) % RING
                        act.wait_ge(g_T, j + 1)
                        if after(j, RING):
                            act.wait_ge(mm2_done, j - RING + 1)
                        act.activation(gT[o][:], ps2[q][:, 0:P], ACT.Copy).then_inc(gT_ready, 1)

                S.run(act, step)


def phase_shared1(nc, D, M):
    NC = 2 * B
    FIRST = SHARED_EARLY
    with Names(nc, "s1_") as n:
        gathered = [n.sem(f"gathered{i}") for i in range(NC)]
        weighed, x_steps, stored = n.sem("weighed"), n.sem("x_steps"), n.sem("stored")
        psG, psU = [n.ps(f"psG{i}", [P, 512]) for i in range(2)], [n.ps(f"psU{i}", [P, 512]) for i in range(2)]
        shared = SharedExpert(n, M, range(FIRST, NC), psG, psU)
        routed = [n.sb(f"routed{i}", [P, 4, P]) for i in range(2)]
        turns = [([2 * i, 2 * i + 1] if i < len(shared.chunks) else [], FIRST + i - 1 if i else None)
                 for i in range(len(shared.chunks) + 1)]
        order, has_routed, has_shared = [], set(), set(range(FIRST))
        for two, late in turns:
            has_shared |= {late}
            has_routed |= set(two)
            order += sorted(c for c in (has_routed & has_shared) - set(order))
        with nc.Block() as block:
            @block.gpsimd
            def _(pool):
                for i in range(NT):
                    pool.indirect_dma_start(
                        out=M.h[:, i, :], out_offset=None, in_=M.result[1][:, :],
                        in_offset=bass.IndirectOffsetOnAxis(ap=M.slot[:, i:i + 1], axis=0)).then_inc(gathered[i // 4], 16)
                for g in gathered:
                    pool.wait_ge(g, 64)

            @block.tensor
            def _(pe):
                for i in range(len(shared.chunks) + 1):
                    if i < len(shared.chunks):
                        for f in range(FCS):
                            shared.up(pe, i, f)
                    if i >= 1:
                        shared.down(pe, i - 1)

            @block.scalar
            def _(act):
                shared.silu(act)

            @block.vector
            def _(dve):
                def add_routed(c):
                    dve.wait_ge(gathered[c], 64)
                    if c >= 2:
                        dve.wait_ge(x_steps, c - 1)
                    gb = M.mod[:, 1, c // 2, GB * P:(GB + 1) * P].unsqueeze(1).to_broadcast([P, 4, P])
                    dve.tensor_tensor(routed[c % 2][:], M.h[:, 4 * c:4 * c + 4, :], gb, ALU.mult).then_inc(weighed, 1)
                    dve.wait_ge(weighed, c + 1)
                    if c >= FIRST:
                        if c - FIRST < shared.finished:
                            dve.wait_ge(shared.x_added, c - FIRST + 1)
                    xc = M.x[:, 4 * c:4 * c + 4, :]
                    dve.tensor_tensor(xc, xc, routed[c % 2][:], ALU.add).then_inc(x_steps, 1)

                for i, (two, late) in enumerate(turns):
                    if i < len(shared.chunks):
                        shared.gate(dve, i)
                    if late is not None:
                        if late < 2 * i:
                            dve.wait_ge(x_steps, late + 1)
                        shared.finish(dve, i - 1)
                    for c in two:
                        add_routed(c)

            @block.sync
            def _(sp):
                for c in order:
                    sp.wait_ge(x_steps, c + 1)
                    if c >= FIRST:
                        sp.wait_ge(shared.x_added, c - FIRST + 1)
                    sp.dma_start(D["out"][c // 2].rearrange("(t p) e -> p t e", p=P)[:, 4 * (c % 2):4 * (c % 2) + 4, :],
                                 M.x[:, 4 * c:4 * c + 4, :]).then_inc(stored, 16)
                sp.wait_ge(stored, 16 * NC)


def program(nc, D, out):
    D["out"] = out
    Names.start(nc)
    with Names(nc) as M:
        declare(nc, M)
        with Names(nc) as heads:
            declare_heads(M, heads)
            M.qk_stored, M.v_stored = [M.sem(f"qk_stored{i}") for i in range(2)], M.sem("v_stored")
            M.group_in = [M.sem(f"group_in{i}") for i in range(2)]
            with Names(nc) as rows:
                M.h = rows.sb("h_l0", [P, NT, P])
                with Names(nc) as layer0:
                    declare_experts0(M, layer0)
                    M.wmod1, M.scb1 = layer0.sb("wmod1", [P, 6 * P]), layer0.sb("scb1", [P, B, P])
                    phase_load(nc, D, M)
                    phase_linear_attention(nc, D, M)
                    with Names(nc) as turned:
                        M.hT = turned.sb("hT_l0", [P, NT * P])
                        phase_route(nc, D, M, 0)
                    phase_experts0(nc, D, M)
                phase_project1(nc, D, M)
            with Names(nc) as attended:
                M.attn = attended.sb("attn", [P, NGRP * 2, 512])
                phase_attention1(nc, D, M)
                phase_output1(nc, D, M)
        with Names(nc) as layer1:
            declare_experts1(M, layer1)
            M.h, M.hT = layer1.sb("h_l1", [P, NT, P]), layer1.sb("hT_l1", [P, NT * P])
            phase_route(nc, D, M, 1)
            phase_experts1(nc, D, M)
            phase_shared1(nc, D, M)


def declare(nc, M):
    M.x = M.sb("x", [P, NT, P])
    M.stats = M.sb("stats", [P, NT, 6])
    M.ln_d, M.ln_v = M.sb("ln_d", [P, NT]), M.sb("ln_v", [P, NT])
    M.mean, M.rstd, M.half = M.sb("mean", [P, NT]), M.sb("rstd", [P, NT]), M.sb("half", [P, NT])
    M.mod = M.sb("mod", [P, 2, B, 6 * P])
    M.modcol = M.sb("modcol", [P, 2, 2, B])
    M.gate, M.zeros = M.sb("gate", [P, NT]), M.sb("zeros", [P, P])
    M.slot, M.expert = M.sb("slot", [P, NT], I32), M.sb("expert", [1, NS1], I32)
    M.sorted = [nc.dram_tensor(f"sorted{l}", [s * P, P], F32).ap() for l, s in enumerate((NS0, NS1))]
    M.result = [nc.dram_tensor(f"result{l}", [s * P, P], F32).ap() for l, s in enumerate((NS0, NS1))]
    M.qk_rows = [nc.dram_tensor(f"{x}_rows", [B * H, KROWS, L], BF16).ap() for x in "qk"]
    M.v_rows = nc.dram_tensor("v_rows", [NGRP, P, KC, VC], F32).ap()
    M.m_rows = nc.dram_tensor("m_rows", [2, MROWS * QUAD * 4, P], BF16).ap()
    M.ident, M.identb = M.sb("ident", [P, P]), M.sb("identb", [P, P], BF16)
    M.wq0, M.wkv0, M.wo0 = M.sb("wq0", [P, P]), M.sb("wkv0", [P, 2 * P]), M.sb("wo0", [P, P])
    M.bq0, M.bkv0, M.bo0 = M.sb("bq0", [P, 1]), M.sb("bkv0", [P, 2 * P]), M.sb("bo0", [P, P])
    M.blockmask, M.headmask = M.sb("blockmask", [P, P]), M.sb("headmask", [P, H])
    M.tri, M.onesm = M.sb("tri", [P, P]), M.sb("onesm", [P, P])
    M.idents, M.tiles = M.sb("idents", [P, E1]), M.sb("tiles", [P, NS1])
    M.wr0, M.br0 = M.sb("wr0", [P, E0]), M.sb("br0", [P, E0])
    M.wd1, M.wuq1, M.wukv1, M.wkr1 = (M.sb("wd1", [P, 2 * DR]), M.sb("wuq1", [P, 3 * P]),
                                      M.sb("wukv1", [P, 2 * P]), M.sb("wkr1", [P, 2 * P]))
    M.bcol1, M.bv1 = M.sb("bcol1", [P, 8]), M.sb("bv1", [P, P])
    M.wo1, M.bo1 = M.sb("wo1", [P, P]), M.sb("bo1", [P, P])
    M.wr1 = M.sb("wr1", [P, E1])


def declare_experts0(M, n):
    M.w10, M.w20 = n.sb("w10", [P, E0, F0]), n.sb("w20", [P, E0, FC0, P])
    M.b10, M.b20 = n.sb("b10", [P, E0, F0]), n.sb("b20", [P, E0, P])


def declare_experts1(M, n):
    M.wgu1, M.wdn1 = n.sb("wgu1", [P, E1, 2 * F1]), n.sb("wdn1", [P, E1, P])
    M.wsg1, M.wsd1 = n.sb("wsg1", [P, 2 * FS]), n.sb("wsd1", [P, FCS, P])


def rope_tables():
    ids = np.arange(P // 2, dtype=np.float32)
    theta = (np.float32(10000.0) ** (np.float32(-2.0) * ids)).astype(np.float32) / np.float32(P // 2)
    r = np.arange(L, dtype=np.float32)[:, None] * theta[None, :]
    cos, sin = np.cos(r), np.sin(r)
    both = np.empty((2, P, L), np.float32)
    both[0, 0::2], both[0, 1::2] = cos.T, cos.T
    both[1, 0::2], both[1, 1::2] = -sin.T, sin.T
    return both


def layout(a):
    row = lambda v: np.ascontiguousarray(v)
    swap = np.arange(P) ^ 1
    r = np.arange(P)
    return {
        "x": a["L0_attn_query"],
        "cT": np.stack([a["L0_c"].T, a["L1_c"].T], 1),
        "wmod": np.stack([a["L0_wmod"], a["L1_wmod"]], 1),
        "ident": np.eye(P, dtype=np.float32),
        "wq0": a["L0_attn_Wq"].T, "wkv0": np.concatenate([a["L0_attn_Wk"].T, a["L0_attn_Wv"].T], 1),
        "wo0": a["L0_attn_Wo"].T, "bq0": a["L0_attn_bq"][:, None],
        "bkv0": np.concatenate([a["L0_attn_bk"], a["L0_attn_bv"]]), "bo0": a["L0_attn_bo"],
        "blockmask": (r[:, None] // HD == r[None, :] // HD).astype(np.float32),
        "headmask": (r[:, None] // HD == np.arange(H)[None, :]).astype(np.float32),
        "tri": (r[:, None] < r[None, :]).astype(np.float32), "onesm": np.ones((P, P), np.float32),
        "idents": np.arange(E1, dtype=np.float32), "tiles": np.arange(NS1, dtype=np.float32),
        "wr0": a["L0_ffn_Wr"], "br0": a["L0_ffn_br"],
        "w10": a["L0_ffn_W1"].transpose(1, 0, 2),
        "w20": a["L0_ffn_W2"].reshape(E0, FC0, P, P).transpose(2, 0, 1, 3),
        "b10": a["L0_ffn_b1"], "b20": a["L0_ffn_b2"],
        "wd1": np.concatenate([a["L1_attn_Wd_q_w"], a["L1_attn_Wd_kv_w"]], 1),
        "wuq1": np.concatenate([np.concatenate([a["L1_attn_Wu_q_w"], a["L1_attn_Wq_r_w"], a["L1_attn_Wq_r_w"][:, swap]], 1),
                                np.zeros((DR, 3 * P), np.float32)], 0),
        "wukv1": np.concatenate([np.zeros((DR, 2 * P), np.float32),
                                 np.concatenate([a["L1_attn_Wu_k_w"], a["L1_attn_Wu_v_w"]], 1)], 0),
        "wkr1": np.concatenate([a["L1_attn_Wk_r_w"], a["L1_attn_Wk_r_w"][:, swap]], 1),
        "bcol1": np.stack([np.concatenate([a["L1_attn_Wd_q_b"], a["L1_attn_Wd_kv_b"]]),
                           a["L1_attn_Wu_q_b"], a["L1_attn_Wq_r_b"], a["L1_attn_Wq_r_b"][swap],
                           a["L1_attn_Wu_k_b"], a["L1_attn_Wk_r_b"], a["L1_attn_Wk_r_b"][swap],
                           np.zeros(P, np.float32)], 1),
        "bv1": a["L1_attn_Wu_v_b"], "wo1": a["L1_attn_Wo_w"], "bo1": a["L1_attn_Wo_b"],
        "wr1": a["L1_ffn_router_w"].T,
        "wgu1": a["L1_ffn_gate_up_proj"].transpose(1, 0, 2), "wdn1": a["L1_ffn_down_proj"].transpose(1, 0, 2),
        "wsg1": np.concatenate([a["L1_ffn_shared_gate_w"].T, a["L1_ffn_shared_up_w"].T], 1),
        "wsd1": a["L1_ffn_shared_down_w"].T.reshape(FCS, P, P).transpose(1, 0, 2),
        "rope": rope_tables().transpose(1, 0, 2),
    }


def kernel(**inputs):
    import concourse.bacc as bacc
    from concourse.bass_utils import run_bass_kernel_spmd

    nc = bacc.Bacc("TRN2", target_bir_lowering=False, num_devices=1)
    arrays, D = {}, {}
    for name, a in layout(inputs).items():
        arrays[f"in_{name}"] = np.ascontiguousarray(a)
        D[name] = nc.dram_tensor(f"in_{name}", list(a.shape), F32, kind="ExternalInput").ap()
    out = nc.dram_tensor("out_0", [B, L, P], F32, kind="ExternalOutput").ap()
    program(nc, D, out)
    return run_bass_kernel_spmd(nc, [arrays], core_ids=[0]).results[0]["out_0"]
```
